# Optimizing a Trainium2 kernel written in Bass

```python
import numpy as np
import jax
import jax.numpy as jnp

def _softmax(x, axis=-1):
    return jax.nn.softmax(x, axis=axis)

def _gelu(x):
    return jax.nn.gelu(x, approximate=True)

def _silu(x):
    return jax.nn.silu(x)

def _sigmoid(x):
    return jax.nn.sigmoid(x)

def _layernorm(x, axis=-1, eps=1e-05):
    m = jnp.mean(x, axis=axis, keepdims=True)
    v = jnp.var(x, axis=axis, keepdims=True)
    return (x - m) / jnp.sqrt(v + eps)

def _scatter_add(tgt, idx, src, axis=0):
    return tgt.at[idx].add(src)

def _segment_sum(src, seg, n):
    return jax.ops.segment_sum(src, seg, n)
kernel_name = 'mk_xattn_ffn_d2_seqx_r8_bbb144'

def setup_inputs(seed: int=0):
    np.random.seed(seed)
    _w = jnp.asarray

    def _rec_inputs():
        import jax
        import jax.numpy as jnp
        _rk = jax.random.key(seed)
        x = 0.002226 + 0.9996 * jax.random.normal(jax.random.fold_in(_rk, 1), (8, 128, 128), jnp.float32)
        _lenS = 128 - jax.random.randint(jax.random.fold_in(_rk, 7), (8,), 0, max(1, 128 // 4) + 1, jnp.int32)
        _lenS2 = 77 - jax.random.randint(jax.random.fold_in(_rk, 8), (8,), 0, max(1, 77 // 4) + 1, jnp.int32)
        _ctx_1024P = jax.random.normal(jax.random.fold_in(_rk, 11), (8, 16, 128), jnp.float32)
        _ctx_1024c = jax.random.dirichlet(jax.random.fold_in(_rk, 511), 0.3 * jnp.ones((16,), jnp.float32), (8, 77))
        _ctx_1024t = jnp.einsum('bsk,bkd->bsd', _ctx_1024c, _ctx_1024P)
        _ctx_1024t = _ctx_1024t * jax.lax.rsqrt(jnp.mean(jnp.square(_ctx_1024t)) + 1e-12) * 0.953939
        ctx_1024 = -7.10856e-05 + 0.999911 * (_ctx_1024t + 0.3 * jax.random.normal(jax.random.fold_in(_rk, 611), (8, 77, 128), jnp.float32))
        _validS = jnp.arange(128)[None, :] < _lenS[:, None]
        _validS2 = jnp.arange(77)[None, :] < _lenS2[:, None]
        _causal = jnp.tril(jnp.ones((128, 128), dtype=bool))
        mask_BxS2_bk0 = jnp.logical_not(jnp.broadcast_to(_validS2[:, :], (8, 77)))
        return (x, ctx_1024, mask_BxS2_bk0)
    x, ctx_1024, mask_BxS2_bk0 = _rec_inputs()

    def _L0_xattn_setup():
        import jax, jax.numpy as jnp
        import numpy as np
        DIM, DIM_HEAD, HEADS, SCALE = (128, 64, 8, 8.0)
        INNER = DIM_HEAD * HEADS
        LN_EPS = 1e-05
        L2_EPS = 1e-12

        def layer_norm(x, w, b):
            mu = jnp.mean(x, axis=-1, keepdims=True)
            var = jnp.mean(jnp.square(x - mu), axis=-1, keepdims=True)
            return (x - mu) * jax.lax.rsqrt(var + LN_EPS) * w + b

        def l2norm(t):
            n = jnp.sqrt(jnp.sum(jnp.square(t), axis=-1, keepdims=True))
            return t / jnp.maximum(n, L2_EPS)
        key = jax.random.key(seed)
        ks = jax.random.split(key, 8)
        b, n, m = (8, 1024, 64)
        x = jax.random.normal(ks[0], (b, n, DIM), dtype=jnp.float32)
        latents = jax.random.normal(ks[1], (b, m, DIM), dtype=jnp.float32)
        mask = jax.random.randint(ks[2], (b, n), 0, 2) > 0
        Wq = jax.random.normal(ks[3], (DIM, INNER), dtype=jnp.float32) * DIM ** (-0.5)
        Wkv = jax.random.normal(ks[4], (DIM, 2 * INNER), dtype=jnp.float32) * DIM ** (-0.5)
        Wo = jax.random.normal(ks[5], (INNER, DIM), dtype=jnp.float32) * INNER ** (-0.5)
        return {'x': x, 'latents': latents, 'mask': mask, 'ln_x_w': jnp.ones((DIM,)), 'ln_x_b': jnp.zeros((DIM,)), 'ln_l_w': jnp.ones((DIM,)), 'ln_l_b': jnp.zeros((DIM,)), 'Wq': Wq, 'Wkv': Wkv, 'q_scale': jnp.ones((DIM_HEAD,)), 'k_scale': jnp.ones((DIM_HEAD,)), 'Wo': Wo, 'ln_o_w': jnp.ones((DIM,)), 'ln_o_b': jnp.zeros((DIM,))}
    _L0_xattn_all = _L0_xattn_setup()
    _L0_xattn_in = {k: v for k, v in _L0_xattn_all.items() if k in ('ln_x_w', 'ln_x_b', 'ln_l_w', 'ln_l_b', 'Wq', 'Wkv', 'q_scale', 'k_scale', 'Wo', 'ln_o_w', 'ln_o_b')}
    del _L0_xattn_all

    def _L0_ffn_setup():
        import jax, jax.numpy as jnp
        import numpy as np
        JITTER_EPS = 0.01

        def phi_routing(logits, jitter_eps=JITTER_EPS):
            m, sel = jax.lax.top_k(logits, 2)
            T, E = logits.shape
            m1 = m[:, :1]
            factor1 = jnp.maximum(jnp.abs(logits), m1)
            mask1 = (m1 - logits) / factor1 > 2.0 * jitter_eps
            p1 = jax.nn.softmax(jnp.where(mask1, -jnp.inf, logits), axis=-1)
            mult1 = jnp.take_along_axis(p1, sel[:, :1], axis=-1)
            m2 = m[:, 1:2]
            factor2 = jnp.maximum(jnp.abs(logits), m2)
            mask2 = (m2 - logits) / factor2 > 2.0 * jitter_eps
            drop_top1 = jnp.arange(E)[None, :] == sel[:, :1]
            p2 = jax.nn.softmax(jnp.where(mask2 | drop_top1, -jnp.inf, logits), axis=-1)
            mult2 = jnp.take_along_axis(p2, sel[:, 1:2], axis=-1)
            return (jnp.concatenate([mult1, mult2], axis=-1), sel)
        key = jax.random.key(seed)
        k = jax.random.split(key, 5)
        B, S, H, F, E = (1, 64, 128, 512, 8)
        return {'hidden_states': jax.random.normal(k[0], (B, S, H), jnp.float32), 'gate_w': jax.random.normal(k[1], (E, H), jnp.float32) * 0.02, 'w1': jax.random.normal(k[2], (E, F, H), jnp.float32) * 0.02, 'w2': jax.random.normal(k[3], (E, H, F), jnp.float32) * 0.02, 'w3': jax.random.normal(k[4], (E, F, H), jnp.float32) * 0.02}
    _L0_ffn_all = _L0_ffn_setup()
    _L0_ffn_in = {k: v for k, v in _L0_ffn_all.items() if k in ('gate_w', 'w1', 'w2', 'w3')}
    del _L0_ffn_all

    def _L1_xattn_setup():
        import jax, jax.numpy as jnp
        import numpy as np
        DIM = 128
        H = 16
        DH = 64
        INNER = H * DH
        SCALE = DH ** (-0.5)
        key = jax.random.key(seed)
        ks = jax.random.split(key, 6)
        B, L, R = (4, 512, 64)
        x = jax.random.normal(ks[0], (B, L, DIM), dtype=jnp.float32)
        context = jax.random.normal(ks[1], (B, R, DIM), dtype=jnp.float32)
        s = DIM ** (-0.5)
        Wq = jax.random.normal(ks[2], (DIM, INNER), dtype=jnp.float32) * s
        Wk = jax.random.normal(ks[3], (DIM, INNER), dtype=jnp.float32) * s
        Wv = jax.random.normal(ks[4], (DIM, INNER), dtype=jnp.float32) * s
        Wo = jax.random.normal(ks[5], (INNER, DIM), dtype=jnp.float32) * INNER ** (-0.5)
        return {'x': x, 'context': context, 'Wq': Wq, 'Wk': Wk, 'Wv': Wv, 'Wo': Wo}
    _L1_xattn_all = _L1_xattn_setup()
    _L1_xattn_in = {k: v for k, v in _L1_xattn_all.items() if k in ('Wq', 'Wk', 'Wv', 'Wo')}
    del _L1_xattn_all

    def _L1_ffn_setup():
        import jax, jax.numpy as jnp
        import numpy as np
        BLOCK = 32
        W_BITS = 4
        ACT_BITS = 16

        def act_qdq(x):
            qmax = 2.0 ** (ACT_BITS - 1) - 1.0
            scale = jnp.maximum(jnp.max(jnp.abs(x)) / qmax, 1e-12)
            return jnp.clip(jnp.round(x / scale), -qmax - 1.0, qmax) * scale

        def fixed_qdq_u16(x):
            scale = 1.0 / 65536.0
            return jnp.clip(jnp.round(x / scale), 0.0, 65535.0) * scale

        def lpbq_dequant(w):
            O, I = w.shape
            qmax = 2.0 ** (W_BITS - 1) - 1.0
            wb = w.reshape(O, I // BLOCK, BLOCK)
            s = jnp.maximum(jnp.max(jnp.abs(wb), axis=-1, keepdims=True) / qmax, 1e-12)
            wq = jnp.clip(jnp.round(wb / s), -qmax - 1.0, qmax) * s
            return wq.reshape(O, I)
        key = jax.random.key(seed)
        k1, k2, k3, k4 = jax.random.split(key, 4)
        B, S, H, I = (2, 512, 128, 384)
        x = jax.random.normal(k1, (B, S, H), jnp.float32)
        w_gate = jax.random.normal(k2, (I, H), jnp.float32) * 0.02
        w_up = jax.random.normal(k3, (I, H), jnp.float32) * 0.02
        w_down = jax.random.normal(k4, (H, I), jnp.float32) * 0.02
        return {'x': x, 'w_gate': w_gate, 'w_up': w_up, 'w_down': w_down}
    _L1_ffn_all = _L1_ffn_setup()
    _L1_ffn_in = {k: v for k, v in _L1_ffn_all.items() if k in ('w_gate', 'w_up', 'w_down')}
    del _L1_ffn_all
    return {'x': x, 'ctx_1024': ctx_1024, 'mask_BxS2_bk0': mask_BxS2_bk0, 'L0_xattn_ln_x_w': _L0_xattn_in['ln_x_w'], 'L0_xattn_ln_x_b': _L0_xattn_in['ln_x_b'], 'L0_xattn_ln_l_w': _L0_xattn_in['ln_l_w'], 'L0_xattn_ln_l_b': _L0_xattn_in['ln_l_b'], 'L0_xattn_Wq': _L0_xattn_in['Wq'], 'L0_xattn_Wkv': _L0_xattn_in['Wkv'], 'L0_xattn_q_scale': _L0_xattn_in['q_scale'], 'L0_xattn_k_scale': _L0_xattn_in['k_scale'], 'L0_xattn_Wo': _L0_xattn_in['Wo'], 'L0_xattn_ln_o_w': _L0_xattn_in['ln_o_w'], 'L0_xattn_ln_o_b': _L0_xattn_in['ln_o_b'], 'L0_ffn_gate_w': _L0_ffn_in['gate_w'], 'L0_ffn_w1': _L0_ffn_in['w1'], 'L0_ffn_w2': _L0_ffn_in['w2'], 'L0_ffn_w3': _L0_ffn_in['w3'], 'L1_xattn_Wq': _L1_xattn_in['Wq'], 'L1_xattn_Wk': _L1_xattn_in['Wk'], 'L1_xattn_Wv': _L1_xattn_in['Wv'], 'L1_xattn_Wo': _L1_xattn_in['Wo'], 'L1_ffn_w_gate': _L1_ffn_in['w_gate'], 'L1_ffn_w_up': _L1_ffn_in['w_up'], 'L1_ffn_w_down': _L1_ffn_in['w_down']}

def reference(x, ctx_1024, mask_BxS2_bk0, L0_xattn_ln_x_w, L0_xattn_ln_x_b, L0_xattn_ln_l_w, L0_xattn_ln_l_b, L0_xattn_Wq, L0_xattn_Wkv, L0_xattn_q_scale, L0_xattn_k_scale, L0_xattn_Wo, L0_xattn_ln_o_w, L0_xattn_ln_o_b, L0_ffn_gate_w, L0_ffn_w1, L0_ffn_w2, L0_ffn_w3, L1_xattn_Wq, L1_xattn_Wk, L1_xattn_Wv, L1_xattn_Wo, L1_ffn_w_gate, L1_ffn_w_up, L1_ffn_w_down):
    import jax
    import jax.numpy as jnp

    def _L0_xattn_ref(x, latents, mask, ln_x_w, ln_x_b, ln_l_w, ln_l_b, Wq, Wkv, q_scale, k_scale, Wo, ln_o_w, ln_o_b):
        import jax, jax.numpy as jnp
        import numpy as np
        DIM, DIM_HEAD, HEADS, SCALE = (128, 64, 8, 8.0)
        INNER = DIM_HEAD * HEADS
        LN_EPS = 1e-05
        L2_EPS = 1e-12

        def layer_norm(x, w, b):
            mu = jnp.mean(x, axis=-1, keepdims=True)
            var = jnp.mean(jnp.square(x - mu), axis=-1, keepdims=True)
            return (x - mu) * jax.lax.rsqrt(var + LN_EPS) * w + b

        def l2norm(t):
            n = jnp.sqrt(jnp.sum(jnp.square(t), axis=-1, keepdims=True))
            return t / jnp.maximum(n, L2_EPS)
        b, n, _ = x.shape
        m = latents.shape[1]
        x = layer_norm(x, ln_x_w, ln_x_b)
        latents = layer_norm(latents, ln_l_w, ln_l_b)
        q = latents @ Wq
        kv_input = jnp.concatenate([x, latents], axis=1)
        kv = kv_input @ Wkv
        k, v = jnp.split(kv, 2, axis=-1)

        def to_heads(t):
            return t.reshape(t.shape[0], t.shape[1], HEADS, DIM_HEAD).transpose(0, 2, 1, 3)
        q, k, v = map(to_heads, (q, k, v))
        q = l2norm(q) * q_scale
        k = l2norm(k) * k_scale
        sim = jnp.einsum('bhid,bhjd->bhij', q, k) * SCALE
        full_mask = jnp.concatenate([mask, jnp.ones((b, m), dtype=bool)], axis=1)[:, None, None, :]
        max_neg = -jnp.finfo(sim.dtype).max
        sim = jnp.where(full_mask, sim, max_neg)
        attn = jax.nn.softmax(sim.astype(jnp.float32), axis=-1).astype(sim.dtype)
        out = jnp.einsum('bhij,bhjd->bhid', attn, v)
        out = out.transpose(0, 2, 1, 3).reshape(b, m, INNER)
        return layer_norm(out @ Wo, ln_o_w, ln_o_b)

    def _L0_ffn_ref(hidden_states, gate_w, w1, w2, w3):
        import jax, jax.numpy as jnp
        import numpy as np
        JITTER_EPS = 0.01

        def phi_routing(logits, jitter_eps=JITTER_EPS):
            m, sel = jax.lax.top_k(logits, 2)
            T, E = logits.shape
            m1 = m[:, :1]
            factor1 = jnp.maximum(jnp.abs(logits), m1)
            mask1 = (m1 - logits) / factor1 > 2.0 * jitter_eps
            p1 = jax.nn.softmax(jnp.where(mask1, -jnp.inf, logits), axis=-1)
            mult1 = jnp.take_along_axis(p1, sel[:, :1], axis=-1)
            m2 = m[:, 1:2]
            factor2 = jnp.maximum(jnp.abs(logits), m2)
            mask2 = (m2 - logits) / factor2 > 2.0 * jitter_eps
            drop_top1 = jnp.arange(E)[None, :] == sel[:, :1]
            p2 = jax.nn.softmax(jnp.where(mask2 | drop_top1, -jnp.inf, logits), axis=-1)
            mult2 = jnp.take_along_axis(p2, sel[:, 1:2], axis=-1)
            return (jnp.concatenate([mult1, mult2], axis=-1), sel)
        B, S, H = hidden_states.shape
        E = w1.shape[0]
        x = hidden_states.reshape(-1, H)
        logits = x @ gate_w.T
        routing_weights, selected = phi_routing(logits)
        T = x.shape[0]
        wte = jnp.zeros((T, E), x.dtype).at[jnp.arange(T)[:, None], selected].add(routing_weights)
        out = jnp.zeros_like(x)
        for e in range(E):
            h = jax.nn.silu(x @ w1[e].T) * (x @ w3[e].T)
            out = out + wte[:, e:e + 1] * (h @ w2[e].T)
        return out.reshape(B, S, H)

    def _L1_xattn_ref(x, context, Wq, Wk, Wv, Wo):
        import jax, jax.numpy as jnp
        import numpy as np
        DIM = 128
        H = 16
        DH = 64
        INNER = H * DH
        SCALE = DH ** (-0.5)
        B, L, _ = x.shape
        R = context.shape[1]
        q = (x @ Wq).reshape(B, L, H, DH).transpose(0, 2, 1, 3)
        k = (context @ Wk).reshape(B, R, H, DH).transpose(0, 2, 1, 3)
        v = (context @ Wv).reshape(B, R, H, DH).transpose(0, 2, 1, 3)
        scores = jnp.einsum('bhld,bhrd->bhlr', q, k) * SCALE
        attn = jax.nn.softmax(scores, axis=-1)
        out = jnp.einsum('bhlr,bhrd->bhld', attn, v)
        out = out.transpose(0, 2, 1, 3).reshape(B, L, INNER)
        return out @ Wo

    def _L1_ffn_ref(x, w_gate, w_up, w_down):
        import jax, jax.numpy as jnp
        import numpy as np
        BLOCK = 32
        W_BITS = 4
        ACT_BITS = 16

        def act_qdq(x):
            qmax = 2.0 ** (ACT_BITS - 1) - 1.0
            scale = jnp.maximum(jnp.max(jnp.abs(x)) / qmax, 1e-12)
            return jnp.clip(jnp.round(x / scale), -qmax - 1.0, qmax) * scale

        def fixed_qdq_u16(x):
            scale = 1.0 / 65536.0
            return jnp.clip(jnp.round(x / scale), 0.0, 65535.0) * scale

        def lpbq_dequant(w):
            O, I = w.shape
            qmax = 2.0 ** (W_BITS - 1) - 1.0
            wb = w.reshape(O, I // BLOCK, BLOCK)
            s = jnp.maximum(jnp.max(jnp.abs(wb), axis=-1, keepdims=True) / qmax, 1e-12)
            wq = jnp.clip(jnp.round(wb / s), -qmax - 1.0, qmax) * s
            return wq.reshape(O, I)
        x = act_qdq(x)
        up = act_qdq(x @ lpbq_dequant(w_up).T)
        gate = act_qdq(x @ lpbq_dequant(w_gate).T)
        sig = fixed_qdq_u16(jax.nn.sigmoid(gate))
        gate = act_qdq(gate * sig)
        o = act_qdq(gate * up)
        return o @ lpbq_dequant(w_down).T
    x = x + _L0_xattn_ref(ctx_1024, _layernorm(x, axis=-1), mask_BxS2_bk0, L0_xattn_ln_x_w, L0_xattn_ln_x_b, L0_xattn_ln_l_w, L0_xattn_ln_l_b, L0_xattn_Wq, L0_xattn_Wkv, L0_xattn_q_scale, L0_xattn_k_scale, L0_xattn_Wo, L0_xattn_ln_o_w, L0_xattn_ln_o_b)
    x = x + _L0_ffn_ref(_layernorm(x, axis=-1), L0_ffn_gate_w, L0_ffn_w1, L0_ffn_w2, L0_ffn_w3)
    x = x + _L1_xattn_ref(_layernorm(x, axis=-1), ctx_1024, L1_xattn_Wq, L1_xattn_Wk, L1_xattn_Wv, L1_xattn_Wo)
    x = x + _L1_ffn_ref(_layernorm(x, axis=-1), L1_ffn_w_gate, L1_ffn_w_up, L1_ffn_w_down)
    return x

_drawn_inputs = setup_inputs


def setup_inputs(seed=0):
    import zlib

    import numpy as np

    out = dict(_drawn_inputs(seed))
    spreads = {'L0_xattn_ln_x_w': (1.0, 0.2),
     'L0_xattn_ln_x_b': (0.0, 0.1),
     'L0_xattn_ln_l_w': (1.0, 0.2),
     'L0_xattn_ln_l_b': (0.0, 0.1),
     'L0_xattn_q_scale': (1.0, 0.2),
     'L0_xattn_k_scale': (1.0, 0.2),
     'L0_xattn_ln_o_w': (1.0, 0.2),
     'L0_xattn_ln_o_b': (0.0, 0.1)}
    factors = {'L0_ffn_gate_w': 6.211,
     'L0_ffn_w1': 5.336,
     'L0_ffn_w2': 5.295,
     'L0_ffn_w3': 5.289,
     'L1_ffn_w_gate': 8.0,
     'L1_ffn_w_up': 8.0,
     'L1_ffn_w_down': 8.0}
    for name, (base, spread) in spreads.items():
        noise = np.random.default_rng([zlib.crc32(name.encode()), seed]).standard_normal(out[name].shape)
        drawn = base * np.exp(spread * noise) if base else spread * noise
        out[name] = jnp.asarray(drawn.astype(out[name].dtype))
    for name, factor in factors.items():
        out[name] = (out[name] * factor).astype(out[name].dtype)
    return out
```

```python
from contextlib import ExitStack

import numpy as np
import concourse.bass as bass
from concourse import mybir

F32 = mybir.dt.float32
F32R = mybir.dt.float32r
BF16 = mybir.dt.bfloat16
I32 = mybir.dt.int32
U8 = mybir.dt.uint8
ALU = mybir.AluOpType
ACT = mybir.ActivationFunctionType
AX = mybir.AxisListType

NB, P, D = 8, 128, 128
TOK = NB * P
CR = 77
CTX = NB * CR
HALF = TOK // 2
CHALF = CTX // 2
H0, H1, DH = 8, 16, 64
C0, C1 = H0 * DH // P, H1 * DH // P
KEYS0 = P + CR
NE, FF = 8, 512
CF = FF // P
FFQ = 384
CQ = FFQ // P
QBLK = 32
YCOL = 512 - D
LN_EPS = 1e-5
L2_EPS2 = 1e-24
NEG = 1e30
MAGIC = 1.5 * 2.0 ** 23
QMAX = 32767.0
RSQRT_SEED = float(0x5F3759DF)


def two_layer_kernel(nc, a, out):
    ctx = ExitStack()
    with ctx:
        def sb(name, shape, dt=F32):
            return ctx.enter_context(nc.sbuf_tensor(name, shape, dt))

        def sem(name):
            return ctx.enter_context(nc.semaphore(name))

        ps = ctx.enter_context(nc.psum_tensor("ps", [P, 8, 512], F32))

        x = sb("x", [P, NB, D])
        xn = sb("xn", [P, NB, D])
        cn = sb("cn", [P, NB, D])
        feat = sb("feat", [P, 2, TOK + CTX], F32R)
        kt1 = sb("kt1", [P, C1, CTX])
        qk = sb("qk", [P, 8, TOK])
        kc = sb("kc", [P, C0, CTX])
        vv = sb("vv", [P, 16, 512])
        sq = sb("sq", [P, 4, 512])
        wraw = [sb(f"wraw{i}", [P, 1536]) for i in range(2)]
        wsp = [sb(f"wsp{i}", [P, 2, 1536], F32R) for i in range(2)]
        kv1w = sb("kv1w", [P, 2, 2048], F32R)
        pr = sb("pr", [P, 2048])
        pt = sb("pt", [P, 2, 512])
        ot = sb("ot", [P, C1, P])
        qst = sb("qst", [P, C1, P])
        kst = sb("kst", [P, C0 * KEYS0])
        ident = sb("ident", [P, P])
        lno = sb("lno", [P, 2, D])
        vec = sb("vec", [P, 6])
        qks = sb("qks", [P, 1])
        bones = sb("bones", [P, 2])
        gatew = sb("gatew", [P, NE])
        gatesp = sb("gatesp", [P, 2, NE], F32R)
        maskb = sb("maskb", [P, CTX], BF16)
        rowone = sb("rowone", [P, P], BF16)
        onesr = sb("onesr", [1, P])
        st = sb("st", [P, 16, 6])
        mv = sb("mv", [P, 16, 2])
        var = sb("var", [P, 16])
        rstd = sb("rstd", [P, 16])
        nt = sb("nt", [P, 192])
        rn = sb("rn", [P, 192])
        rqst = sb("rqst", [P, H0])
        mx = sb("mx", [P, H1])
        nbias = sb("nbias", [P, H0])
        sums = sb("sums", [P, H1])
        rsum = sb("rsum", [P, H1])
        wtes = sb("wtes", [P, NB])
        qs = sb("qs", [P, 24])
        grow = sb("grow", [1, 8])

        xf = x[:].rearrange("p b d -> p (b d)")
        xnf = xn[:].rearrange("p b d -> p (b d)")
        cnf = cn[:].rearrange("p b d -> p (b d)")
        ktf = kt1[:].rearrange("p c k -> p (c k)")
        featf = ktf[:, 0:TOK + CTX]
        qkf = qk[:].rearrange("p c k -> p (c k)")
        kcf = kc[:].rearrange("p c k -> p (c k)")
        vvf = vv[:].rearrange("p c k -> p (c k)")
        sqf = sq[:].rearrange("p c k -> p (c k)")
        wo1 = sqf[:, 0:C1 * D].rearrange("p (c d) -> p c d", c=C1)
        kstv0 = kst[:, 0:C0 * KEYS0].rearrange("p (c k) -> p c k", c=C0)
        kstv1 = kst[:, 0:C1 * CR].rearrange("p (c k) -> p c k", c=C1)
        prv0 = pr[:].rearrange("p (h k) -> p h k", h=H0)
        prv1 = pr[:].rearrange("p (h k) -> p h k", h=H1)
        silu = qkf[:, 0:1024].rearrange("p (s n) -> p s n", s=2)
        hid = qkf[:, 1024:2048].rearrange("p (s n) -> p s n", s=2)
        ytmp = qkf[:, 2048:3072].rearrange("p (s n) -> p s n", s=2)
        yacc = qkf[:, 3072:4096]
        wteb = qkf[:, 4096:5120]
        hidsp = kv1w[:].rearrange("p s n -> p (s n)")[:, 0:2048].rearrange("p (a s n) -> p a s n", a=2, s=2)
        NQ = CQ * TOK
        upb, gab, sgb, prb = qkf[:, 0:NQ], qkf[:, NQ:2 * NQ], vvf[:, 0:NQ], vvf[:, NQ:2 * NQ]
        osp = [wsp[0][:].rearrange("p s n -> p (s n)"), kv1w[:].rearrange("p s n -> p (s n)")]

        rkhi, rklo = feat[0:H0, 0, :], feat[0:H0, 1, :]
        hselr = wsp[1][0:H0, 0, 0:C0 * P]
        wo0 = sqf[:, C1 * D:(C1 + C0) * D].rearrange("p (c d) -> p c d", c=C0)
        wqn = kcf[:, 0:3 * CQ * D].rearrange("p (c d) -> p c d", d=D)
        rt = kcf[:, 3 * CQ * D:3 * CQ * D + 12 * NB * NE].rearrange("p (k n) -> p k n", n=NB * NE)
        hsel = pt[0:H0, 0, :]

        wqs = kcf[:, 2048:2048 + 9 * CQ * D // QBLK].rearrange("p (k n) -> p k n", k=3)
        n2 = kst[:, 0:192]
        mask8 = kst[0:1, 256:256 + CTX // 4].bitcast(U8)
        wtef = rt[:, 11, :]

        loads = {}

        def load_sem(name):
            loads[name] = sem("ld_" + name)
            return loads[name]

        for name in ("x", "ctx", "ident", "vec", "w0", "w0kv", "small", "mask", "wo0", "wqn", "lno", "gate",
                     "hsel", "ctxraw", "kv1k", "kv1v", "q1", "wo1"):
            load_sem(name)
        ld_moe = [sem("ld_moe0"), sem("ld_moe1")]
        s_out = sem("s_out")
        dv = sem("dve_chain")
        pl = sem("pool_chain")
        ac = sem("act_chain")
        s_norm1 = sem("lat_ctx_normed")
        s_trn1 = sem("feat1_in_psum")
        s_ff1 = sem("feat1_f32")
        s_fhi1 = sem("feat1_hi")
        s_flo1 = sem("feat1_lo")
        s_w0 = sem("w0_split")
        s_qks = sem("qk_scale")
        s_pq, s_pk, s_pv = sem("proj_q"), sem("proj_k"), sem("proj_v")
        s_qev, s_kev = sem("q_evacuated"), sem("k_evacuated")
        s_sqq, s_sqk = sem("q_squared"), sem("k_squared")
        s_n2q, s_n2k = sem("q_norms_psum"), sem("k_norms_psum")
        s_va, s_vd = sem("v_evac_act"), sem("v_evac_dve")
        s_rn = sem("head_rnorm")
        s_rkp, s_rkt, s_rkhi = sem("rk_rows_psum"), sem("rk_rows_split"), sem("rk_rows_hi")
        s_rkb, s_kfin = sem("rk_bcast_psum"), sem("k_final")
        s_mask, s_rone, s_padz = sem("mask_bias"), sem("ones_row"), sem("pad_zeroed")
        s_hsel = sem("hsel_r")
        s_st0 = sem("qk_staged0")
        s_s0, s_nb0, s_ex0 = sem("scores0"), sem("bias0"), sem("probs0")
        s_mx0 = sem("max0")
        s_pt0, s_pta0, s_ptd0 = sem("pt0_psum"), sem("pt0_sb_act"), sem("pt0_sb_dve")
        s_pv0, s_rs0, s_on0 = sem("pv0"), sem("rsum0"), sem("o0_scaled")
        s_ot0, s_ots0, s_y0, s_ys0 = sem("ot0_psum"), sem("ot0_sb"), sem("y0_psum"), sem("y0_sb")
        s_cs = sem("ctxraw_split")
        s_kv1w = sem("kv1_weights_split")
        s_k1, s_k1e, s_v1, s_v1e = sem("k1_psum"), sem("k1_sb"), sem("v1_psum"), sem("v1_sb")
        s_xn, s_xt, s_xhi, s_xlo = sem("x_normed"), sem("xt_psum"), sem("xt_hi"), sem("xt_lo")
        s_gw, s_lg, s_rex, s_rin = sem("gate_split"), sem("logits"), sem("route_exp"), sem("route_in")
        s_wte = sem("token_weights")
        s_msp = [sem("moe_split0"), sem("moe_split1")]
        s_g, s_u, s_sil, s_h = sem("moe_g"), sem("moe_u"), sem("moe_silu"), sem("moe_h")
        s_hhi, s_hlo, s_yy = sem("moe_h_hi"), sem("moe_h_lo"), sem("moe_y_step")
        s_wst, s_wb, s_wbs = sem("wte_staged"), sem("wte_bcast_psum"), sem("wte_bcast_sb")
        s_yt, s_ya = sem("y_weighted"), sem("y_added")
        s_msub = sem("moe_split_hi")
        s_yT = sem("moe_out_tok")
        s_wq, s_wqt, s_wqhi, s_wqf, s_wqlo = (sem("wq_dequant"), sem("wqT_psum"), sem("wqT_hi"), sem("wqT_f32"),
                                              sem("wqT_lo"))
        s_q1w = sem("q1w_split")
        s_q1, s_q1a, s_q1d = sem("q1_psum"), sem("q1_sb_act"), sem("q1_sb_dve")
        s_st1, s_s1, s_mx1, s_sub1 = sem("qk_staged1"), sem("scores1"), sem("max1"), sem("shifted1")
        s_ex1, s_rs1 = sem("probs1"), sem("rsum1")
        s_sum1 = sem("sum1")
        s_pt1, s_pta1, s_ptd1 = sem("pt1_psum"), sem("pt1_sb_act"), sem("pt1_sb_dve")
        s_pv1, s_on1, s_ot1, s_ota1, s_otd1 = (sem("pv1"), sem("o1_scaled"), sem("ot1_psum"), sem("ot1_sb_act"),
                                               sem("ot1_sb_dve"))
        s_y1, s_x3 = sem("y1_psum"), sem("x3")
        s_am, s_amt, s_gm, s_gmb = sem("absmax_col"), sem("absmax_row"), sem("absmax_all"), sem("absmax_bcast")
        s_xq, s_xqt, s_xqhi, s_xqlo = sem("x_ints"), sem("x_intsT"), sem("x_ints_hi"), sem("x_ints_lo")
        s_ug, s_uge, s_ugr = sem("upgate_psum"), sem("upgate_sb"), sem("upgate_absmax")
        s_gint, s_sig = sem("gate_ints"), sem("gate_sigmoid")
        s_ohi, s_olo, s_oint = sem("o_hi"), sem("o_lo"), sem("o_ints")
        s_dn, s_res = sem("down_psum"), sem("result")

        QKSEQ = []
        for c in range(C0):
            QKSEQ += [("q", c, 0), ("k", c, 0), ("q", c, 1), ("k", c, 1), ("k", c, 2), ("k", c, 3)]
        QSEQ = [g for g in QKSEQ if g[0] == "q"]
        KSEQ = [g for g in QKSEQ if g[0] == "k"]

        def cols(part):
            return (part * HALF, HALF) if part < 2 else (TOK + (part - 2) * CHALF, CHALF)

        def kdst(c, part):
            if part < 2:
                return qk[:, C0 + c, part * HALF:(part + 1) * HALF]
            return kc[:, c, (part - 2) * CHALF:(part - 1) * CHALF]

        def tile_cols(t):
            return (t * P, P) if t < NB else (TOK + (t - NB) * CR, CR)

        block = ctx.enter_context(nc.Block())

        @block.sync
        def _(sp):
            def load(dst, src, name):
                sp.dma_start(dst, src).then_inc(loads[name], 16)

            load(x[:], a["x"].rearrange("b t d -> t b d"), "x")
            load(cn[0:CR], a["ctx"].rearrange("b t d -> t b d"), "ctx")
            load(wraw[0][:, 0:512], a["Wq"], "w0")
            load(wraw[0][:, 512:1536], a["Wkv"], "w0kv")
            load(wraw[1][:, 0:1024], a["W1k"], "kv1k")
            load(lno[:], a["lno"], "lno")
            sp.wait_ge(s_w0, 2)
            load(wraw[0][:, 0:1024], a["W1v"], "kv1v")
            sp.wait_ge(s_flo1, 4)
            load(ktf[:, 0:CTX], a["ctxT"], "ctxraw")
            sp.wait_ge(s_n2q, len(QSEQ))
            sp.wait_ge(s_n2k, len(KSEQ))
            load(wo0, a["Wo"].rearrange("(c p) d -> p c d", p=P), "wo0")
            load(wo1, a["W1o"].rearrange("(c p) d -> p c d", p=P), "wo1")
            sp.wait_ge(s_kv1w, 4)
            for e in range(2):
                sp.dma_start(wraw[e][:], a["moe"][e]).then_inc(ld_moe[e], 16)
            sp.wait_ge(s_st0, 8 * NB)
            load(wqn[:, 0:CQ], a["wup"].rearrange("(c p) d -> p c d", p=P), "wqn")
            load(wqn[:, CQ:2 * CQ], a["wgate"].rearrange("(c p) d -> p c d", p=P), "wqn")
            load(wqn[:, 2 * CQ:3 * CQ], a["wdown"].rearrange("p (c k) -> p c k", c=CQ), "wqn")
            with sp.Fori(0, NE // 2 - 1) as i:
                for par in range(2):
                    sp.wait_ge(s_msp[par], i + 1)
                    sp.dma_start(wraw[par][:].unsqueeze(1), a["moe"].rearrange("e p n -> p e n")
                                 [:, bass.ds(i * 2 + (2 + par), 1), :]).then_inc(ld_moe[par], 16)
            sp.wait_ge(s_msp[0], NE // 2)
            load(wraw[0][:, 0:1024], a["W1q"], "q1")
            sp.wait_ge(s_res, 2)
            sp.dma_start(out.rearrange("b t d -> t b d"), xn[:]).then_inc(s_out, 16)
            sp.wait_ge(s_out, 16)

        @block.gpsimd
        def _(pool):
            g = nc.gpsimd
            n = [0]

            def link(ins):
                n[0] += 1
                ins.then_inc(pl, 1)
                pool.wait_ge(pl, n[0])

            g.memset(rowone[:], 0.0).then_inc(pl, 1)
            g.memset(maskb[:], 0.0).then_inc(pl, 1)
            n[0] = 2
            pool.wait_ge(pl, 2)
            g.memset(rowone[0:1, :], 1.0).then_inc(s_rone, 1)
            g.memset(onesr[:], 1.0).then_inc(s_rone, 1)
            g.memset(pr[:], 0.0).then_inc(s_padz, 1)
            pool.wait_ge(loads["mask"], 16)
            g.tensor_scalar(maskb[0:1, :], mask8, -1.0, NEG, ALU.add, ALU.mult).then_inc(s_mask, 1)

            def split(dst, lo_cols, raw, s):
                k, w = lo_cols
                link(g.tensor_copy(dst[:, 0, k:k + w], raw))
                g.tensor_tensor(dst[:, 1, k:k + w], raw, dst[:, 0, k:k + w].bitcast(F32), ALU.subtract).then_inc(s, 1)

            pool.wait_ge(loads["w0"], 16)
            split(wsp[0], (0, 512), wraw[0][:, 0:512], s_w0)
            pool.wait_ge(loads["w0kv"], 16)
            split(wsp[0], (512, 1024), wraw[0][:, 512:1536], s_w0)
            pool.wait_ge(loads["gate"], 16)
            split(gatesp, (0, NE), gatew[:], s_gw)
            pool.wait_ge(loads["kv1k"], 16)
            split(kv1w, (0, 512), wraw[1][:, 0:512], s_kv1w)
            split(kv1w, (512, 512), wraw[1][:, 512:1024], s_kv1w)
            pool.wait_ge(loads["kv1v"], 16)
            split(kv1w, (1024, 512), wraw[0][:, 0:512], s_kv1w)
            split(kv1w, (1536, 512), wraw[0][:, 512:1024], s_kv1w)

            def stage0(b, hf, first=False):
                c = slice(2 * hf, 2 * hf + 2)
                ck = slice(C0 + 2 * hf, C0 + 2 * hf + 2)
                if not first:
                    pool.wait_ge(s_s0, b * 2 + (hf - 1))
                g.tensor_copy(qst[:, c, :], qk[:, c, bass.ds(b * P, P)]).then_inc(s_st0, 1)
                g.tensor_copy(kstv0[:, c, 0:P], qk[:, ck, bass.ds(b * P, P)]).then_inc(s_st0, 1)
                g.tensor_copy(kstv0[:, c, P:KEYS0], kc[:, c, bass.ds(b * CR, CR)]).then_inc(s_st0, 1)
                if not first:
                    pool.wait_ge(s_ex0, b * 2 + (hf - 1))
                pool.wait_ge(s_rn, 1)
                g.tensor_copy(rqst[:, 4 * hf:4 * hf + 4], rn[:, bass.ds(b * H0 + 4 * hf, 4)]).then_inc(s_st0, 1)

            pool.wait_ge(s_qev, len(QSEQ))
            pool.wait_ge(s_kfin, len(KSEQ))
            stage0(0, 0, first=True)
            stage0(0, 1, first=True)
            with pool.Fori(1, NB) as b:
                stage0(b, 0)
                stage0(b, 1)

            pool.wait_ge(loads["ctxraw"], 16)
            pool.wait_ge(s_pk, len(KSEQ))
            pool.wait_ge(s_pv, 16)
            pool.wait_ge(s_rkb, len(KSEQ))
            split(feat, (TOK, CTX), ktf[:, 0:CTX], s_cs)

            for e in range(2):
                pool.wait_ge(ld_moe[e], 16)
                split(wsp[e], (0, 1536), wraw[e][:], s_msp[e])
            pool.wait_ge(s_wte, 1)

            def add_expert(e):
                for th in range(2):
                    pool.wait_ge(s_yt, e * 2 + (th + 1))
                    g.tensor_tensor(yacc[:, th * HALF:(th + 1) * HALF], yacc[:, th * HALF:(th + 1) * HALF],
                                    ytmp[:, th, :], ALU.add).then_inc(s_ya, 1)

            for th in range(2):
                g.memset(yacc[:, th * HALF:(th + 1) * HALF], 0.0).then_inc(s_ya, 1)
            with pool.Fori(0, NE // 2 - 1) as i:
                for par in range(2):
                    pool.wait_ge(s_msub, i * 2 + (1 + par))
                    g.tensor_tensor(wsp[par][:, 1, :], wraw[par][:], wsp[par][:, 0, :].bitcast(F32),
                                    ALU.subtract).then_inc(s_msp[par], 1)
                    e = i * 2 + par
                    pool.wait_ge(s_ya, e * 2 + 2)
                    add_expert(e)
            pool.wait_ge(loads["q1"], 16)
            pool.wait_ge(s_yy, 8 * (NE - 1))
            split(wsp[0], (0, 1024), wraw[0][:, 0:1024], s_q1w)
            for e in (NE - 2, NE - 1):
                pool.wait_ge(s_ya, e * 2 + 2)
                add_expert(e)

            pool.wait_ge(s_wqf, 3)
            pool.wait_ge(s_wqhi, 3)
            g.tensor_tensor(wsp[1][:, 1, 0:3 * CQ * D], wraw[1][:, 0:3 * CQ * D],
                            wsp[1][:, 0, 0:3 * CQ * D].bitcast(F32), ALU.subtract).then_inc(s_wqlo, 1)

            def stage1(b, hf, first=False):
                c = slice(4 * hf, 4 * hf + 4)
                if not first:
                    pool.wait_ge(s_s1, b * 2 + (hf - 1))
                pool.wait_ge(s_k1e, 2 * C1)
                g.tensor_copy(qst[:, c, :], qk[:, c, bass.ds(b * P, P)]).then_inc(s_st1, 1)
                g.tensor_copy(kstv1[:, c, :], kt1[:, c, bass.ds(b * CR, CR)]).then_inc(s_st1, 1)

            pool.wait_ge(s_q1a, 8)
            pool.wait_ge(s_q1d, 8)
            stage1(0, 0, first=True)
            stage1(0, 1, first=True)
            with pool.Fori(1, NB) as b:
                stage1(b, 0)
                stage1(b, 1)

        @block.scalar
        def _(act):
            s = nc.scalar

            def load(dst, src, name):
                act.dma_start(dst, src).then_inc(loads[name], 16)

            load(ident[:], a["ident"], "ident")
            load(vec[:], a["vec"], "vec")
            load(bones[:], a["bones"], "small")
            load(mask8, a["mask"], "mask")
            load(gatew[:], a["gateT"], "gate")
            load(hsel, a["hsel"], "hsel")
            act.wait_ge(loads["hsel"], 16)
            s.activation(hselr, hsel, ACT.Copy).then_inc(s_hsel, 1)

            for i in range(4):
                k, w = cols(i)
                act.wait_ge(s_ff1, i + 1)
                s.activation(feat[:, 0, k:k + w], featf[:, k:k + w], ACT.Copy).then_inc(s_fhi1, 1)
            nq = nk = 0
            act.wait_ge(s_qks, 1)
            for kind, c, part in QKSEQ:
                if kind == "q":
                    act.wait_ge(s_pq, nq + 1)
                    if nq >= 2:
                        act.wait_ge(s_n2q, nq - 1)
                    bank = ps[:, 4 + nq % 2, :]
                    s.activation(sq[:, nq % 2, :], bank, ACT.Square).then_inc(s_sqq, 1)
                    s.activation(qk[:, c, part * HALF:(part + 1) * HALF], bank, ACT.Identity,
                                 scale=qks[:]).then_inc(s_qev, 1)
                    nq += 1
                else:
                    w = cols(part)[1]
                    act.wait_ge(s_kev, nk + 1)
                    if nk >= 2:
                        act.wait_ge(s_n2k, nk - 1)
                    s.activation(sq[:, 2 + nk % 2, 0:w], kdst(c, part), ACT.Square).then_inc(s_sqk, 1)
                    nk += 1
            for t in range(0, 16, 2):
                r = tile_cols(t)[1]
                act.wait_ge(s_pv, t + 1)
                s.activation(vv[0:r, t, :], ps[0:r, 4 + (t // 2) % 2, :], ACT.Copy).then_inc(s_va, 1)
            for i in range(4):
                k, w = cols(i)
                act.wait_ge(s_rkp, i + 1)
                s.activation(rkhi[:, k:k + w], ps[0:H0, i, 0:w], ACT.Copy).then_inc(s_rkhi, 1)

            def exps0(b, hf):
                act.wait_ge(s_nb0, b * 2 + (hf + 1))
                for h in range(4 * hf, 4 * hf + 4):
                    j, i = h % 2, (h // 2) % 2
                    ins = s.activation(prv0[:, h, 0:KEYS0], ps[:, 2 * hf + j, i * KEYS0:(i + 1) * KEYS0], ACT.Exp,
                                       bias=nbias[:, h:h + 1], scale=rqst[:, h:h + 1], accum_out=sums[:, h:h + 1])
                ins.then_inc(s_ex0, 1)

            def ot_evac0(b):
                act.wait_ge(s_ot0, b + 1)
                s.activation(ot[:, 0:C0, :], ps[:, 7, :], ACT.Copy).then_inc(s_ots0, 1)

            def body0(b, first=False, last=False):
                if not last:
                    act.wait_ge(s_pt0, b * 4 + 2)
                    act.wait_ge(s_rs0, b * 2 + 1)
                    exps0(b + 1, 0)
                if not first:
                    ot_evac0(b - 1)
                if not last:
                    act.wait_ge(s_pt0, b * 4 + 4)
                    act.wait_ge(s_rs0, b * 2 + 2)
                    exps0(b + 1, 1)

            act.wait_ge(s_padz, 1)
            exps0(0, 0)
            exps0(0, 1)
            body0(0, first=True)
            with act.Fori(1, NB - 1) as b:
                body0(b)
            body0(NB - 1, last=True)
            ot_evac0(NB - 1)

            def k1_evac(i):
                c, half = i // 2, i % 2
                act.wait_ge(s_k1, i + 1)
                s.activation(kt1[:, c, half * CHALF:(half + 1) * CHALF], ps[:, i % 2, 0:CHALF],
                             ACT.Copy).then_inc(s_k1e, 1)

            def v1_evac(i):
                act.wait_ge(s_v1, i + 1)
                s.activation(vv[0:CR, i, :], ps[0:CR, i % 2, :], ACT.Copy).then_inc(s_v1e, 1)

            act.wait_ge(s_cs, 1)
            for i in range(2 * C1):
                k1_evac(i)
            for i in range(2 * NB):
                v1_evac(i)

            def feat_hi(n0):
                for i in range(2):
                    act.wait_ge(s_xt, n0 + i + 1)
                    s.activation(feat[:, 0, i * HALF:(i + 1) * HALF], ps[:, 2 + i, :], ACT.Copy).then_inc(s_xhi, 1)

            feat_hi(0)
            for i in range(2):
                act.wait_ge(s_rin, i + 1)
                s.activation(rt[:, 6 + i, :], rt[:, 6 + i, :], ACT.Exp).then_inc(s_rex, 1)

            def moe(e):
                for i in range(8):
                    slot = i % 2
                    act.wait_ge(s_g, e * 8 + (i + 1))
                    if isinstance(e, int) and e == 0 and i < 2:
                        pass
                    else:
                        act.wait_ge(s_h, e * 8 + (i - 1))
                    s.activation(silu[:, slot, :], ps[:, slot, :], ACT.Silu).then_inc(s_sil, 1)
                    if i == 5:
                        for th in range(2):
                            act.wait_ge(s_wb, e * 2 + (th + 1))
                            if not (isinstance(e, int) and e == 0):
                                act.wait_ge(s_yt, e * 2)
                            s.activation(wteb[:, th * HALF:(th + 1) * HALF], ps[:, 6 + th, :],
                                         ACT.Copy).then_inc(s_wbs, 1)
                    act.wait_ge(s_h, e * 8 + (i + 1))
                    if not (isinstance(e, int) and e == 0 and i < 2):
                        act.wait_ge(s_yy, e * 8 + (i - 1))
                    s.activation(hidsp[:, 0, slot, :], hid[:, slot, :], ACT.Copy).then_inc(s_hhi, 1)

            moe(0)
            with act.Fori(1, NE) as e:
                moe(e)

            for i in range(3):
                act.wait_ge(s_wqt, i + 1)
                s.activation(wsp[1][:, 0, i * FFQ:(i + 1) * FFQ], ps[:, 4 + i, 0:FFQ], ACT.Copy).then_inc(s_wqhi, 1)
                s.activation(wraw[1][:, i * FFQ:(i + 1) * FFQ], ps[:, 4 + i, 0:FFQ], ACT.Copy).then_inc(s_wqf, 1)
            feat_hi(2)
            for i in range(0, 16, 2):
                c, half = i % C1, i // C1
                act.wait_ge(s_q1, i + 1)
                s.activation(qk[:, c, half * HALF:(half + 1) * HALF], ps[:, 4 + (i // 2) % 2, :], ACT.Copy,
                             scale=DH ** -0.5).then_inc(s_q1a, 1)

            def exps1(b, hf):
                act.wait_ge(s_sub1, b * 2 + (hf + 1))
                v = prv1[:, 8 * hf:8 * hf + 8, 0:CR]
                s.activation(v, v, ACT.Exp).then_inc(s_ex1, 1)

            def pt_evac1(b, g):
                act.wait_ge(s_pt1, b * 4 + (g + 1))
                if not (isinstance(b, int) and b == 0 and g < 2):
                    act.wait_ge(s_pv1, b * 4 + (g - 1))
                s.activation(pt[0:CR, g % 2, :], ps[0:CR, 4 + g % 2, :], ACT.Copy).then_inc(s_pta1, 1)

            def ot_evac1(b, k):
                act.wait_ge(s_ot1, b * 2 + (k + 1))
                s.activation(ot[:, 4 * k:4 * k + 4, :], ps[:, 4 + k, :], ACT.Copy).then_inc(s_ota1, 1)

            def body1(b, first=False, last=False):
                pt_evac1(b, 0)
                pt_evac1(b, 1)
                if not first:
                    ot_evac1(b - 1, 0)
                if not last:
                    exps1(b + 1, 0)
                if not first:
                    ot_evac1(b - 1, 1)
                pt_evac1(b, 2)
                pt_evac1(b, 3)
                if not last:
                    exps1(b + 1, 1)

            exps1(0, 0)
            exps1(0, 1)
            body1(0, first=True)
            with act.Fori(1, NB - 1) as b:
                body1(b)
            body1(NB - 1, last=True)
            ot_evac1(NB - 1, 0)
            ot_evac1(NB - 1, 1)

            for i in range(2):
                act.wait_ge(s_xqt, i + 1)
                s.activation(feat[:, 0, i * HALF:(i + 1) * HALF], ps[:, i, :], ACT.Copy).then_inc(s_xqhi, 1)
            for i in range(4 * CQ):
                dst = upb if i < 2 * CQ else gab
                k = i % (2 * CQ)
                act.wait_ge(s_ug, i + 1)
                s.activation(dst[:, k * HALF:(k + 1) * HALF], ps[:, 2 + i % 4, :], ACT.Copy).then_inc(s_uge, 1)
            for c in range(CQ):
                act.wait_ge(s_gint, c + 1)
                s.activation(sgb[:, c * TOK:(c + 1) * TOK], gab[:, c * TOK:(c + 1) * TOK], ACT.Sigmoid,
                             scale=qs[:, 7:8]).then_inc(s_sig, 1)
            for c in range(CQ):
                act.wait_ge(s_oint, c + 1)
                s.activation(osp[0][:, c * TOK:(c + 1) * TOK], gab[:, c * TOK:(c + 1) * TOK], ACT.Copy)\
                    .then_inc(s_ohi, 1)

        @block.vector
        def _(dve):
            v = nc.vector
            n = [0]

            def link(*steps):
                n[0] += 1
                steps[-1].then_inc(dv, 1)
                dve.wait_ge(dv, n[0])

            def rsqrt(y, xx, t):
                link(v.tensor_scalar(t.bitcast(I32), xx.bitcast(I32), 1, None, ALU.logical_shift_right))
                link(v.tensor_scalar(y.bitcast(I32), t.bitcast(I32), -1.0, RSQRT_SEED, ALU.mult, ALU.add))
                for step in range(3):
                    link(v.tensor_tensor(t, y, y, ALU.mult))
                    link(v.scalar_tensor_tensor(out=t, in0=xx, scalar=-0.5, in1=t, op0=ALU.mult, op1=ALU.mult))
                    last = v.scalar_tensor_tensor(out=y, in0=t, scalar=1.5, in1=y, op0=ALU.add, op1=ALU.mult)
                    if step < 2:
                        link(last)
                return last

            def layer_norm(sets, eps=LN_EPS):
                for dst, src, rows, k in sets:
                    for t in range(NB):
                        i1 = v.bn_stats(st[0:rows, k + t, :], src[0:rows, t, :])
                link(i1)
                for dst, src, rows, k in sets:
                    for t in range(NB):
                        i1 = v.bn_aggr(mv[0:rows, k + t, :], st[0:rows, k + t, :])
                link(i1)
                for dst, src, rows, k in sets:
                    i1 = v.tensor_scalar(var[0:rows, k:k + NB], mv[0:rows, k:k + NB, 1], eps, None, ALU.add)
                link(i1)
                lo, hi = min(k for *_, k in sets), max(k for *_, k in sets) + NB
                link(rsqrt(rstd[:, lo:hi], var[:, lo:hi], nt[:, lo:hi]))
                for dst, src, rows, k in sets:
                    for t in range(NB):
                        i1 = v.tensor_scalar(dst[0:rows, t, :], src[0:rows, t, :], mv[0:rows, k + t, 0:1],
                                             rstd[0:rows, k + t:k + t + 1], ALU.subtract, ALU.mult)
                return i1

            v.memset(n2, 1.0)
            link(v.memset(var[:], 1.0))
            dve.wait_ge(loads["x"], 16)
            link(layer_norm([(xn, x, P, 0)]))
            layer_norm([(xn, xn, P, 0)]).then_inc(s_norm1, 1)
            dve.wait_ge(loads["ctx"], 16)
            dve.wait_ge(s_norm1, 1)
            layer_norm([(cn, cn, CR, 8)]).then_inc(s_norm1, 1)
            dve.wait_ge(loads["vec"], 16)
            v.scalar_tensor_tensor(out=qks[:], in0=vec[:, 4:5], scalar=8.0, in1=vec[:, 5:6], op0=ALU.mult,
                                   op1=ALU.mult).then_inc(s_qks, 1)

            def feat_affine(i):
                k, w = cols(i)
                wb = 2 if i < 2 else 0
                dve.wait_ge(s_trn1, i + 1)
                v.tensor_scalar(featf[:, k:k + w], ps[:, i, 0:w], vec[:, wb:wb + 1], vec[:, wb + 1:wb + 2], ALU.mult,
                                ALU.add).then_inc(s_ff1, 1)

            def feat_lo(i):
                k, w = cols(i)
                dve.wait_ge(s_ff1, i + 1)
                dve.wait_ge(s_fhi1, i + 1)
                v.tensor_tensor(feat[:, 1, k:k + w], featf[:, k:k + w], feat[:, 0, k:k + w].bitcast(F32),
                                ALU.subtract).then_inc(s_flo1, 1)

            feat_affine(0)
            feat_affine(1)
            feat_lo(0)
            feat_affine(2)
            feat_lo(1)
            feat_affine(3)
            feat_lo(2)
            feat_lo(3)
            for i, (_, c, part) in enumerate(KSEQ):
                w = cols(part)[1]
                dve.wait_ge(s_pk, i + 1)
                v.tensor_copy(kdst(c, part), ps[:, i % 2, 0:w]).then_inc(s_kev, 1)
            dve.wait_ge(s_n2q, len(QSEQ))
            dve.wait_ge(s_n2k, len(KSEQ))
            v.tensor_scalar(n2[:, 0:128], ps[:, 6, 0:128], L2_EPS2, None, ALU.max)
            link(v.tensor_scalar(n2[0:CR, 128:192], ps[0:CR, 6, 128:192], L2_EPS2, None, ALU.max))
            rsqrt(rn[:], n2, nt[:]).then_inc(s_rn, 1)
            for t in range(1, 16, 2):
                r = tile_cols(t)[1]
                dve.wait_ge(s_pv, t + 1)
                v.tensor_copy(vv[0:r, t, :], ps[0:r, (t // 2) % 2, :]).then_inc(s_vd, 1)
            for i in range(4):
                k, w = cols(i)
                dve.wait_ge(s_rkhi, i + 1)
                v.tensor_tensor(rklo[:, k:k + w], ps[0:H0, i, 0:w], rkhi[:, k:k + w].bitcast(F32),
                                ALU.subtract).then_inc(s_rkt, 1)
            for i, (_, c, part) in enumerate(KSEQ):
                w = cols(part)[1]
                dve.wait_ge(s_rkb, i + 1)
                v.tensor_tensor(kdst(c, part), kdst(c, part), ps[:, 4 + i % 2, 0:w], ALU.mult).then_inc(s_kfin, 1)

            def smax0(b, hf):
                dve.wait_ge(s_s0, b * 2 + (hf + 1))
                dve.wait_ge(s_st0, b * 8 + (4 * hf + 4))
                v.tensor_reduce(mx[:, 4 * hf:4 * hf + 4].rearrange("p (i j) -> p j i", j=2),
                                ps[:, 2 * hf:2 * hf + 2, 0:2 * KEYS0].rearrange("p j (i k) -> p j i k", i=2),
                                AX.X, ALU.max, negate=True).then_inc(s_mx0, 1)
                dve.wait_ge(s_mx0, b * 2 + (hf + 1))
                v.tensor_tensor(nbias[:, 4 * hf:4 * hf + 4], mx[:, 4 * hf:4 * hf + 4], rqst[:, 4 * hf:4 * hf + 4],
                                ALU.mult).then_inc(s_nb0, 1)

            def pt_evac0(b, g):
                dve.wait_ge(s_pt0, b * 4 + (g + 1))
                if not (isinstance(b, int) and b == 0 and g < 2):
                    dve.wait_ge(s_pv0, b * 4 + (g - 1))
                v.tensor_copy(pt[:, g % 2, :], ps[:, 4 + g % 2, :]).then_inc(s_ptd0, 1)

            def rsum0(b, k):
                dve.wait_ge(s_ex0, b * 2 + (k + 1))
                if not (isinstance(b, int) and b == 0):
                    dve.wait_ge(s_on0, b)
                v.reciprocal(rsum[:, 4 * k:4 * k + 4], sums[:, 4 * k:4 * k + 4]).then_inc(s_rs0, 1)

            def scale0(b, first=False):
                dve.wait_ge(s_pv0, b * 4 + 4)
                dve.wait_ge(s_rs0, b * 2 + 2)
                if not first:
                    dve.wait_ge(s_ot0, b)
                v.tensor_tensor(cnf[:, 0:512].rearrange("p (h d) -> p h d", h=H0),
                                ps[:, 6, :].rearrange("p (h d) -> p h d", h=H0),
                                rsum[:, 0:H0].unsqueeze(2).to_broadcast([P, H0, DH]), ALU.mult).then_inc(s_on0, 1)

            def y_evac0(b):
                dve.wait_ge(s_y0, b + 1)
                dve.wait_ge(s_y0, 1)
                v.tensor_copy(xnf[:, bass.ds(b * D, D)], ps[:, 7, 0:D]).then_inc(s_ys0, 1)

            def body0(b, first=False, last=False):
                rsum0(b, 0)
                pt_evac0(b, 0)
                pt_evac0(b, 1)
                if not last:
                    smax0(b + 1, 0)
                rsum0(b, 1)
                pt_evac0(b, 2)
                pt_evac0(b, 3)
                if not last:
                    smax0(b + 1, 1)
                if not first:
                    y_evac0(b - 1)
                scale0(b, first)

            smax0(0, 0)
            smax0(0, 1)
            body0(0, first=True)
            with dve.Fori(1, NB - 1) as b:
                body0(b)
            body0(NB - 1, last=True)
            y_evac0(NB - 1)

            dve.wait_ge(s_ys0, NB)
            link(layer_norm([(xn, xn, P, 0)]))
            dve.wait_ge(loads["lno"], 16)
            link(v.tensor_tensor(xn[:], xn[:], lno[:, 0:1, :].to_broadcast([P, NB, D]), ALU.mult))
            link(v.tensor_tensor(xn[:], xn[:], lno[:, 1:2, :].to_broadcast([P, NB, D]), ALU.add))
            link(v.tensor_tensor(xf, xf, xnf, ALU.add))
            layer_norm([(xn, x, P, 0)]).then_inc(s_xn, 1)

            def feat_lo_x(n0):
                for i in range(2):
                    dve.wait_ge(s_xhi, n0 + i + 1)
                    v.tensor_tensor(feat[:, 1, i * HALF:(i + 1) * HALF], ps[:, 2 + i, :],
                                    feat[:, 0, i * HALF:(i + 1) * HALF].bitcast(F32), ALU.subtract).then_inc(s_xlo, 1)

            feat_lo_x(0)

            def R(i):
                return rt[:, i, :].rearrange("p (b e) -> p b e", e=NE)

            def bc(col):
                return col.unsqueeze(2).to_broadcast([P, NB, NE])

            LOG, EQ1, LOG2, EQ2, T, ABS, E1, E2, RANK, CAND = range(10)
            small = rt[:, 10, :].rearrange("p (k b) -> p k b", b=NB)
            M1, M2, S1, S2, C1_, C2_ = (small[:, i, :] for i in range(6))
            rank_c = rt[:, RANK, :].rearrange("p (b e) -> p b e", e=NE)
            for e in range(NE):
                i1 = v.memset(rank_c[:, :, e], float(NE - e))
            dve.wait_ge(s_lg, 1)
            link(v.tensor_copy(rt[:, LOG, :], ps[:, 4, 0:64]))
            link(v.scalar_tensor_tensor(out=R(ABS), in0=R(LOG), scalar=-1.0, in1=R(LOG), op0=ALU.mult, op1=ALU.max))

            def choose(src, m, cand_col, eq):
                link(v.tensor_reduce(m, R(src), AX.X, ALU.max))
                link(v.tensor_tensor(R(T), R(src), bc(m), ALU.is_equal))
                link(v.tensor_tensor(R(T), R(T), R(RANK), ALU.mult))
                link(v.tensor_reduce(cand_col, R(T), AX.X, ALU.max))
                link(v.tensor_tensor(R(eq), R(T), bc(cand_col), ALU.is_equal))

            def softmax_in(src, m, e):
                v.tensor_tensor(R(e), R(src), bc(m), ALU.subtract).then_inc(s_rin, 1)

            def keep_sum(m, e, ssum, drop):
                link(v.tensor_tensor(R(T), R(ABS), bc(m), ALU.max))
                link(v.tensor_tensor(R(CAND), bc(m), R(LOG), ALU.subtract))
                link(v.scalar_tensor_tensor(out=R(T), in0=R(T), scalar=0.02, in1=R(CAND), op0=ALU.mult,
                                            op1=ALU.is_ge))
                if drop is not None:
                    link(v.scalar_tensor_tensor(out=R(CAND), in0=R(drop), scalar=0.0, in1=R(T), op0=ALU.is_equal,
                                                op1=ALU.mult))
                    keep = CAND
                else:
                    keep = T
                link(v.tensor_tensor(R(CAND), R(keep), R(e), ALU.mult))
                link(v.tensor_reduce(ssum, R(CAND), AX.X, ALU.add))
                link(v.reciprocal(ssum, ssum))

            choose(LOG, M1, C1_, EQ1)
            softmax_in(LOG, M1, E1)
            link(v.scalar_tensor_tensor(out=R(LOG2), in0=R(EQ1), scalar=-NEG, in1=R(LOG), op0=ALU.mult,
                                        op1=ALU.add))
            choose(LOG2, M2, C2_, EQ2)
            softmax_in(LOG2, M2, E2)
            dve.wait_ge(s_rex, 1)
            keep_sum(M1, E1, S1, None)
            dve.wait_ge(s_rex, 2)
            keep_sum(M2, E2, S2, EQ1)
            link(v.tensor_tensor(R(EQ1), R(EQ1), bc(S1), ALU.mult))
            link(v.tensor_tensor(R(EQ2), R(EQ2), bc(S2), ALU.mult))
            v.tensor_tensor(wtef.rearrange("p (e b) -> p b e", b=NB), R(EQ1), R(EQ2), ALU.add).then_inc(s_wte, 1)
            dve.wait_ge(s_wte, 1)

            def weigh(e, first=False):
                for th in range(2):
                    dve.wait_ge(s_yy, e * 8 + (7 + th))
                    dve.wait_ge(s_wbs, e * 2 + (th + 1))
                    if not first:
                        dve.wait_ge(s_ya, e * 2 + 2)
                    v.tensor_tensor(ytmp[:, th, :], ps[:, 4 + th, :], wteb[:, th * HALF:(th + 1) * HALF],
                                    ALU.mult).then_inc(s_yt, 1)

            def moe(e, first=False, loaded=None, par=None):
                for i in range(8):
                    slot = i % 2
                    if i == 2 and not first:
                        weigh_prev(e)
                    if i == 2 and loaded is not None:
                        dve.wait_ge(ld_moe[par], loaded)
                        dve.wait_ge(s_yy, e * 8)
                        v.tensor_copy(wsp[par][:, 0, :], wraw[par][:]).then_inc(s_msub, 1)
                    dve.wait_ge(s_u, e * 8 + (i + 1))
                    dve.wait_ge(s_sil, e * 8 + (i + 1))
                    if not (first and i < 2):
                        dve.wait_ge(s_hhi, e * 8 + (i - 1))
                        dve.wait_ge(s_hlo, e * 8 + (i - 1))
                    v.tensor_tensor(hid[:, slot, :], silu[:, slot, :], ps[:, 2 + slot, :], ALU.mult).then_inc(s_h, 1)
                    dve.wait_ge(s_hhi, e * 8 + (i + 1))
                    v.tensor_tensor(hidsp[:, 1, slot, :], hid[:, slot, :], hidsp[:, 0, slot, :].bitcast(F32),
                                    ALU.subtract).then_inc(s_hlo, 1)
                    if i == 1:
                        if not first:
                            dve.wait_ge(s_wb, e * 2)
                            dve.wait_ge(s_wte, 1)
                        v.tensor_copy(wtes[:], wtef[:, bass.ds(e * NB, NB)]).then_inc(s_wst, 1)

            def weigh_prev(e):
                weigh(e - 1, first=isinstance(e, int) and e == 1)

            moe(0, first=True)
            moe(1, loaded=32, par=0)
            dve.wait_ge(loads["wqn"], 48)
            wblk = wqn.rearrange("p c (k w) -> p (c k) w", w=QBLK)
            nblk = 3 * CQ * D // QBLK
            wmax, wscale, winv = (wqs[:, i, :] for i in range(3))

            def wbc(col):
                return col.unsqueeze(2).to_broadcast([P, nblk, QBLK])

            link(v.tensor_reduce(wmax, wblk, AX.X, ALU.max, apply_absolute_value=True))
            link(v.tensor_scalar(wscale, wmax, 1.0 / 7.0, 1e-12, ALU.mult, ALU.max))
            link(v.reciprocal(winv, wscale))
            link(v.tensor_tensor(wblk, wblk, wbc(winv), ALU.mult))
            link(v.tensor_scalar(wblk, wblk, MAGIC, MAGIC, ALU.add, ALU.subtract))
            v.tensor_tensor(wblk, wblk, wbc(wscale), ALU.mult).then_inc(s_wq, 1)

            with dve.Fori(1, NE // 2 - 1) as i:
                moe(i * 2, loaded=i * 16 + 16, par=1)
                moe(i * 2 + 1, loaded=i * 16 + 32, par=0)
            moe(NE - 2, loaded=16 * (NE // 2), par=1)
            moe(NE - 1)
            weigh(NE - 1)

            for i in range(2):
                dve.wait_ge(s_yT, i + 1)
                i1 = v.tensor_tensor(xf[:, i * HALF:(i + 1) * HALF], xf[:, i * HALF:(i + 1) * HALF], ps[:, i, :],
                                     ALU.add)
            link(i1)
            layer_norm([(xn, x, P, 0)]).then_inc(s_xn, 1)
            feat_lo_x(2)
            for i in range(1, 16, 2):
                c, half = i % C1, i // C1
                dve.wait_ge(s_q1, i + 1)
                v.tensor_scalar(qk[:, c, half * HALF:(half + 1) * HALF], ps[:, (i // 2) % 2, :], DH ** -0.5, None,
                                ALU.mult).then_inc(s_q1d, 1)

            def sub1(b, hf):
                def S():
                    return ps[:, 2 * hf:2 * hf + 2, 0:4 * CR].rearrange("p j (i k) -> p j i k", i=4)

                m = mx[:, 8 * hf:8 * hf + 8].rearrange("p (i j) -> p j i", j=2)
                dve.wait_ge(s_s1, b * 2 + (hf + 1))
                v.tensor_reduce(m, S(), AX.X, ALU.max).then_inc(s_mx1, 1)
                dve.wait_ge(s_mx1, b * 2 + (hf + 1))
                v.tensor_tensor(prv1[:, 8 * hf:8 * hf + 8, 0:CR].rearrange("p (i j) k -> p j i k", j=2), S(),
                                m.unsqueeze(3).to_broadcast([P, 2, 4, CR]), ALU.subtract).then_inc(s_sub1, 1)

            def sums1(b, k):
                dve.wait_ge(s_ex1, b * 2 + (k + 1))
                if not (isinstance(b, int) and b == 0):
                    dve.wait_ge(s_on1, b * 2 + (k - 1))
                h = slice(8 * k, 8 * k + 8)
                v.tensor_reduce(sums[:, h], prv1[:, h, 0:CR], AX.X, ALU.add).then_inc(s_sum1, 1)
                dve.wait_ge(s_sum1, b * 2 + (k + 1))
                v.reciprocal(rsum[:, h], sums[:, h]).then_inc(s_rs1, 1)

            def scale1(b, k, first=False):
                dve.wait_ge(s_pv1, b * 4 + (2 * k + 2))
                dve.wait_ge(s_rs1, b * 2 + (k + 1))
                if not first:
                    dve.wait_ge(s_ot1, b * 2 + (k - 1))
                v.tensor_tensor(cnf[:, 512 * k:512 * k + 512].rearrange("p (h d) -> p h d", h=8),
                                ps[:, 6 + k, :].rearrange("p (h d) -> p h d", h=8),
                                rsum[:, 8 * k:8 * k + 8].unsqueeze(2).to_broadcast([P, 8, DH]),
                                ALU.mult).then_inc(s_on1, 1)

            def add_y1(b):
                dve.wait_ge(s_y1, b + 1)
                xb = xf[:, bass.ds(b * D, D)]
                v.tensor_tensor(xb, xb, ps[:, 0, YCOL:YCOL + D], ALU.add).then_inc(s_x3, 1)

            def body1(b, first=False, last=False):
                sums1(b, 0)
                if not last:
                    dve.wait_ge(s_pt1, b * 4 + 2)
                    sub1(b + 1, 0)
                scale1(b, 0, first)
                sums1(b, 1)
                if not last:
                    dve.wait_ge(s_pt1, b * 4 + 4)
                    sub1(b + 1, 1)
                if not first:
                    add_y1(b - 1)
                scale1(b, 1, first)

            sub1(0, 0)
            sub1(0, 1)
            body1(0, first=True)
            with dve.Fori(1, NB - 1) as b:
                body1(b)
            body1(NB - 1, last=True)
            add_y1(NB - 1)

            dve.wait_ge(s_x3, NB)
            link(layer_norm([(xn, x, P, 0)]))
            gcount = [0]

            def global_scale(col, inv, scale, unit):
                k = gcount[0]
                gcount[0] += 1
                col.then_inc(s_am, 1)
                dve.wait_ge(s_amt, k + 1)
                v.tensor_reduce(grow[:, 0:1], ps[0:1, 7, 0:P], AX.X, ALU.max).then_inc(s_gm, 1)
                dve.wait_ge(s_gmb, k + 1)
                if unit is None:
                    link(v.tensor_scalar(scale, ps[:, 7, 0:1], 1.0 / QMAX, 1e-12, ALU.mult, ALU.max))
                    link(v.reciprocal(inv, scale))
                else:
                    link(v.tensor_scalar(scale, ps[:, 7, 0:1], unit, 1.0 / QMAX, ALU.mult, ALU.mult))
                    link(v.tensor_scalar(scale, scale, 1e-12, None, ALU.max))
                    link(v.reciprocal(inv, scale))
                    link(v.tensor_scalar(inv, inv, unit, None, ALU.mult))

            def q(i):
                return qs[:, i:i + 1]

            SX, IX, SU, IU, SG, IG, SG2, IG2, SO, IO, USG, UO = 1, 2, 3, 4, 7, 8, 9, 10, 11, 12, 13, 14
            v_abs = dict(apply_absolute_value=True)
            global_scale(v.tensor_reduce(q(0), xnf, AX.X, ALU.max, **v_abs), q(IX), q(SX), None)
            link(v.tensor_scalar(xnf, xnf, q(IX), MAGIC, ALU.mult, ALU.add))
            v.tensor_scalar(xnf, xnf, MAGIC, None, ALU.subtract).then_inc(s_xq, 1)
            for i in range(2):
                dve.wait_ge(s_xqhi, i + 1)
                v.tensor_tensor(feat[:, 1, i * HALF:(i + 1) * HALF], ps[:, i, :],
                                feat[:, 0, i * HALF:(i + 1) * HALF].bitcast(F32), ALU.subtract).then_inc(s_xqlo, 1)
            for i in range(4 * CQ):
                src = upb if i < 2 * CQ else gab
                k = i % (2 * CQ)
                dve.wait_ge(s_uge, i + 1)
                i1 = v.tensor_reduce(rt[:, 0, i:i + 1], src[:, k * HALF:(k + 1) * HALF], AX.X, ALU.max, **v_abs)
            link(i1)
            global_scale(v.tensor_reduce(q(0), rt[:, 0, 2 * CQ:4 * CQ], AX.X, ALU.max), q(IG), q(SG), q(SX))
            for c in range(CQ):
                w = gab[:, c * TOK:(c + 1) * TOK]
                link(v.tensor_scalar(w, w, q(IG), MAGIC, ALU.mult, ALU.add))
                v.tensor_scalar(w, w, MAGIC, None, ALU.subtract).then_inc(s_gint, 1)
            global_scale(v.tensor_reduce(q(0), rt[:, 0, 0:2 * CQ], AX.X, ALU.max), q(IU), q(SU), q(SX))
            link(v.tensor_scalar(upb, upb, q(IU), MAGIC, ALU.mult, ALU.add))
            for c in range(CQ):
                w, gi = sgb[:, c * TOK:(c + 1) * TOK], gab[:, c * TOK:(c + 1) * TOK]
                dve.wait_ge(s_sig, c + 1)
                link(v.tensor_scalar(w, w, 65536.0, MAGIC, ALU.mult, ALU.add))
                link(v.tensor_scalar(w, w, MAGIC + 65535.0, MAGIC, ALU.min, ALU.max))
                dve.wait_ge(s_gint, CQ)
                link(v.scalar_tensor_tensor(out=gi, in0=w, scalar=MAGIC, in1=gi, op0=ALU.subtract, op1=ALU.mult))
                link(v.tensor_reduce(rt[:, 1, c:c + 1], gi, AX.X, ALU.max, **v_abs))
            link(v.tensor_scalar(q(USG), q(SG), 1.0 / 65536.0, None, ALU.mult))
            global_scale(v.tensor_reduce(q(0), rt[:, 1, 0:CQ], AX.X, ALU.max), q(IG2), q(SG2), q(USG))
            link(v.tensor_scalar(gab, gab, q(IG2), MAGIC, ALU.mult, ALU.add))
            link(v.tensor_scalar(gab, gab, MAGIC, None, ALU.subtract))
            link(v.scalar_tensor_tensor(out=gab, in0=upb, scalar=MAGIC, in1=gab, op0=ALU.subtract, op1=ALU.mult))
            link(v.tensor_scalar(q(UO), q(SG2), q(SU), None, ALU.mult))
            global_scale(v.tensor_reduce(q(0), gab, AX.X, ALU.max, **v_abs), q(IO), q(SO), q(UO))
            for c in range(CQ):
                w = gab[:, c * TOK:(c + 1) * TOK]
                link(v.tensor_scalar(w, w, q(IO), MAGIC, ALU.mult, ALU.add))
                v.tensor_scalar(w, w, MAGIC, None, ALU.subtract).then_inc(s_oint, 1)
            for c in range(CQ):
                dve.wait_ge(s_ohi, c + 1)
                dve.wait_ge(s_oint, c + 1)
                v.tensor_tensor(osp[1][:, c * TOK:(c + 1) * TOK], gab[:, c * TOK:(c + 1) * TOK],
                                osp[0][:, c * TOK:(c + 1) * TOK].bitcast(F32), ALU.subtract).then_inc(s_olo, 1)
            for i in range(2):
                dve.wait_ge(s_dn, i + 1)
                v.scalar_tensor_tensor(out=xnf[:, i * HALF:(i + 1) * HALF], in0=ps[:, i, :], scalar=q(SO),
                                       in1=xf[:, i * HALF:(i + 1) * HALF], op0=ALU.mult, op1=ALU.add)\
                    .then_inc(s_res, 1)

        @block.tensor
        def _(pe):
            t_ = nc.tensor

            def mm3(dst, lhs, rhs, start=True, stop=True, **kw):
                t_.matmul(dst, lhs[0], rhs[1], start=start, stop=False, **kw)
                t_.matmul(dst, lhs[1], rhs[0], start=False, stop=False, **kw)
                return t_.matmul(dst, lhs[0], rhs[0], start=False, stop=stop, **kw)

            def two(buf, k, w):
                return buf[:, 0, k:k + w], buf[:, 1, k:k + w]

            pe.wait_ge(loads["ident"], 16)
            pe.wait_ge(s_norm1, 1)
            for t in range(NB):
                ins = t_.transpose(ps[:, t // 4, (t % 4) * P:(t % 4 + 1) * P], xn[:, t, :], ident[:])
                if t % 4 == 3:
                    ins.then_inc(s_trn1, 1)
            pe.wait_ge(s_norm1, 2)
            for t in range(NB):
                ins = t_.transpose(ps[:, 2 + t // 4, (t % 4) * CR:(t % 4 + 1) * CR], cn[0:CR, t, :],
                                   ident[0:CR, 0:CR])
                if t % 4 == 3:
                    ins.then_inc(s_trn1, 1)

            pe.wait_ge(loads["small"], 16)
            pe.wait_ge(s_w0, 1)
            pe.wait_ge(s_ff1, 2)
            cnt = {"q": 0, "k": 0}
            ncnt = {"q": 0, "k": 0}

            def proj(kind, c, part):
                i = cnt[kind]
                cnt[kind] += 1
                k, w = cols(part)
                pe.wait_ge(s_flo1, part + 1)
                if kind == "k":
                    pe.wait_ge(s_w0, 2)
                    if i >= 2:
                        pe.wait_ge(s_kev, i - 1)
                elif i >= 2:
                    pe.wait_ge(s_qev, i - 1)
                bank = ps[:, (4 if kind == "q" else 0) + i % 2, 0:w]
                wcol = (0 if kind == "q" else 512) + c * P
                mm3(bank, two(wsp[0], wcol, P), two(feat, k, w)).then_inc(s_pq if kind == "q" else s_pk, 1)

            def norms(kind, c, part):
                i = ncnt[kind]
                ncnt[kind] += 1
                pe.wait_ge(s_sqq if kind == "q" else s_sqk, i + 1)
                slot = (0 if kind == "q" else 2) + i % 2
                rows = P if part < 2 else CR
                base = 0 if kind == "q" else (64 if part < 2 else 128)
                for j in range(4):
                    b = (part % 2) * 4 + j
                    k = base + b * H0 + 2 * c
                    ins = t_.matmul(ps[0:rows, 6, k:k + 2], sq[:, slot, j * rows:(j + 1) * rows], bones[:],
                                    start=True, stop=True)
                ins.then_inc(s_n2q if kind == "q" else s_n2k, 1)

            LAG = 3
            for i, g in enumerate(QKSEQ):
                proj(*g)
                if i >= LAG:
                    norms(*QKSEQ[i - LAG])
            for g in QKSEQ[-LAG:]:
                norms(*g)
            pe.wait_ge(s_qev, len(QSEQ))
            pe.wait_ge(s_kev, len(KSEQ))
            for t in range(16):
                k, w = tile_cols(t)
                m = t // 2
                if m >= 2:
                    pe.wait_ge(s_va if t % 2 == 0 else s_vd, m - 1)
                mm3(ps[0:w, (4 if t % 2 == 0 else 0) + m % 2, :], two(feat, k, w), two(wsp[0], 1024, 512))\
                    .then_inc(s_pv, 1)
            pe.wait_ge(s_rn, 1)
            pe.wait_ge(s_vd, 8)
            pe.wait_ge(s_ff1, 4)
            for t in range(16):
                k, w = tile_cols(t)
                part = (t // 4)
                ins = t_.transpose(ps[0:H0, part, (t % 4) * w:(t % 4 + 1) * w],
                                   rn[0:w, 64 + t * H0:64 + (t + 1) * H0], ident[0:w, 0:w])
                if t % 4 == 3:
                    ins.then_inc(s_rkp, 1)
            pe.wait_ge(s_hsel, 1)
            pe.wait_ge(s_va, 8)
            for i, (_, c, part) in enumerate(KSEQ):
                k, w = cols(part)
                pe.wait_ge(s_rkt, part + 1)
                pe.wait_ge(s_rkhi, part + 1)
                if i >= 2:
                    pe.wait_ge(s_kfin, i - 1)
                bank = ps[:, 4 + i % 2, 0:w]
                t_.matmul(bank, hselr[:, c * P:(c + 1) * P], rklo[:, k:k + w], start=True, stop=False)
                t_.matmul(bank, hselr[:, c * P:(c + 1) * P], rkhi[:, k:k + w], start=False, stop=True)\
                    .then_inc(s_rkb, 1)

            def scores0(b, hf):
                pe.wait_ge(s_st0, b * 8 + (4 * hf + 3))
                if not (isinstance(b, int) and b == 0):
                    pe.wait_ge(s_ex0, b * 2 + (hf - 1))
                for i in range(2):
                    for j in range(2):
                        c = 2 * hf + i
                        t_.matmul(ps[:, 2 * hf + j, i * KEYS0:(i + 1) * KEYS0], qst[DH * j:DH * (j + 1), c, :],
                                  kstv0[DH * j:DH * (j + 1), c, :], start=(i == 0), stop=False,
                                  skip_group_check=True)
                mask = maskb[:, bass.ds(b * CR, CR)]
                for j in range(2):
                    for i in range(2):
                        ins = t_.matmul(ps[:, 2 * hf + j, i * KEYS0 + P:(i + 1) * KEYS0], rowone[:], mask,
                                        start=False, stop=(i == 1), skip_group_check=True)
                ins.then_inc(s_s0, 1)

            def pts0(b, g):
                pe.wait_ge(s_ex0, b * 2 + (g // 2 + 1))
                if not (isinstance(b, int) and b == 0 and g < 2):
                    pe.wait_ge(s_ptd0, b * 4 + (g - 1))
                for i in range(2):
                    for j in range(2):
                        ins = t_.transpose(ps[:, 4 + g % 2, (2 * i + j) * P:(2 * i + j + 1) * P],
                                           prv0[:, 2 * g + i, j * P:(j + 1) * P], ident[:])
                ins.then_inc(s_pt0, 1)

            def pv0(b, g):
                pe.wait_ge(s_ptd0, b * 4 + (g + 1))
                if not (isinstance(b, int) and b == 0) and g == 0:
                    pe.wait_ge(s_on0, b)
                for i in range(2):
                    h = 2 * g + i
                    dst = ps[:, 6, h * DH:(h + 1) * DH]
                    t_.matmul(dst, pt[:, g % 2, 2 * i * P:(2 * i + 1) * P],
                              vvf[:, bass.ds(b * 512 + h * DH, DH)], start=True, stop=False,
                              skip_group_check=True)
                    ins = t_.matmul(dst, pt[0:CR, g % 2, (2 * i + 1) * P:(2 * i + 2) * P],
                                    vvf[0:CR, bass.ds(b * 512 + (8 * 512 + h * DH), DH)], start=False,
                                    stop=True, skip_group_check=True)
                ins.then_inc(s_pv0, 1)

            def ot0(b):
                pe.wait_ge(s_on0, b + 1)
                for c in range(C0):
                    ins = t_.transpose(ps[:, 7, c * P:(c + 1) * P], cnf[:, c * P:(c + 1) * P], ident[:])
                ins.then_inc(s_ot0, 1)

            def y0(b):
                pe.wait_ge(s_ots0, b + 1)
                for c in range(C0):
                    ins = t_.matmul(ps[:, 7, 0:D], ot[:, c, :], wo0[:, c, :], start=(c == 0), stop=(c == C0 - 1))
                ins.then_inc(s_y0, 1)

            def body0(b, first=False, last=False):
                pts0(b, 0)
                pts0(b, 1)
                if not last:
                    scores0(b + 1, 0)
                pv0(b, 0)
                pv0(b, 1)
                if not first:
                    ot0(b - 1)
                pts0(b, 2)
                pts0(b, 3)
                if not last:
                    scores0(b + 1, 1)
                pv0(b, 2)
                if not first:
                    y0(b - 1)
                pv0(b, 3)

            pe.wait_ge(loads["wo0"], 16)
            pe.wait_ge(s_mask, 1)
            pe.wait_ge(s_rone, 2)
            scores0(0, 0)
            scores0(0, 1)
            body0(0, first=True)
            with pe.Fori(1, NB - 1) as b:
                body0(b)
            body0(NB - 1, last=True)
            ot0(NB - 1)
            y0(NB - 1)

            pe.wait_ge(s_cs, 1)
            pe.wait_ge(s_kv1w, 4)
            pe.wait_ge(s_ex0, 2 * NB)
            for i in range(2 * C1):
                c, half = i // 2, i % 2
                if i >= 2:
                    pe.wait_ge(s_k1e, i - 1)
                mm3(ps[:, i % 2, 0:CHALF], two(kv1w, c * P, P), two(feat, TOK + half * CHALF, CHALF))\
                    .then_inc(s_k1, 1)
            pe.wait_ge(s_k1e, 2 * C1)
            for i in range(2 * NB):
                b, half = i // 2, i % 2
                if i >= 2:
                    pe.wait_ge(s_v1e, i - 1)
                mm3(ps[0:CR, i % 2, :], two(feat, TOK + b * CR, CR), two(kv1w, 1024 + half * 512, 512))\
                    .then_inc(s_v1, 1)

            def feat_t(k):
                pe.wait_ge(s_xn, k)
                for t in range(NB):
                    ins = t_.transpose(ps[:, 2 + t // 4, (t % 4) * P:(t % 4 + 1) * P], xn[:, t, :], ident[:])
                    if t % 4 == 3:
                        ins.then_inc(s_xt, 1)

            feat_t(1)
            pe.wait_ge(s_gw, 1)
            pe.wait_ge(s_xlo, 2)
            for t in range(NB):
                ins = mm3(ps[:, 4, t * NE:(t + 1) * NE], two(feat, t * P, P), two(gatesp, 0, NE))
            ins.then_inc(s_lg, 1)

            def gu(e, par, i):
                c, th = i // 2, i % 2
                if not (isinstance(e, int) and e == 0 and i < 2):
                    pe.wait_ge(s_sil, e * 8 + (i - 1))
                rhs = two(feat, th * HALF, HALF)
                mm3(ps[:, i % 2, :], two(wsp[par], c * P, P), rhs).then_inc(s_g, 1)
                if not (isinstance(e, int) and e == 0 and i < 2):
                    pe.wait_ge(s_h, e * 8 + (i - 1))
                ins = mm3(ps[:, 2 + i % 2, :], two(wsp[par], FF + c * P, P), rhs)
                ins.then_inc(s_u, 1)

            def y(e, par, i):
                c, th = i // 2, i % 2
                pe.wait_ge(s_hhi, e * 8 + (i + 1))
                pe.wait_ge(s_hlo, e * 8 + (i + 1))
                if c == 0:
                    if not (isinstance(e, int) and e == 0):
                        pe.wait_ge(s_yt, e * 2 + (th - 1))
                    else:
                        pe.wait_ge(s_wte, 1)
                ins = mm3(ps[:, 4 + th, :], two(wsp[par], 2 * FF + c * P, P),
                          (hidsp[:, 0, i % 2, :], hidsp[:, 1, i % 2, :]), start=(c == 0), stop=(c == CF - 1))
                ins.then_inc(s_yy, 1)
                return ins

            def expert(e, par, next_ready):
                for i in range(8):
                    if i + 2 < 8:
                        gu(e, par, i + 2)
                    elif next_ready is not None:
                        if i == 6:
                            pe.wait_ge(s_msp[1 - par], next_ready)
                        gu(e + 1, 1 - par, i - 6)
                    y(e, par, i)
                    if i == 4:
                        pe.wait_ge(s_wst, e + 1)
                        if not (isinstance(e, int) and e == 0):
                            pe.wait_ge(s_wbs, e * 2)
                        for t in range(NB):
                            ins = t_.transpose(ps[:, 6 + t // 4, (t % 4) * P:(t % 4 + 1) * P],
                                               wtes[:, t:t + 1].to_broadcast([P, P]), ident[:])
                            if t % 4 == 3:
                                ins.then_inc(s_wb, 1)

            pe.wait_ge(s_msp[0], 1)
            pe.wait_ge(s_v1e, 2 * NB)
            gu(0, 0, 0)
            gu(0, 0, 1)
            expert(0, 0, 1)
            expert(1, 1, 2)
            with pe.Fori(1, NE // 2 - 1) as i:
                expert(i * 2, 0, i + 1)
                expert(i * 2 + 1, 1, i + 2)
            expert(NE - 2, 0, NE // 2)
            expert(NE - 1, 1, None)

            pe.wait_ge(s_wq, 1)
            pe.wait_ge(s_yt, 2 * NE)
            pe.wait_ge(s_wbs, 2 * NE)
            for i in range(3):
                for c in range(CQ):
                    ins = t_.transpose(ps[:, 4 + i, c * P:(c + 1) * P], wqn[:, i * CQ + c, :], ident[:])
                ins.then_inc(s_wqt, 1)
            pe.wait_ge(s_ya, 2 * NE + 2)
            for t in range(NB):
                ins = t_.transpose(ps[:, t // 4, (t % 4) * P:(t % 4 + 1) * P], yacc[:, t * P:(t + 1) * P], ident[:])
                if t % 4 == 3:
                    ins.then_inc(s_yT, 1)
            feat_t(2)
            pe.wait_ge(s_q1w, 1)
            pe.wait_ge(s_wqf, 3)
            for i in range(2 * C1):
                c, half = i % C1, i // C1
                pe.wait_ge(s_xlo, 3 + half)
                if i // 2 >= 2:
                    pe.wait_ge(s_q1a if i % 2 == 0 else s_q1d, i // 2 - 1)
                mm3(ps[:, (4 if i % 2 == 0 else 0) + (i // 2) % 2, :], two(wsp[0], c * P, P),
                    two(feat, half * HALF, HALF)).then_inc(s_q1, 1)

            def scores1(b, hf):
                pe.wait_ge(s_st1, b * 4 + (2 * hf + 2))
                if not (isinstance(b, int) and b == 0):
                    pe.wait_ge(s_sub1, b * 2 + (hf - 1))
                    if hf == 0 and not (isinstance(b, int) and b < 3):
                        pe.wait_ge(s_x3, b - 2)
                for i in range(4):
                    for j in range(2):
                        c = 4 * hf + i
                        ins = t_.matmul(ps[:, 2 * hf + j, i * CR:(i + 1) * CR], qst[DH * j:DH * (j + 1), c, :],
                                        kstv1[DH * j:DH * (j + 1), c, :], start=True, stop=True,
                                        skip_group_check=True)
                ins.then_inc(s_s1, 1)

            def pts1(b, g):
                pe.wait_ge(s_ex1, b * 2 + (g // 2 + 1))
                if g < 2:
                    if not (isinstance(b, int) and b == 0):
                        pe.wait_ge(s_pta1, b * 4 + (g - 1))
                elif not (isinstance(b, int) and b == 0):
                    pe.wait_ge(s_ota1, b * 2 + (g - 3))
                for i in range(4):
                    ins = t_.transpose(ps[0:CR, 4 + g % 2, i * P:(i + 1) * P], prv1[:, 4 * g + i, 0:CR], ident[:])
                ins.then_inc(s_pt1, 1)

            def pv1(b, g):
                pe.wait_ge(s_pta1, b * 4 + (g + 1))
                if not (isinstance(b, int) and b == 0) and g % 2 == 0:
                    pe.wait_ge(s_on1, b * 2 + (g // 2 - 1))
                for i in range(4):
                    h = 4 * g + i
                    k = (h % 8) * DH
                    ins = t_.matmul(ps[:, 6 + g // 2, k:k + DH], pt[0:CR, g % 2, i * P:(i + 1) * P],
                                    vvf[0:CR, bass.ds(b * 1024 + h * DH, DH)], start=True, stop=True,
                                    skip_group_check=True)
                ins.then_inc(s_pv1, 1)

            def ot1(b, k):
                pe.wait_ge(s_on1, b * 2 + (k + 1))
                for c in range(4):
                    ins = t_.transpose(ps[:, 4 + k, c * P:(c + 1) * P], cnf[:, (4 * k + c) * P:(4 * k + c + 1) * P],
                                       ident[:])
                ins.then_inc(s_ot1, 1)

            def y1(b, last_scores=None):
                pe.wait_ge(s_ota1, b * 2 + 2)
                pe.wait_ge(s_sub1, b * 2 + 5 if last_scores is None else last_scores)
                if last_scores == 2 * NB:
                    pe.wait_ge(s_x3, b)
                for c in range(C1):
                    ins = t_.matmul(ps[:, 0, YCOL:YCOL + D], ot[:, c, :], wo1[:, c, :], start=(c == 0),
                                    stop=(c == C1 - 1), skip_group_check=True)
                ins.then_inc(s_y1, 1)

            def body1(b, first=False, last=False):
                pts1(b, 0)
                pts1(b, 1)
                if not last:
                    scores1(b + 1, 0)
                pv1(b, 0)
                if not first:
                    ot1(b - 1, 0)
                pv1(b, 1)
                if not first:
                    ot1(b - 1, 1)
                if not last:
                    scores1(b + 1, 1)
                pts1(b, 2)
                pts1(b, 3)
                if not first:
                    y1(b - 1, 2 * NB if last else None)
                pv1(b, 2)
                pv1(b, 3)

            pe.wait_ge(loads["wo1"], 16)
            pe.wait_ge(s_q1a, C1)
            pe.wait_ge(s_q1d, C1)
            scores1(0, 0)
            scores1(0, 1)
            body1(0, first=True)
            body1(1)
            with pe.Fori(2, NB - 1) as b:
                body1(b)
            body1(NB - 1, last=True)
            pe.wait_ge(s_pta1, 4 * NB)
            ot1(NB - 1, 0)
            ot1(NB - 1, 1)
            y1(NB - 1, 2 * NB)

            gcount = [0]

            def global_max():
                k = gcount[0]
                gcount[0] += 1
                pe.wait_ge(s_am, k + 1)
                t_.transpose(ps[0:1, 7, 0:P], qs[:, 0:1], ident[:]).then_inc(s_amt, 1)
                pe.wait_ge(s_gm, k + 1)
                t_.matmul(ps[:, 7, 0:1], onesr[:], grow[:, 0:1], start=True, stop=True).then_inc(s_gmb, 1)

            global_max()
            pe.wait_ge(s_xq, 1)
            for t in range(NB):
                ins = t_.transpose(ps[:, t // 4, (t % 4) * P:(t % 4 + 1) * P], xn[:, t, :], ident[:])
                if t % 4 == 3:
                    ins.then_inc(s_xqt, 1)
            pe.wait_ge(s_wqlo, 1)
            for i in range(4 * CQ):
                pe.wait_ge(s_xqlo, i % 2 + 1)
                if i >= 4:
                    pe.wait_ge(s_uge, i - 3)
                mm3(ps[:, 2 + i % 4, :], two(wsp[1], (i // 2) * P, P), two(feat, (i % 2) * HALF, HALF))\
                    .then_inc(s_ug, 1)
            for _ in range(4):
                global_max()
            for t in range(NB):
                for c in range(CQ):
                    if t == 0:
                        pe.wait_ge(s_olo, c + 1)
                    k = c * TOK + t * P
                    ins = mm3(ps[:, t // 4, (t % 4) * P:(t % 4 + 1) * P], (osp[0][:, k:k + P], osp[1][:, k:k + P]),
                              two(wsp[1], (2 * CQ + c) * P, P), start=(c == 0), stop=(c == CQ - 1))
                if t % 4 == 3:
                    ins.then_inc(s_dn, 1)


def kernel(**inputs):
    import concourse.bacc as _bacc
    from concourse.bass_utils import run_bass_kernel_spmd as _run

    g = {k: np.asarray(v) for k, v in inputs.items()}
    f32 = np.float32
    arrays = {
        "x": g["x"], "ctx": g["ctx_1024"],
        "ctxT": g["ctx_1024"].reshape(CTX, D).T,
        "mask": g["mask_BxS2_bk0"].reshape(1, CTX),
        "vec": np.stack([g["L0_xattn_ln_x_w"], g["L0_xattn_ln_x_b"], g["L0_xattn_ln_l_w"], g["L0_xattn_ln_l_b"],
                         np.tile(g["L0_xattn_q_scale"], 2), np.tile(g["L0_xattn_k_scale"], 2)], axis=1),
        "lno": np.broadcast_to(np.stack([g["L0_xattn_ln_o_w"], g["L0_xattn_ln_o_b"]]), (P, 2, D)),
        "Wq": g["L0_xattn_Wq"], "Wkv": g["L0_xattn_Wkv"], "Wo": g["L0_xattn_Wo"],
        "gateT": g["L0_ffn_gate_w"].T,
        "moe": np.concatenate([g["L0_ffn_w1"].transpose(0, 2, 1), g["L0_ffn_w3"].transpose(0, 2, 1),
                               g["L0_ffn_w2"].transpose(0, 2, 1).reshape(NE, CF, P, D).transpose(0, 2, 1, 3)
                               .reshape(NE, P, CF * D)], axis=2),
        "W1q": g["L1_xattn_Wq"], "W1k": g["L1_xattn_Wk"], "W1v": g["L1_xattn_Wv"], "W1o": g["L1_xattn_Wo"],
        "wup": g["L1_ffn_w_up"], "wgate": g["L1_ffn_w_gate"], "wdown": g["L1_ffn_w_down"],
        "ident": np.eye(P, dtype=f32),
        "bones": np.repeat(np.eye(2, dtype=f32), DH, axis=0),
        "hsel": np.repeat(np.eye(H0, dtype=f32), DH, axis=1),
    }
    arrays = {k: np.ascontiguousarray(v) for k, v in arrays.items()}
    nc = _bacc.Bacc("TRN2", target_bir_lowering=False, num_devices=1)
    aps = {k: nc.dram_tensor(f"in_{k}", v.shape, mybir.dt.from_np(v.dtype), kind="ExternalInput").ap()
           for k, v in arrays.items()}
    out = nc.dram_tensor("out_dram", (NB, P, D), F32, kind="ExternalOutput").ap()
    two_layer_kernel(nc, aps, out)
    r = _run(nc, [{f"in_{k}": v for k, v in arrays.items()}], core_ids=[0])
    return r.results[0]["out_dram"]
```

```python
from contextlib import ExitStack

import numpy as np
import concourse.bass as bass
from concourse import mybir

F32 = mybir.dt.float32
F32R = mybir.dt.float32r
BF16 = mybir.dt.bfloat16
I32 = mybir.dt.int32
U8 = mybir.dt.uint8
ALU = mybir.AluOpType
ACT = mybir.ActivationFunctionType
AX = mybir.AxisListType

NB, P, D = 8, 128, 128
TOK = NB * P
CR = 77
CTX = NB * CR
HALF = TOK // 2
CHALF = CTX // 2
H0, H1, DH = 8, 16, 64
C0, C1 = H0 * DH // P, H1 * DH // P
KEYS0 = P + CR
NE, FF = 8, 512
CF = FF // P
MP = 3
FFQ = 384
CQ = FFQ // P
QBLK = 32
YCOL = 512 - D
LN_EPS = 1e-5
L2_EPS2 = 1e-24
NEG = 1e30
MAGIC = 1.5 * 2.0 ** 23
QMAX = 32767.0
RSQRT_SEED = float(0x5F3759DF)


def two_layer_kernel(nc, a, out):
    ctx = ExitStack()
    with ctx:
        def sb(name, shape, dt=F32):
            return ctx.enter_context(nc.sbuf_tensor(name, shape, dt))

        def sem(name):
            return ctx.enter_context(nc.semaphore(name))

        ps = ctx.enter_context(nc.psum_tensor("ps", [P, 8, 512], F32))

        x = sb("x", [P, NB, D])
        xn = sb("xn", [P, NB, D])
        cn = sb("cn", [P, NB, D])
        feat = sb("feat", [P, 2, TOK + CTX], F32R)
        kt1 = sb("kt1", [P, C1, CTX])
        qk = sb("qk", [P, 8, TOK])
        kc = sb("kc", [P, C0, CTX])
        vv = sb("vv", [P, 16, 512])
        sq = sb("sq", [P, 4, 512])
        wraw = [sb(f"wraw{i}", [P, 1536]) for i in range(2)]
        wsp = [sb(f"wsp{i}", [P, 2, 1536], F32R) for i in range(2)]
        kv1w = sb("kv1w", [P, 2, 2048], F32R)
        pr = sb("pr", [P, 2048])
        pt = sb("pt", [P, 2, 512])
        ot = sb("ot", [P, C1, P])
        qst = sb("qst", [P, C1, P])
        kst = sb("kst", [P, C0 * KEYS0])
        ident = sb("ident", [P, P])
        lno = sb("lno", [P, 2, D])
        vec = sb("vec", [P, 6])
        qks = sb("qks", [P, 1])
        bones = sb("bones", [P, 2])
        gatew = sb("gatew", [P, NE])
        gatesp = sb("gatesp", [P, 2, NE], F32R)
        maskb = sb("maskb", [P, CTX], BF16)
        rowone = sb("rowone", [P, P], BF16)
        st = sb("st", [P, 16, 6])
        mv = sb("mv", [P, 16, 2])
        var = sb("var", [P, 16])
        rstd = sb("rstd", [P, 16])
        nmr = sb("nmr", [P, NB])
        nt = sb("nt", [P, 192])
        rn = sb("rn", [P, 192])
        rqst = sb("rqst", [P, H0])
        mx = sb("mx", [P, H1])
        nbias = sb("nbias", [P, H0])
        sums = sb("sums", [P, H1])
        rsum = sb("rsum", [P, H1])
        wtes = sb("wtes", [P, NB])
        qs = sb("qs", [P, 24])
        magic = sb("magic", [P, 4])

        xf = x[:].rearrange("p b d -> p (b d)")
        xnf = xn[:].rearrange("p b d -> p (b d)")
        cnf = cn[:].rearrange("p b d -> p (b d)")
        ktf = kt1[:].rearrange("p c k -> p (c k)")
        featf = ktf[:, 0:TOK + CTX]
        qkf = qk[:].rearrange("p c k -> p (c k)")
        kcf = kc[:].rearrange("p c k -> p (c k)")
        vvf = vv[:].rearrange("p c k -> p (c k)")
        sqf = sq[:].rearrange("p c k -> p (c k)")
        wo1 = sqf[:, 0:C1 * D].rearrange("p (c d) -> p c d", c=C1)
        kstv0 = kst[:, 0:C0 * KEYS0].rearrange("p (c k) -> p c k", c=C0)
        kstv1 = wraw[0][:, 0:C1 * 2 * CR].rearrange("p (c k) -> p c k", c=C1)
        prv0 = pr[:].rearrange("p (h k) -> p h k", h=H0)
        prv1 = pr[:].rearrange("p (h k) -> p h k", h=H1)
        silu = qkf[:, 0:1024].rearrange("p (s n) -> p s n", s=2)
        hid = qkf[:, 1024:2048].rearrange("p (s n) -> p s n", s=2)
        ytmp = qkf[:, 2048:3072].rearrange("p (s n) -> p s n", s=2)
        yacc = qkf[:, 3072:4096]
        wteb = qkf[:, 4096:5120]
        hidsp = kv1w[:].rearrange("p s n -> p (s n)")[:, 0:2048].rearrange("p (a s n) -> p a s n", a=2, s=2)
        NQ = CQ * TOK
        upb, gab, sgb, prb = qkf[:, 0:NQ], qkf[:, NQ:2 * NQ], vvf[:, 0:NQ], vvf[:, NQ:2 * NQ]
        SX, IX, SU, IU, SG, IG, SG2, IG2, SO, IO, UX = range(1, 12)

        rkhi, rklo = feat[0:H0, 0, :], feat[0:H0, 1, :]
        hselr = wsp[1][0:H0, 0, 0:C0 * P]
        wo0 = sqf[:, C1 * D:(C1 + C0) * D].rearrange("p (c d) -> p c d", c=C0)
        wqn = kcf[:, 0:3 * CQ * D].rearrange("p (c d) -> p c d", d=D)
        rt = kcf[:, 3 * CQ * D:3 * CQ * D + 12 * NB * NE].rearrange("p (k n) -> p k n", n=NB * NE)
        hsel = pt[0:H0, 0, :]

        wqs = kcf[:, 2048:2048 + 9 * CQ * D // QBLK].rearrange("p (k n) -> p k n", k=3)
        n2 = kst[:, 0:192]
        mask8 = kst[0:1, 256:256 + CTX // 4].bitcast(U8)
        wtef = rt[:, 11, :]

        loads = {}

        def load_sem(name):
            loads[name] = sem("ld_" + name)
            return loads[name]

        for name in ("x", "ctx", "ident", "vec", "w0", "w0kv", "small", "mask", "wo0", "wqn", "lno", "gate",
                     "hsel", "ctxraw", "kv1k", "kv1v", "q1", "wo1"):
            load_sem(name)
        ld_moe = [sem("ld_moe0"), sem("ld_moe1")]
        s_out = sem("s_out")
        dv = sem("dve_chain")
        pl = sem("pool_chain")
        ac = sem("act_chain")
        s_norm1, s_cnorm1 = sem("latents_normed"), sem("ctx_normed")
        s_trn1 = sem("feat1_in_psum")
        s_ff1 = sem("feat1_f32")
        s_fhi1 = sem("feat1_hi")
        s_flo1 = sem("feat1_lo")
        s_w0hi, s_w0 = sem("w0_hi"), sem("w0_split")
        s_nmr = sem("ctx_mean_rstd")
        s_qks = sem("qk_scale")
        s_pq, s_pk, s_pv = sem("proj_q"), sem("proj_k"), sem("proj_v")
        s_qev, s_kev = sem("q_evacuated"), sem("k_evacuated")
        s_sqq, s_sqk = sem("q_squared"), sem("k_squared")
        s_n2q, s_n2k = sem("q_norms_psum"), sem("k_norms_psum")
        s_va, s_vd = sem("v_evac_act"), sem("v_evac_dve")
        s_rn = sem("head_rnorm")
        s_rkp, s_rkt, s_rkhi = sem("rk_rows_psum"), sem("rk_rows_split"), sem("rk_rows_hi")
        s_rkb, s_kfin = sem("rk_bcast_psum"), sem("k_final")
        s_mask, s_rone, s_padz = sem("mask_bias"), sem("ones_row"), sem("pad_zeroed")
        s_hsel = sem("hsel_r")
        s_st0 = sem("qk_staged0")
        s_s0, s_nb0, s_ex0 = sem("scores0"), sem("bias0"), sem("probs0")
        s_mx0 = sem("max0")
        s_pt0, s_pta0, s_ptd0 = sem("pt0_psum"), sem("pt0_sb_act"), sem("pt0_sb_dve")
        s_pv0, s_rs0, s_on0 = sem("pv0"), sem("rsum0"), sem("o0_scaled")
        s_ot0, s_ots0, s_y0, s_ys0 = sem("ot0_psum"), sem("ot0_sb"), sem("y0_psum"), sem("y0_sb")
        s_xb = sem("x_plus_bias")
        s_cs = sem("ctxraw_split")
        s_kv1w = sem("kv1_weights_split")
        s_k1, s_k1e, s_v1, s_v1e = sem("k1_psum"), sem("k1_sb"), sem("v1_psum"), sem("v1_sb")
        s_xn, s_xt, s_xhi, s_xlo = sem("x_normed"), sem("xt_psum"), sem("xt_hi"), sem("xt_lo")
        s_gw, s_lg, s_rex, s_rin = sem("gate_split"), sem("logits"), sem("route_exp"), sem("route_in")
        s_wte = sem("token_weights")
        s_msp = [sem("moe_split0"), sem("moe_split1")]
        s_g, s_u, s_sil, s_h = sem("moe_g"), sem("moe_u"), sem("moe_silu"), sem("moe_h")
        s_hhi, s_hlo, s_yy = sem("moe_h_hi"), sem("moe_h_lo"), sem("moe_y_step")
        s_wst, s_wb, s_wbs = sem("wte_staged"), sem("wte_bcast_psum"), sem("wte_bcast_sb")
        s_yt, s_ya = sem("y_weighted"), sem("y_added")
        s_msub = sem("moe_split_hi")
        s_yT = sem("moe_out_tok")
        s_wq, s_wqt, s_wqhi, s_wqf, s_wqlo = (sem("wq_dequant"), sem("wqT_psum"), sem("wqT_hi"), sem("wqT_f32"),
                                              sem("wqT_lo"))
        s_q1w = sem("q1w_split")
        s_q1, s_q1a, s_q1d = sem("q1_psum"), sem("q1_sb_act"), sem("q1_sb_dve")
        s_st1, s_s1, s_mx1, s_sub1 = sem("qk_staged1"), sem("scores1"), sem("max1"), sem("shifted1")
        s_ex1, s_rs1 = sem("probs1"), sem("rsum1")
        s_sum1 = sem("sum1")
        s_pt1, s_pta1, s_ptd1 = sem("pt1_psum"), sem("pt1_sb_act"), sem("pt1_sb_dve")
        s_pv1, s_on1, s_ot1, s_ota1, s_otd1 = (sem("pv1"), sem("o1_scaled"), sem("ot1_psum"), sem("ot1_sb_act"),
                                               sem("ot1_sb_dve"))
        s_y1, s_x3 = sem("y1_psum"), sem("x3")
        s_am, s_gmb = sem("absmax_col"), sem("absmax_bcast")
        s_x4, s_xqt, s_xsc = sem("x4_normed"), sem("x4T_psum"), sem("x4_scale")
        s_xqm, s_xqhi, s_xqlo = sem("x_ints_magic"), sem("x_ints_hi"), sem("x_ints_lo")
        s_ug, s_uge = sem("gate_up_psum"), sem("gate_up_sb")
        s_magic = sem("magic_cols")
        s_gint, s_sig, s_sgm = sem("gate_ints"), sem("gate_sigmoid"), sem("sigmoid_magic")
        s_usc, s_upm, s_up = sem("up_scale"), sem("up_ints_magic"), sem("up_ints")
        s_g2s, s_g2m = sem("g2_scale"), sem("g2_ints_magic")
        s_oint = sem("o_ints")
        s_dn, s_res = sem("down_psum"), sem("result")

        QKSEQ = []
        for c in range(C0):
            QKSEQ += [("q", c, 0), ("k", c, 0), ("q", c, 1), ("k", c, 1), ("k", c, 2), ("k", c, 3)]
        QSEQ = [g for g in QKSEQ if g[0] == "q"]
        KSEQ = [g for g in QKSEQ if g[0] == "k"]
        V_AMONG = 9
        ORDER = []
        for i, group in enumerate(QKSEQ):
            ORDER.append(group)
            if i >= 6 and i % 2 == 0:
                ORDER.append(("v", (i - 6) // 2, None))
        KFIN = [(c, part) for parts in ((0, 2), (1, 3)) for part in parts for c in range(C0)]
        KFIN_AHEAD = 12

        def v_on_act(t):
            return t >= V_AMONG or t % 2 == 0

        def v_out(t):
            return (s_va if v_on_act(t) else s_vd), sum(v_on_act(u) == v_on_act(t) for u in range(t + 1))

        def v_bank(t):
            return (2, 3, 7)[t % 3]

        def row_bank(part):
            return (0, 1, 4, 5)[part]

        XT_BANK = (4, 2)

        def kfin_bank(i):
            return (6, 7, 4, 5)[i % 4]

        def cols(part):
            return (part * HALF, HALF) if part < 2 else (TOK + (part - 2) * CHALF, CHALF)

        def kdst(c, part):
            if part < 2:
                return qk[:, C0 + c, part * HALF:(part + 1) * HALF]
            return kc[:, c, (part - 2) * CHALF:(part - 1) * CHALF]

        def tile_cols(t):
            return (t * P, P) if t < NB else (TOK + (t - NB) * CR, CR)

        block = ctx.enter_context(nc.Block())

        @block.sync
        def _(sp):
            def load(dst, src, name):
                sp.dma_start(dst, src).then_inc(loads[name], 16)

            load(x[:], a["x"].rearrange("b t d -> t b d"), "x")
            load(cn[0:CR], a["ctx"].rearrange("b t d -> t b d"), "ctx")
            load(wraw[0][:, 0:512], a["Wq"], "w0")
            load(wraw[0][:, 512:1536], a["Wkv"], "w0kv")
            load(wraw[1][:, 0:1024], a["W1k"], "kv1k")
            load(lno[:], a["lno"], "lno")
            sp.wait_ge(s_w0, 2)
            load(wraw[0][:, 0:1024], a["W1v"], "kv1v")
            sp.wait_ge(s_flo1, 4)
            load(ktf[:, 0:CTX], a["ctxT"], "ctxraw")
            sp.wait_ge(s_n2q, len(QSEQ))
            sp.wait_ge(s_n2k, len(KSEQ))
            load(wo0, a["Wo"].rearrange("(c p) d -> p c d", p=P), "wo0")
            load(wo1, a["W1o"].rearrange("(c p) d -> p c d", p=P), "wo1")
            sp.wait_ge(s_kv1w, 4)
            for e in range(2):
                sp.dma_start(wraw[e][:], a["moe"][e]).then_inc(ld_moe[e], 16)
            sp.wait_ge(s_st0, 8 * NB)
            load(wqn[:, 0:CQ], a["wup"].rearrange("(c p) d -> p c d", p=P), "wqn")
            load(wqn[:, CQ:2 * CQ], a["wgate"].rearrange("(c p) d -> p c d", p=P), "wqn")
            load(wqn[:, 2 * CQ:3 * CQ], a["wdown"].rearrange("p (c k) -> p c k", c=CQ), "wqn")
            with sp.Fori(0, NE // 2 - 1) as i:
                for par in range(2):
                    sp.wait_ge(s_msp[par], i * MP + MP)
                    sp.dma_start(wraw[par][:].unsqueeze(1), a["moe"].rearrange("e p n -> p e n")
                                 [:, bass.ds(i * 2 + (2 + par), 1), :]).then_inc(ld_moe[par], 16)
            sp.wait_ge(s_msp[0], NE // 2 * MP)
            load(wraw[0][:, 0:1024], a["W1q"], "q1")
            sp.wait_ge(s_res, 2)
            sp.dma_start(out.rearrange("b t d -> t b d"), xn[:]).then_inc(s_out, 16)
            sp.wait_ge(s_out, 16)

        @block.gpsimd
        def _(pool):
            g = nc.gpsimd
            n = [0]

            def link(ins):
                n[0] += 1
                ins.then_inc(pl, 1)
                pool.wait_ge(pl, n[0])

            g.memset(rowone[:], 0.0).then_inc(pl, 1)
            g.memset(maskb[:], 0.0).then_inc(pl, 1)
            n[0] = 2
            pool.wait_ge(pl, 2)
            g.memset(rowone[0:1, :], 1.0).then_inc(s_rone, 1)
            g.memset(pr[:], 0.0).then_inc(s_padz, 1)
            g.memset(magic[:, 0:1], MAGIC).then_inc(s_magic, 1)
            g.memset(magic[:, 1:2], -MAGIC).then_inc(s_magic, 1)
            g.memset(magic[:, 2:3], 0.0).then_inc(s_magic, 1)
            pool.wait_ge(loads["mask"], 16)
            g.tensor_scalar(maskb[0:1, :], mask8, -1.0, NEG, ALU.add, ALU.mult).then_inc(s_mask, 1)

            def split(dst, lo_cols, raw, s):
                k, w = lo_cols
                link(g.tensor_copy(dst[:, 0, k:k + w], raw))
                g.tensor_tensor(dst[:, 1, k:k + w], raw, dst[:, 0, k:k + w].bitcast(F32), ALU.subtract).then_inc(s, 1)

            for i, k in enumerate((slice(0, 512), slice(512, 1536))):
                pool.wait_ge(s_w0hi, i + 1)
                g.tensor_tensor(wsp[0][:, 1, k], wraw[0][:, k], wsp[0][:, 0, k].bitcast(F32),
                                ALU.subtract).then_inc(s_w0, 1)
            pool.wait_ge(loads["gate"], 16)
            split(gatesp, (0, NE), gatew[:], s_gw)
            pool.wait_ge(loads["kv1k"], 16)
            split(kv1w, (0, 512), wraw[1][:, 0:512], s_kv1w)
            split(kv1w, (512, 512), wraw[1][:, 512:1024], s_kv1w)
            pool.wait_ge(loads["kv1v"], 16)
            split(kv1w, (1024, 512), wraw[0][:, 0:512], s_kv1w)
            split(kv1w, (1536, 512), wraw[0][:, 512:1024], s_kv1w)

            pool.wait_ge(loads["lno"], 16)
            pool.wait_ge(s_norm1, 2)
            g.tensor_tensor(x[:], x[:], lno[:, 1:2, :].to_broadcast([P, NB, D]), ALU.add).then_inc(s_xb, 1)

            def stage0(b, hf, first=False):
                c = slice(2 * hf, 2 * hf + 2)
                ck = slice(C0 + 2 * hf, C0 + 2 * hf + 2)
                if not first:
                    pool.wait_ge(s_s0, b * 2 + (hf - 1))
                g.tensor_copy(qst[:, c, :], qk[:, c, bass.ds(b * P, P)]).then_inc(s_st0, 1)
                g.tensor_copy(kstv0[:, c, 0:P], qk[:, ck, bass.ds(b * P, P)]).then_inc(s_st0, 1)
                g.tensor_copy(kstv0[:, c, P:KEYS0], kc[:, c, bass.ds(b * CR, CR)]).then_inc(s_st0, 1)
                if not first:
                    pool.wait_ge(s_ex0, b * 2 + (hf - 1))
                pool.wait_ge(s_rn, 1)
                g.tensor_copy(rqst[:, 4 * hf:4 * hf + 4], rn[:, bass.ds(b * H0 + 4 * hf, 4)]).then_inc(s_st0, 1)

            pool.wait_ge(s_qev, len(QSEQ))
            pool.wait_ge(s_kfin, len(KFIN) // 2)
            stage0(0, 0, first=True)
            stage0(0, 1, first=True)
            pool.wait_ge(s_kfin, len(KFIN))
            with pool.Fori(1, NB) as b:
                stage0(b, 0)
                stage0(b, 1)

            pool.wait_ge(loads["ctxraw"], 16)
            pool.wait_ge(s_pk, len(KSEQ))
            pool.wait_ge(s_pv, 16)
            pool.wait_ge(s_rkb, len(KSEQ))
            split(feat, (TOK, CTX), ktf[:, 0:CTX], s_cs)

            for e in range(2):
                pool.wait_ge(ld_moe[e], 16)
                for j in range(MP):
                    split(wsp[e], (j * FF, FF), wraw[e][:, j * FF:(j + 1) * FF], s_msp[e])
            pool.wait_ge(s_ys0, NB)

            def add_expert(e):
                for th in range(2):
                    pool.wait_ge(s_yt, e * 2 + (th + 1))
                    g.tensor_tensor(yacc[:, th * HALF:(th + 1) * HALF], yacc[:, th * HALF:(th + 1) * HALF],
                                    ytmp[:, th, :], ALU.add).then_inc(s_ya, 1)

            for th in range(2):
                g.memset(yacc[:, th * HALF:(th + 1) * HALF], 0.0).then_inc(s_ya, 1)
            with pool.Fori(0, NE // 2 - 1) as i:
                for par in range(2):
                    for j in range(MP):
                        k = slice(j * FF, (j + 1) * FF)
                        pool.wait_ge(s_msub, i * (2 * MP) + (par * MP + j + 1))
                        g.tensor_tensor(wsp[par][:, 1, k], wraw[par][:, k], wsp[par][:, 0, k].bitcast(F32),
                                        ALU.subtract).then_inc(s_msp[par], 1)
                    e = i * 2 + par
                    pool.wait_ge(s_ya, e * 2 + 2)
                    add_expert(e)
            pool.wait_ge(loads["q1"], 16)
            pool.wait_ge(s_yy, 8 * (NE - 1))
            split(wsp[0], (0, 1024), wraw[0][:, 0:1024], s_q1w)
            pool.wait_ge(s_ya, (NE - 2) * 2 + 2)
            add_expert(NE - 2)

            pool.wait_ge(s_wqf, 3)
            pool.wait_ge(s_wqhi, 3)
            g.tensor_tensor(wsp[1][:, 1, 0:3 * CQ * D], wraw[1][:, 0:3 * CQ * D],
                            wsp[1][:, 0, 0:3 * CQ * D].bitcast(F32), ALU.subtract).then_inc(s_wqlo, 1)

            def stage1(b, hf, first=False):
                c = slice(4 * hf, 4 * hf + 4)
                if not (isinstance(b, int) and b == 0 and hf == 0):
                    pool.wait_ge(s_st1, b * 6 + 3 * hf)
                if not first:
                    pool.wait_ge(s_s1, b * 2 + (hf - 1))
                pool.wait_ge(s_k1e, 2 * C1)
                g.tensor_copy(qst[:, c, :], qk[:, c, bass.ds(b * P, P)]).then_inc(s_st1, 1)
                for j in range(2):
                    pool.wait_ge(s_st1, b * 6 + (3 * hf + j + 1))
                    pool.wait_ge(s_k1e, 2 * C1)
                    g.tensor_copy(kstv1[DH * j:DH * (j + 1), c, CR * j:CR * (j + 1)],
                                  kt1[DH * j:DH * (j + 1), c, bass.ds(b * CR, CR)]).then_inc(s_st1, 1)

            pool.wait_ge(s_q1w, 1)
            link(g.memset(wraw[0][:, 0:C1 * 2 * CR], 0.0))
            pool.wait_ge(s_q1a, C1 // 2)
            pool.wait_ge(s_q1d, C1 // 2)
            stage1(0, 0, first=True)
            stage1(0, 1, first=True)
            pool.wait_ge(s_q1a, C1)
            pool.wait_ge(s_q1d, C1)
            with pool.Fori(1, NB) as b:
                stage1(b, 0)
                stage1(b, 1)

        @block.scalar
        def _(act):
            s = nc.scalar

            def load(dst, src, name):
                act.dma_start(dst, src).then_inc(loads[name], 16)

            load(ident[:], a["ident"], "ident")
            load(vec[:], a["vec"], "vec")
            load(bones[:], a["bones"], "small")
            load(mask8, a["mask"], "mask")
            load(gatew[:], a["gateT"], "gate")
            load(hsel, a["hsel"], "hsel")
            for name, k in (("w0", slice(0, 512)), ("w0kv", slice(512, 1536))):
                act.wait_ge(loads[name], 16)
                s.activation(wsp[0][:, 0, k], wraw[0][:, k], ACT.Copy).then_inc(s_w0hi, 1)
            act.wait_ge(loads["hsel"], 16)
            s.activation(hselr, hsel, ACT.Copy).then_inc(s_hsel, 1)
            act.wait_ge(s_nmr, 1)
            for t in range(NB):
                ins = s.activation(cn[0:CR, t, :], cn[0:CR, t, :], ACT.Identity, bias=nmr[0:CR, t:t + 1],
                                   scale=rstd[0:CR, NB + t:NB + t + 1])
                if t % 4 == 3:
                    ins.then_inc(s_cnorm1, 1)
            for i in range(4):
                k, w = cols(i)
                act.wait_ge(s_ff1, i + 1)
                s.activation(feat[:, 0, k:k + w], featf[:, k:k + w], ACT.Copy).then_inc(s_fhi1, 1)
            nq = nk = 0
            act.wait_ge(s_qks, 1)

            def v_evac(t):
                r = tile_cols(t)[1]
                act.wait_ge(s_pv, t + 1)
                s.activation(vv[0:r, t, :], ps[0:r, v_bank(t), :], ACT.Copy).then_inc(s_va, 1)

            for kind, c, part in ORDER:
                if kind == "v":
                    if v_on_act(c):
                        v_evac(c)
                elif kind == "q":
                    act.wait_ge(s_pq, nq + 1)
                    if nq >= 2:
                        act.wait_ge(s_n2q, nq - 1)
                    bank = ps[:, 4 + nq % 2, :]
                    s.activation(sq[:, nq % 2, :], bank, ACT.Square).then_inc(s_sqq, 1)
                    s.activation(qk[:, c, part * HALF:(part + 1) * HALF], bank, ACT.Identity,
                                 scale=qks[:]).then_inc(s_qev, 1)
                    nq += 1
                else:
                    w = cols(part)[1]
                    act.wait_ge(s_kev, nk + 1)
                    if nk >= 2:
                        act.wait_ge(s_n2k, nk - 1)
                    s.activation(sq[:, 2 + nk % 2, 0:w], kdst(c, part), ACT.Square).then_inc(s_sqk, 1)
                    nk += 1
            for t in range(V_AMONG, 16):
                v_evac(t)
            for i in range(4):
                k, w = cols(i)
                act.wait_ge(s_rkp, i + 1)
                s.activation(rkhi[:, k:k + w], ps[0:H0, row_bank(i), 0:w], ACT.Copy).then_inc(s_rkhi, 1)

            def exps0(b, hf):
                act.wait_ge(s_nb0, b * 2 + (hf + 1))
                for h in range(4 * hf, 4 * hf + 4):
                    j, i = h % 2, (h // 2) % 2
                    ins = s.activation(prv0[:, h, 0:KEYS0], ps[:, 2 * hf + j, i * KEYS0:(i + 1) * KEYS0], ACT.Exp,
                                       bias=nbias[:, h:h + 1], scale=rqst[:, h:h + 1], accum_out=sums[:, h:h + 1])
                ins.then_inc(s_ex0, 1)

            def ot_evac0(b):
                act.wait_ge(s_ot0, b + 1)
                s.activation(ot[:, 0:C0, :], ps[:, 7, :], ACT.Copy).then_inc(s_ots0, 1)

            def body0(b, first=False, last=False):
                if not last:
                    act.wait_ge(s_pt0, b * 4 + 2)
                    act.wait_ge(s_rs0, b * 2 + 1)
                    exps0(b + 1, 0)
                if not first:
                    ot_evac0(b - 1)
                if not last:
                    act.wait_ge(s_pt0, b * 4 + 4)
                    act.wait_ge(s_rs0, b * 2 + 2)
                    exps0(b + 1, 1)

            act.wait_ge(s_padz, 1)
            exps0(0, 0)
            exps0(0, 1)
            body0(0, first=True)
            with act.Fori(1, NB - 1) as b:
                body0(b)
            body0(NB - 1, last=True)

            def k1_evac(i):
                c, half = i // 2, i % 2
                act.wait_ge(s_k1, i + 1)
                s.activation(kt1[:, c, half * CHALF:(half + 1) * CHALF], ps[:, i % 4, 0:CHALF],
                             ACT.Copy).then_inc(s_k1e, 1)

            def v1_evac(i):
                act.wait_ge(s_v1, i + 1)
                s.activation(vv[0:CR, i, :], ps[0:CR, i % 4, :], ACT.Copy).then_inc(s_v1e, 1)

            act.wait_ge(s_cs, 1)
            for i in range(2 * C1):
                k1_evac(i)
                if i == 1:
                    ot_evac0(NB - 1)
            for i in range(2 * NB):
                v1_evac(i)

            def feat_hi(n0):
                for i in range(2):
                    act.wait_ge(s_xt, n0 + i + 1)
                    s.activation(feat[:, 0, i * HALF:(i + 1) * HALF], ps[:, XT_BANK[n0 // 2] + i, :],
                                 ACT.Copy).then_inc(s_xhi, 1)

            act.wait_ge(s_magic, 3)
            s.activation(magic[:, 3:4], magic[:, 2:3], ACT.Silu).then_inc(ac, 1)
            feat_hi(0)

            def token_weights(e, th):
                act.wait_ge(s_wb, e * 2 + (th + 1))
                if not (isinstance(e, int) and e == 0):
                    act.wait_ge(s_yt, e * 2)
                s.activation(wteb[:, th * HALF:(th + 1) * HALF], ps[:, 6 + th, :], ACT.Copy).then_inc(s_wbs, 1)

            def silu_step(e, i, first=False):
                act.wait_ge(s_g, e * 8 + (i + 1))
                if not first:
                    act.wait_ge(s_h, e * 8 + (i - 1))
                s.activation(silu[:, i % 2, :], ps[:, i % 2, :], ACT.Silu).then_inc(s_sil, 1)

            def moe(e, first=False, last=False):
                for i in range(8):
                    slot = i % 2
                    if not (last and i == 7):
                        silu_step(e, i + 1, first and i == 0)
                    act.wait_ge(s_h, e * 8 + (i + 1))
                    if not (first and i < 2):
                        act.wait_ge(s_yy, e * 8 + (i - 1))
                    s.activation(hidsp[:, 0, slot, :], hid[:, slot, :], ACT.Copy).then_inc(s_hhi, 1)
                    if i in (5, 6) and not first:
                        token_weights(e, i - 5)
                    if i == 2 and first:
                        for k in range(2):
                            act.wait_ge(s_rin, k + 1)
                            s.activation(rt[:, 6 + k, :], rt[:, 6 + k, :], ACT.Exp).then_inc(s_rex, 1)
                if first:
                    token_weights(e, 0)
                    token_weights(e, 1)

            silu_step(0, 0, first=True)
            moe(0, first=True)
            with act.Fori(1, NE - 1) as e:
                moe(e)
            moe(NE - 1, last=True)

            for i in range(3):
                act.wait_ge(s_wqt, i + 1)
                s.activation(wsp[1][:, 0, i * FFQ:(i + 1) * FFQ], ps[:, 4 + i, 0:FFQ], ACT.Copy).then_inc(s_wqhi, 1)
                s.activation(wraw[1][:, i * FFQ:(i + 1) * FFQ], ps[:, 4 + i, 0:FFQ], ACT.Copy).then_inc(s_wqf, 1)
            act.wait_ge(ac, 1)
            s.activation(magic[:, 3:4], magic[:, 2:3], ACT.Exp).then_inc(ac, 1)
            feat_hi(2)
            for i in range(0, 16, 2):
                c, half = i % C1, i // C1
                act.wait_ge(s_q1, i + 1)
                s.activation(qk[:, c, half * HALF:(half + 1) * HALF], ps[:, 4 + (i // 2) % 2, :], ACT.Copy,
                             scale=DH ** -0.5).then_inc(s_q1a, 1)

            def exps1(b, hf):
                act.wait_ge(s_sub1, b * 2 + (hf + 1))
                v = prv1[:, 8 * hf:8 * hf + 8, 0:CR]
                s.activation(v, v, ACT.Exp).then_inc(s_ex1, 1)

            def pt_evac1(b, g):
                act.wait_ge(s_pt1, b * 4 + (g + 1))
                if not (isinstance(b, int) and b == 0 and g < 2):
                    act.wait_ge(s_pv1, b * 4 + (g - 1))
                s.activation(pt[0:CR, g % 2, :], ps[0:CR, 4 + g % 2, :], ACT.Copy).then_inc(s_pta1, 1)

            def ot_evac1(b, k):
                act.wait_ge(s_ot1, b * 2 + (k + 1))
                s.activation(ot[:, 4 * k:4 * k + 4, :], ps[:, 4 + k, :], ACT.Copy).then_inc(s_ota1, 1)

            def body1(b, first=False, last=False):
                pt_evac1(b, 0)
                pt_evac1(b, 1)
                if not first:
                    ot_evac1(b - 1, 0)
                if not last:
                    exps1(b + 1, 0)
                if not first:
                    ot_evac1(b - 1, 1)
                pt_evac1(b, 2)
                pt_evac1(b, 3)
                if not last:
                    exps1(b + 1, 1)

            exps1(0, 0)
            exps1(0, 1)
            body1(0, first=True)
            with act.Fori(1, NB - 1) as b:
                body1(b)
            body1(NB - 1, last=True)
            ot_evac1(NB - 1, 0)
            ot_evac1(NB - 1, 1)

            act.wait_ge(s_xsc, 1)
            for i in range(2):
                act.wait_ge(s_xqt, i + 1)
                t = prb[:, i * HALF:(i + 1) * HALF]
                s.activation(t, ps[:, i, :], ACT.Identity, bias=magic[:, 0:1], scale=qs[:, IX:IX + 1])\
                    .then_inc(s_xqm, 1)
                act.wait_ge(s_xqm, i + 1)
                s.activation(feat[:, 0, i * HALF:(i + 1) * HALF], t, ACT.Identity,
                             bias=magic[:, 1:2]).then_inc(s_xqhi, 1)
            act.wait_ge(ac, 2)
            s.activation(magic[:, 3:4], magic[:, 2:3], ACT.Sigmoid)
            for i in range(4 * CQ):
                dst = gab if i < 2 * CQ else upb
                k = i % (2 * CQ)
                act.wait_ge(s_ug, i + 1)
                s.activation(dst[:, k * HALF:(k + 1) * HALF], ps[:, 2 + i % 4, :], ACT.Copy).then_inc(s_uge, 1)

            def chunk(buf, c):
                return buf[:, c * TOK:(c + 1) * TOK]

            for c in range(CQ):
                act.wait_ge(s_gint, c + 1)
                s.activation(chunk(sgb, c), chunk(gab, c), ACT.Sigmoid, scale=qs[:, SG:SG + 1]).then_inc(s_sig, 1)
                act.wait_ge(s_sig, c + 1)
                s.activation(chunk(sgb, c), chunk(sgb, c), ACT.Identity, bias=magic[:, 0:1],
                             scale=65536.0).then_inc(s_sgm, 1)
            act.wait_ge(s_usc, 1)
            for c in range(CQ):
                s.activation(chunk(upb, c), chunk(upb, c), ACT.Identity, bias=magic[:, 0:1],
                             scale=qs[:, IU:IU + 1]).then_inc(s_upm, 1)
            act.wait_ge(s_g2s, 1)
            for c in range(CQ):
                s.activation(chunk(gab, c), chunk(gab, c), ACT.Identity, bias=magic[:, 0:1],
                             scale=qs[:, IG2:IG2 + 1]).then_inc(s_g2m, 1)
        @block.vector
        def _(dve):
            v = nc.vector
            n = [0]

            def link(*steps):
                n[0] += 1
                steps[-1].then_inc(dv, 1)
                dve.wait_ge(dv, n[0])

            def rsqrt(y, xx, t):
                link(v.tensor_scalar(t.bitcast(I32), xx.bitcast(I32), 1, None, ALU.logical_shift_right))
                link(v.tensor_scalar(y.bitcast(I32), t.bitcast(I32), -1.0, RSQRT_SEED, ALU.mult, ALU.add))
                for step in range(3):
                    link(v.tensor_tensor(t, y, y, ALU.mult))
                    link(v.scalar_tensor_tensor(out=t, in0=xx, scalar=-0.5, in1=t, op0=ALU.mult, op1=ALU.mult))
                    last = v.scalar_tensor_tensor(out=y, in0=t, scalar=1.5, in1=y, op0=ALU.add, op1=ALU.mult)
                    if step < 2:
                        link(last)
                return last

            def layer_norm(sets, done, eps=LN_EPS):
                for dst, src, rows, k in sets:
                    for t in range(NB):
                        i1 = v.bn_stats(st[0:rows, k + t, :], src[0:rows, t, :])
                link(i1)
                for dst, src, rows, k in sets:
                    for t in range(NB):
                        i1 = v.bn_aggr(mv[0:rows, k + t, :], st[0:rows, k + t, :])
                link(i1)
                for dst, src, rows, k in sets:
                    i1 = v.tensor_scalar(var[0:rows, k:k + NB], mv[0:rows, k:k + NB, 1], eps, None, ALU.add)
                link(i1)
                lo, hi = min(k for *_, k in sets), max(k for *_, k in sets) + NB
                link(rsqrt(rstd[:, lo:hi], var[:, lo:hi], nt[:, lo:hi]))
                for dst, src, rows, k in sets:
                    for t in range(NB):
                        i1 = v.tensor_scalar(dst[0:rows, t, :], src[0:rows, t, :], mv[0:rows, k + t, 0:1],
                                             rstd[0:rows, k + t:k + t + 1], ALU.subtract, ALU.mult)
                        if t % 4 == 3:
                            i1.then_inc(done, 1)

            v.memset(n2, 1.0)
            link(v.memset(var[:], 1.0))
            dve.wait_ge(loads["x"], 16)
            for t in range(NB):
                v.bn_stats(st[:, t, :], x[:, t, :])
            dve.wait_ge(loads["ctx"], 16)
            for t in range(NB):
                i1 = v.bn_stats(st[0:CR, NB + t, :], cn[0:CR, t, :])
            link(i1)
            for t in range(NB):
                v.bn_aggr(mv[:, t, :], st[:, t, :])
                i1 = v.bn_aggr(mv[0:CR, NB + t, :], st[0:CR, NB + t, :])
            link(i1)
            v.tensor_scalar(var[:, 0:NB], mv[:, 0:NB, 1], 1.0 + LN_EPS, LN_EPS * LN_EPS, ALU.mult, ALU.add)
            link(v.tensor_scalar(var[0:CR, NB:2 * NB], mv[0:CR, NB:2 * NB, 1], LN_EPS, None, ALU.add))
            link(rsqrt(rstd[:], var[:], nt[:, 0:2 * NB]))
            v.scalar_tensor_tensor(out=nmr[0:CR, :], in0=mv[0:CR, NB:2 * NB, 0], scalar=-1.0,
                                   in1=rstd[0:CR, NB:2 * NB], op0=ALU.mult, op1=ALU.mult).then_inc(s_nmr, 1)
            for t in range(NB):
                i1 = v.tensor_scalar(xn[:, t, :], x[:, t, :], mv[:, t, 0:1], rstd[:, t:t + 1], ALU.subtract, ALU.mult)
                if t % 4 == 3:
                    i1.then_inc(s_norm1, 1)
            dve.wait_ge(loads["vec"], 16)
            v.scalar_tensor_tensor(out=qks[:], in0=vec[:, 4:5], scalar=8.0, in1=vec[:, 5:6], op0=ALU.mult,
                                   op1=ALU.mult).then_inc(s_qks, 1)

            def feat_affine(i):
                k, w = cols(i)
                wb = 2 if i < 2 else 0
                dve.wait_ge(s_trn1, i + 1)
                v.tensor_scalar(featf[:, k:k + w], ps[:, i, 0:w], vec[:, wb:wb + 1], vec[:, wb + 1:wb + 2], ALU.mult,
                                ALU.add).then_inc(s_ff1, 1)

            def feat_lo(i):
                k, w = cols(i)
                dve.wait_ge(s_ff1, i + 1)
                dve.wait_ge(s_fhi1, i + 1)
                v.tensor_tensor(feat[:, 1, k:k + w], featf[:, k:k + w], feat[:, 0, k:k + w].bitcast(F32),
                                ALU.subtract).then_inc(s_flo1, 1)

            feat_affine(0)
            feat_affine(1)
            feat_lo(0)
            feat_affine(2)
            feat_lo(1)
            feat_affine(3)
            feat_lo(2)
            feat_lo(3)
            i = 0
            for kind, c, part in ORDER:
                if kind == "k":
                    dve.wait_ge(s_pk, i + 1)
                    v.tensor_copy(kdst(c, part), ps[:, i % 2, 0:cols(part)[1]]).then_inc(s_kev, 1)
                    i += 1
                if kind == "v" and not v_on_act(c):
                    r = tile_cols(c)[1]
                    dve.wait_ge(s_pv, c + 1)
                    v.tensor_copy(vv[0:r, c, :], ps[0:r, v_bank(c), :]).then_inc(s_vd, 1)
            dve.wait_ge(s_n2q, len(QSEQ))
            dve.wait_ge(s_n2k, len(KSEQ))
            v.tensor_scalar(n2[:, 0:128], ps[:, 6, 0:128], L2_EPS2, None, ALU.max)
            link(v.tensor_scalar(n2[0:CR, 128:192], ps[0:CR, 6, 128:192], L2_EPS2, None, ALU.max))
            rsqrt(rn[:], n2, nt[:]).then_inc(s_rn, 1)
            for i in range(4):
                k, w = cols(i)
                dve.wait_ge(s_rkhi, i + 1)
                v.tensor_tensor(rklo[:, k:k + w], ps[0:H0, row_bank(i), 0:w], rkhi[:, k:k + w].bitcast(F32),
                                ALU.subtract).then_inc(s_rkt, 1)

            def key_over_norm(i):
                c, part = KFIN[i]
                dve.wait_ge(s_rkb, i + 1)
                v.tensor_tensor(kdst(c, part), kdst(c, part), ps[:, kfin_bank(i), 0:cols(part)[1]],
                                ALU.mult).then_inc(s_kfin, 1)

            for i in range(KFIN_AHEAD):
                key_over_norm(i)

            def smax0(b, hf):
                dve.wait_ge(s_s0, b * 2 + (hf + 1))
                dve.wait_ge(s_st0, b * 8 + (4 * hf + 4))
                v.tensor_reduce(mx[:, 4 * hf:4 * hf + 4].rearrange("p (i j) -> p j i", j=2),
                                ps[:, 2 * hf:2 * hf + 2, 0:2 * KEYS0].rearrange("p j (i k) -> p j i k", i=2),
                                AX.X, ALU.max, negate=True).then_inc(s_mx0, 1)
                dve.wait_ge(s_mx0, b * 2 + (hf + 1))
                v.tensor_tensor(nbias[:, 4 * hf:4 * hf + 4], mx[:, 4 * hf:4 * hf + 4], rqst[:, 4 * hf:4 * hf + 4],
                                ALU.mult).then_inc(s_nb0, 1)

            def pt_evac0(b, g):
                dve.wait_ge(s_pt0, b * 4 + (g + 1))
                if not (isinstance(b, int) and b == 0 and g < 2):
                    dve.wait_ge(s_pv0, b * 4 + (g - 1))
                v.tensor_copy(pt[:, g % 2, :], ps[:, 4 + g % 2, :]).then_inc(s_ptd0, 1)

            def rsum0(b, k):
                dve.wait_ge(s_ex0, b * 2 + (k + 1))
                if not (isinstance(b, int) and b == 0):
                    dve.wait_ge(s_on0, b)
                v.reciprocal(rsum[:, 4 * k:4 * k + 4], sums[:, 4 * k:4 * k + 4]).then_inc(s_rs0, 1)

            def scale0(b, first=False):
                dve.wait_ge(s_pv0, b * 4 + 4)
                dve.wait_ge(s_rs0, b * 2 + 2)
                if not first:
                    dve.wait_ge(s_ot0, b)
                v.tensor_tensor(cnf[:, 0:512].rearrange("p (h d) -> p h d", h=H0),
                                ps[:, 6, :].rearrange("p (h d) -> p h d", h=H0),
                                rsum[:, 0:H0].unsqueeze(2).to_broadcast([P, H0, DH]), ALU.mult).then_inc(s_on0, 1)

            def y_evac0(b):
                dve.wait_ge(s_y0, b + 1)
                dve.wait_ge(s_y0, 1)
                v.tensor_copy(xnf[:, bass.ds(b * D, D)], ps[:, 7, 0:D])
                v.bn_stats(st[:, bass.ds(b, 1), :], ps[:, 7, 0:D]).then_inc(s_ys0, 1)

            def body0(b, first=False, last=False):
                rsum0(b, 0)
                pt_evac0(b, 0)
                pt_evac0(b, 1)
                if not last:
                    smax0(b + 1, 0)
                rsum0(b, 1)
                pt_evac0(b, 2)
                pt_evac0(b, 3)
                if not last:
                    smax0(b + 1, 1)
                if not first:
                    y_evac0(b - 1)
                scale0(b, first)

            smax0(0, 0)
            smax0(0, 1)
            for i in range(KFIN_AHEAD, len(KFIN)):
                key_over_norm(i)
            body0(0, first=True)
            with dve.Fori(1, NB - 1) as b:
                body0(b)
            body0(NB - 1, last=True)
            y_evac0(NB - 1)

            dve.wait_ge(s_ys0, NB)
            dve.wait_ge(loads["lno"], 16)
            for t in range(NB):
                i1 = v.bn_aggr(mv[:, t, :], st[:, t, :])
            link(i1)
            for t in range(NB):
                v.scalar_tensor_tensor(out=xn[:, t, :], in0=xn[:, t, :], scalar=mv[:, t, 0:1], in1=lno[:, 0, :],
                                       op0=ALU.subtract, op1=ALU.mult)
            link(v.tensor_scalar(var[:, 0:NB], mv[:, 0:NB, 1], LN_EPS, None, ALU.add))
            link(rsqrt(rstd[:, 0:NB], var[:, 0:NB], nt[:, 0:NB]))
            dve.wait_ge(s_xb, 1)
            for t in range(NB):
                i1 = v.scalar_tensor_tensor(out=x[:, t, :], in0=xn[:, t, :], scalar=rstd[:, t:t + 1], in1=x[:, t, :],
                                            op0=ALU.mult, op1=ALU.add)
            link(i1)
            layer_norm([(xn, x, P, 0)], s_xn)

            def feat_lo_x(n0):
                for i in range(2):
                    dve.wait_ge(s_xhi, n0 + i + 1)
                    v.tensor_tensor(feat[:, 1, i * HALF:(i + 1) * HALF], ps[:, XT_BANK[n0 // 2] + i, :],
                                    feat[:, 0, i * HALF:(i + 1) * HALF].bitcast(F32), ALU.subtract).then_inc(s_xlo, 1)

            feat_lo_x(0)

            def R(i):
                return rt[:, i, :].rearrange("p (b e) -> p b e", e=NE)

            def bc(col):
                return col.unsqueeze(2).to_broadcast([P, NB, NE])

            LOG, EQ1, LOG2, EQ2, T, ABS, E1, E2, RANK, CAND = range(10)
            small = rt[:, 10, :].rearrange("p (k b) -> p k b", b=NB)
            M1, M2, S1, S2, C1_, C2_ = (small[:, i, :] for i in range(6))
            rank_c = rt[:, RANK, :].rearrange("p (b e) -> p b e", e=NE)
            for e in range(NE):
                i1 = v.memset(rank_c[:, :, e], float(NE - e))
            dve.wait_ge(s_lg, 1)
            link(v.tensor_copy(rt[:, LOG, :], ps[:, 6, 0:64]))
            link(v.scalar_tensor_tensor(out=R(ABS), in0=R(LOG), scalar=-1.0, in1=R(LOG), op0=ALU.mult, op1=ALU.max))

            def choose(src, m, cand_col, eq):
                link(v.tensor_reduce(m, R(src), AX.X, ALU.max))
                link(v.tensor_tensor(R(T), R(src), bc(m), ALU.is_equal))
                link(v.tensor_tensor(R(T), R(T), R(RANK), ALU.mult))
                link(v.tensor_reduce(cand_col, R(T), AX.X, ALU.max))
                link(v.tensor_tensor(R(eq), R(T), bc(cand_col), ALU.is_equal))

            def softmax_in(src, m, e):
                v.tensor_tensor(R(e), R(src), bc(m), ALU.subtract).then_inc(s_rin, 1)

            def keep_sum(m, e, ssum, drop):
                link(v.tensor_tensor(R(T), R(ABS), bc(m), ALU.max))
                link(v.tensor_tensor(R(CAND), bc(m), R(LOG), ALU.subtract))
                link(v.scalar_tensor_tensor(out=R(T), in0=R(T), scalar=0.02, in1=R(CAND), op0=ALU.mult,
                                            op1=ALU.is_ge))
                if drop is not None:
                    link(v.scalar_tensor_tensor(out=R(CAND), in0=R(drop), scalar=0.0, in1=R(T), op0=ALU.is_equal,
                                                op1=ALU.mult))
                    keep = CAND
                else:
                    keep = T
                link(v.tensor_tensor(R(CAND), R(keep), R(e), ALU.mult))
                link(v.tensor_reduce(ssum, R(CAND), AX.X, ALU.add))
                link(v.reciprocal(ssum, ssum))

            def route(k):
                if k == 0:
                    choose(LOG, M1, C1_, EQ1)
                if k == 1:
                    softmax_in(LOG, M1, E1)
                    link(v.scalar_tensor_tensor(out=R(LOG2), in0=R(EQ1), scalar=-NEG, in1=R(LOG), op0=ALU.mult,
                                                op1=ALU.add))
                    choose(LOG2, M2, C2_, EQ2)
                    softmax_in(LOG2, M2, E2)
                if k == 3:
                    dve.wait_ge(s_rex, 1)
                    keep_sum(M1, E1, S1, None)
                if k == 4:
                    dve.wait_ge(s_rex, 2)
                    keep_sum(M2, E2, S2, EQ1)
                if k == 5:
                    link(v.tensor_tensor(R(EQ1), R(EQ1), bc(S1), ALU.mult))
                    link(v.tensor_tensor(R(EQ2), R(EQ2), bc(S2), ALU.mult))
                    v.tensor_tensor(wtef.rearrange("p (e b) -> p b e", b=NB), R(EQ1), R(EQ2), ALU.add)\
                        .then_inc(s_wte, 1)
                    dve.wait_ge(s_wte, 1)
                    stage_weights(0, first=True)

            def weigh(e, th, first=False):
                dve.wait_ge(s_yy, e * 8 + (7 + th))
                dve.wait_ge(s_wbs, e * 2 + (th + 1))
                if not first:
                    dve.wait_ge(s_ya, e * 2 + 2)
                v.tensor_tensor(ytmp[:, th, :], ps[:, 4 + th, :], wteb[:, th * HALF:(th + 1) * HALF],
                                ALU.mult).then_inc(s_yt, 1)

            def stage_weights(e, first=False):
                if not first:
                    dve.wait_ge(s_wb, e * 2)
                    dve.wait_ge(s_wte, 1)
                v.tensor_copy(wtes[:], wtef[:, bass.ds(e * NB, NB)]).then_inc(s_wst, 1)

            def product(e, i, first=False):
                dve.wait_ge(s_u, e * 8 + (i + 1))
                dve.wait_ge(s_sil, e * 8 + (i + 1))
                if not first:
                    dve.wait_ge(s_hhi, e * 8 + (i - 1))
                    dve.wait_ge(s_hlo, e * 8 + (i - 1))
                v.tensor_tensor(hid[:, i % 2, :], silu[:, i % 2, :], ps[:, 2 + i % 2, :], ALU.mult).then_inc(s_h, 1)

            wblk = wqn.rearrange("p c (k w) -> p (c k) w", w=QBLK)
            nblk = 3 * CQ * D // QBLK
            wmax, wscale, winv = (wqs[:, i, :] for i in range(3))

            def wbc(col):
                return col.unsqueeze(2).to_broadcast([P, nblk, QBLK])

            def dequant(k):
                if k == 2:
                    dve.wait_ge(loads["wqn"], 48)
                    link(v.tensor_reduce(wmax, wblk, AX.X, ALU.max, apply_absolute_value=True))
                if k == 3:
                    link(v.tensor_scalar(wscale, wmax, 1.0 / 7.0, 1e-12, ALU.mult, ALU.max))
                    link(v.reciprocal(winv, wscale))
                if k == 4:
                    link(v.tensor_tensor(wblk, wblk, wbc(winv), ALU.mult))
                if k == 5:
                    link(v.tensor_scalar(wblk, wblk, MAGIC, MAGIC, ALU.add, ALU.subtract))
                if k == 6:
                    v.tensor_tensor(wblk, wblk, wbc(wscale), ALU.mult).then_inc(s_wq, 1)

            def moe(e, first=False, last=False, loaded=None, par=None):
                for i in range(8):
                    slot = i % 2
                    if not (last and i == 7):
                        product(e, i + 1, first and i == 0)
                    if not first and i < 2:
                        weigh(e - 1, i, first=isinstance(e, int) and e == 1)
                    dve.wait_ge(s_hhi, e * 8 + (i + 1))
                    v.tensor_tensor(hidsp[:, 1, slot, :], hid[:, slot, :], hidsp[:, 0, slot, :].bitcast(F32),
                                    ALU.subtract).then_inc(s_hlo, 1)
                    if last:
                        dequant(i)
                    if first:
                        route(i)
                    elif i == 1:
                        stage_weights(e)
                    if 2 <= i < 2 + MP and loaded is not None:
                        k = slice((i - 2) * FF, (i - 1) * FF)
                        dve.wait_ge(ld_moe[par], loaded)
                        dve.wait_ge(s_yy, e * 8)
                        v.tensor_copy(wsp[par][:, 0, k], wraw[par][:, k]).then_inc(s_msub, 1)

            product(0, 0, first=True)
            moe(0, first=True)
            moe(1, loaded=32, par=0)

            with dve.Fori(1, NE // 2 - 1) as i:
                moe(i * 2, loaded=i * 16 + 16, par=1)
                moe(i * 2 + 1, loaded=i * 16 + 32, par=0)
            moe(NE - 2, loaded=16 * (NE // 2), par=1)
            moe(NE - 1, last=True)
            for th in range(2):
                weigh(NE - 1, th)
                dve.wait_ge(s_yt, 2 * NE - 1 + th)
                v.tensor_tensor(yacc[:, th * HALF:(th + 1) * HALF], yacc[:, th * HALF:(th + 1) * HALF],
                                ytmp[:, th, :], ALU.add).then_inc(s_ya, 1)

            for i in range(2):
                dve.wait_ge(s_yT, i + 1)
                i1 = v.tensor_tensor(xf[:, i * HALF:(i + 1) * HALF], xf[:, i * HALF:(i + 1) * HALF], ps[:, i, :],
                                     ALU.add)
            link(i1)
            layer_norm([(xn, x, P, 0)], s_xn)
            feat_lo_x(2)
            def q1_evac(i):
                c, half = i % C1, i // C1
                dve.wait_ge(s_q1, i + 1)
                v.tensor_scalar(qk[:, c, half * HALF:(half + 1) * HALF], ps[:, 6 + (i // 2) % 2, :], DH ** -0.5, None,
                                ALU.mult).then_inc(s_q1d, 1)

            for i in range(1, 14, 2):
                q1_evac(i)

            def sub1(b, hf):
                def S():
                    return ps[:, 2 * hf:2 * hf + 2, 0:4 * CR].rearrange("p j (i k) -> p j i k", i=4)

                m = mx[:, 8 * hf:8 * hf + 8].rearrange("p (j i) -> p j i", j=2)
                dve.wait_ge(s_s1, b * 2 + (hf + 1))
                v.tensor_reduce(m, S(), AX.X, ALU.max).then_inc(s_mx1, 1)
                dve.wait_ge(s_mx1, b * 2 + (hf + 1))
                v.tensor_tensor(prv1[:, 8 * hf:8 * hf + 8, 0:CR].rearrange("p (j i) k -> p j i k", j=2), S(),
                                m.unsqueeze(3).to_broadcast([P, 2, 4, CR]), ALU.subtract).then_inc(s_sub1, 1)

            def sums1(b, k):
                dve.wait_ge(s_ex1, b * 2 + (k + 1))
                if not (isinstance(b, int) and b == 0):
                    dve.wait_ge(s_on1, b * 2 + (k - 1))
                h = slice(8 * k, 8 * k + 8)
                v.tensor_reduce(sums[:, h], prv1[:, h, 0:CR], AX.X, ALU.add).then_inc(s_sum1, 1)
                dve.wait_ge(s_sum1, b * 2 + (k + 1))
                v.reciprocal(rsum[:, h], sums[:, h]).then_inc(s_rs1, 1)

            def scale1(b, k, first=False):
                dve.wait_ge(s_pv1, b * 4 + (2 * k + 2))
                dve.wait_ge(s_rs1, b * 2 + (k + 1))
                if not first:
                    dve.wait_ge(s_ot1, b * 2 + (k - 1))
                v.tensor_tensor(cnf[:, 512 * k:512 * k + 512].rearrange("p (h d) -> p h d", h=8),
                                ps[:, 6 + k, :].rearrange("p (h d) -> p h d", h=8),
                                rsum[:, 8 * k:8 * k + 8].unsqueeze(2).to_broadcast([P, 8, DH]),
                                ALU.mult).then_inc(s_on1, 1)

            def add_y1(b):
                dve.wait_ge(s_y1, b + 1)
                xb = xf[:, bass.ds(b * D, D)]
                v.tensor_tensor(xb, xb, ps[:, 0, YCOL:YCOL + D], ALU.add).then_inc(s_x3, 1)

            def body1(b, first=False, last=False):
                sums1(b, 0)
                if not last:
                    dve.wait_ge(s_pt1, b * 4 + 2)
                    sub1(b + 1, 0)
                scale1(b, 0, first)
                sums1(b, 1)
                if not last:
                    dve.wait_ge(s_pt1, b * 4 + 4)
                    sub1(b + 1, 1)
                if not first:
                    add_y1(b - 1)
                scale1(b, 1, first)

            sub1(0, 0)
            q1_evac(15)
            sub1(0, 1)
            body1(0, first=True)
            with dve.Fori(1, NB - 1) as b:
                body1(b)
            body1(NB - 1, last=True)
            add_y1(NB - 1)

            dve.wait_ge(s_x3, NB)
            layer_norm([(xn, x, P, 0)], s_x4)
            dve.wait_ge(s_x4, 2)
            gcount = [0]

            def q(i):
                return qs[:, i:i + 1]

            def global_scale(inv, scale, unit=None):
                k = gcount[0]
                gcount[0] += 1
                if unit is not None:
                    link(v.tensor_scalar(q(UX), unit, 1.0 / QMAX, None, ALU.mult))
                dve.wait_ge(s_gmb, k + 1)
                link(v.tensor_reduce(q(0), ps[:, 7, 0:P], AX.X, ALU.max))
                link(v.tensor_scalar(scale, q(0), 1.0 / QMAX if unit is None else q(UX), 1e-12, ALU.mult, ALU.max))
                last = v.reciprocal(inv, scale)
                if unit is not None:
                    link(last)
                    last = v.tensor_tensor(inv, inv, unit, ALU.mult)
                return last

            def chunk(buf, c):
                return buf[:, c * TOK:(c + 1) * TOK]

            v_abs = dict(apply_absolute_value=True)
            v.tensor_reduce(q(0), xnf, AX.X, ALU.max, **v_abs).then_inc(s_am, 1)
            global_scale(q(IX), q(SX)).then_inc(s_xsc, 1)
            dve.wait_ge(s_xsc, 1)
            for i in range(2):
                dve.wait_ge(s_xqhi, i + 1)
                v.scalar_tensor_tensor(out=feat[:, 1, i * HALF:(i + 1) * HALF], in0=prb[:, i * HALF:(i + 1) * HALF],
                                       scalar=MAGIC, in1=feat[:, 0, i * HALF:(i + 1) * HALF].bitcast(F32),
                                       op0=ALU.subtract, op1=ALU.subtract).then_inc(s_xqlo, 1)

            def absmax(i):
                src = gab if i < 2 * CQ else upb
                k = i % (2 * CQ)
                dve.wait_ge(s_uge, i + 1)
                return v.tensor_reduce(rt[:, 0, i:i + 1], src[:, k * HALF:(k + 1) * HALF], AX.X, ALU.max, **v_abs)

            def gate_ints(c):
                link(v.tensor_scalar(chunk(gab, c), chunk(gab, c), q(IG), MAGIC, ALU.mult, ALU.add))
                v.tensor_scalar(chunk(gab, c), chunk(gab, c), MAGIC, None, ALU.subtract).then_inc(s_gint, 1)

            def gated(c):
                w, gi = chunk(sgb, c), chunk(gab, c)
                dve.wait_ge(s_sgm, c + 1)
                link(v.tensor_scalar(w, w, MAGIC + 65535.0, MAGIC, ALU.min, ALU.subtract))
                link(v.tensor_tensor(gi, w, gi, ALU.mult))
                return v.tensor_reduce(rt[:, 1, c:c + 1], gi, AX.X, ALU.max, **v_abs)

            for i in range(2 * CQ):
                i1 = absmax(i)
            link(i1)
            v.tensor_reduce(q(0), rt[:, 0, 0:2 * CQ], AX.X, ALU.max).then_inc(s_am, 1)
            absmax(2 * CQ)
            link(global_scale(q(IG), q(SG), q(SX)))
            gate_ints(0)
            absmax(2 * CQ + 1)
            absmax(2 * CQ + 2)
            gate_ints(1)
            absmax(2 * CQ + 3)
            absmax(2 * CQ + 4)
            gate_ints(2)
            link(absmax(2 * CQ + 5))
            v.tensor_reduce(q(0), rt[:, 0, 2 * CQ:4 * CQ], AX.X, ALU.max).then_inc(s_am, 1)
            gated(0)
            global_scale(q(IU), q(SU), q(SX)).then_inc(s_usc, 1)
            gated(1)
            link(gated(2))
            v.tensor_reduce(q(0), rt[:, 1, 0:CQ], AX.X, ALU.max).then_inc(s_am, 1)
            for c in range(CQ):
                dve.wait_ge(s_upm, c + 1)
                v.tensor_scalar(chunk(upb, c), chunk(upb, c), MAGIC, None, ALU.subtract).then_inc(s_up, 1)
            link(v.tensor_scalar(q(SG), q(SG), 1.0 / 65536.0, None, ALU.mult))
            global_scale(q(IG2), q(SG2), q(SG)).then_inc(s_g2s, 1)
            for c in range(CQ):
                dve.wait_ge(s_g2m, c + 1)
                dve.wait_ge(s_up, c + 1)
                link(v.scalar_tensor_tensor(out=chunk(prb, c), in0=chunk(gab, c), scalar=MAGIC, in1=chunk(upb, c),
                                            op0=ALU.subtract, op1=ALU.mult))
                i1 = v.tensor_reduce(rt[:, 2, c:c + 1], chunk(prb, c), AX.X, ALU.max, **v_abs)
            link(i1)
            v.tensor_reduce(q(0), rt[:, 2, 0:CQ], AX.X, ALU.max).then_inc(s_am, 1)
            dve.wait_ge(s_g2s, 1)
            dve.wait_ge(s_usc, 1)
            link(v.tensor_scalar(q(SG2), q(SG2), q(SU), None, ALU.mult))
            link(global_scale(q(IO), q(SO), q(SG2)))
            for c in range(CQ):
                link(v.tensor_scalar(chunk(prb, c), chunk(prb, c), q(IO), MAGIC, ALU.mult, ALU.add))
                v.tensor_scalar(chunk(prb, c), chunk(prb, c), MAGIC, None, ALU.subtract).then_inc(s_oint, 1)
            for i in range(2):
                dve.wait_ge(s_dn, i + 1)
                v.scalar_tensor_tensor(out=xnf[:, i * HALF:(i + 1) * HALF], in0=ps[:, i, :], scalar=q(SO),
                                       in1=xf[:, i * HALF:(i + 1) * HALF], op0=ALU.mult, op1=ALU.add)\
                    .then_inc(s_res, 1)

        @block.tensor
        def _(pe):
            t_ = nc.tensor

            def mm3(dst, lhs, rhs, start=True, stop=True, **kw):
                t_.matmul(dst, lhs[0], rhs[1], start=start, stop=False, **kw)
                t_.matmul(dst, lhs[1], rhs[0], start=False, stop=False, **kw)
                return t_.matmul(dst, lhs[0], rhs[0], start=False, stop=stop, **kw)

            def two(buf, k, w):
                return buf[:, 0, k:k + w], buf[:, 1, k:k + w]

            pe.wait_ge(loads["ident"], 16)
            for t in range(NB):
                pe.wait_ge(s_norm1, t // 4 + 1)
                ins = t_.transpose(ps[:, t // 4, (t % 4) * P:(t % 4 + 1) * P], xn[:, t, :], ident[:])
                if t % 4 == 3:
                    ins.then_inc(s_trn1, 1)
            for t in range(NB):
                pe.wait_ge(s_cnorm1, t // 4 + 1)
                ins = t_.transpose(ps[:, 2 + t // 4, (t % 4) * CR:(t % 4 + 1) * CR], cn[0:CR, t, :],
                                   ident[0:CR, 0:CR])
                if t % 4 == 3:
                    ins.then_inc(s_trn1, 1)

            pe.wait_ge(loads["small"], 16)
            pe.wait_ge(s_w0, 1)
            pe.wait_ge(s_ff1, 2)
            cnt = {"q": 0, "k": 0}
            ncnt = {"q": 0, "k": 0}

            def proj(kind, c, part):
                i = cnt[kind]
                cnt[kind] += 1
                k, w = cols(part)
                pe.wait_ge(s_flo1, part + 1)
                if kind == "k":
                    pe.wait_ge(s_w0, 2)
                    if i >= 2:
                        pe.wait_ge(s_kev, i - 1)
                elif i >= 2:
                    pe.wait_ge(s_qev, i - 1)
                bank = ps[:, (4 if kind == "q" else 0) + i % 2, 0:w]
                wcol = (0 if kind == "q" else 512) + c * P
                mm3(bank, two(wsp[0], wcol, P), two(feat, k, w)).then_inc(s_pq if kind == "q" else s_pk, 1)

            def norms(kind, c, part):
                i = ncnt[kind]
                ncnt[kind] += 1
                pe.wait_ge(s_sqq if kind == "q" else s_sqk, i + 1)
                slot = (0 if kind == "q" else 2) + i % 2
                rows = P if part < 2 else CR
                base = 0 if kind == "q" else (64 if part < 2 else 128)
                for j in range(4):
                    b = (part % 2) * 4 + j
                    k = base + b * H0 + 2 * c
                    ins = t_.matmul(ps[0:rows, 6, k:k + 2], sq[:, slot, j * rows:(j + 1) * rows], bones[:],
                                    start=True, stop=True)
                ins.then_inc(s_n2q if kind == "q" else s_n2k, 1)

            def value(t):
                k, w = tile_cols(t)
                pe.wait_ge(s_flo1, t // 4 + 1)
                pe.wait_ge(s_ff1, 4)
                if t >= 3:
                    pe.wait_ge(*v_out(t - 3))
                mm3(ps[0:w, v_bank(t), :], two(feat, k, w), two(wsp[0], 1024, 512)).then_inc(s_pv, 1)

            LAG = 3
            i = 0
            for g in ORDER:
                if g[0] == "v":
                    value(g[1])
                    continue
                proj(*g)
                if i >= LAG:
                    norms(*QKSEQ[i - LAG])
                i += 1
            for g in QKSEQ[-LAG:]:
                norms(*g)
            for t in range(V_AMONG, 16):
                value(t)
            pe.wait_ge(s_rn, 1)
            pe.wait_ge(s_qev, len(QSEQ))
            pe.wait_ge(s_kev, len(KSEQ))
            for t in range(16):
                k, w = tile_cols(t)
                part = (t // 4)
                ins = t_.transpose(ps[0:H0, row_bank(part), (t % 4) * w:(t % 4 + 1) * w],
                                   rn[0:w, 64 + t * H0:64 + (t + 1) * H0], ident[0:w, 0:w])
                if t % 4 == 3:
                    ins.then_inc(s_rkp, 1)
            pe.wait_ge(s_hsel, 1)
            pe.wait_ge(*v_out(15))
            pe.wait_ge(s_rkt, 4)

            def key_norms(i):
                c, part = KFIN[i]
                k, w = cols(part)
                if i >= 4:
                    pe.wait_ge(s_kfin, i - 3)
                bank = ps[:, kfin_bank(i), 0:w]
                t_.matmul(bank, hselr[:, c * P:(c + 1) * P], rklo[:, k:k + w], start=True, stop=False)
                t_.matmul(bank, hselr[:, c * P:(c + 1) * P], rkhi[:, k:k + w], start=False, stop=True)\
                    .then_inc(s_rkb, 1)

            for i in range(KFIN_AHEAD):
                key_norms(i)

            def scores0(b, hf):
                pe.wait_ge(s_st0, b * 8 + (4 * hf + 3))
                if not (isinstance(b, int) and b == 0):
                    pe.wait_ge(s_ex0, b * 2 + (hf - 1))
                for i in range(2):
                    for j in range(2):
                        c = 2 * hf + i
                        t_.matmul(ps[:, 2 * hf + j, i * KEYS0:(i + 1) * KEYS0], qst[DH * j:DH * (j + 1), c, :],
                                  kstv0[DH * j:DH * (j + 1), c, :], start=(i == 0), stop=False,
                                  skip_group_check=True)
                mask = maskb[:, bass.ds(b * CR, CR)]
                for j in range(2):
                    for i in range(2):
                        ins = t_.matmul(ps[:, 2 * hf + j, i * KEYS0 + P:(i + 1) * KEYS0], rowone[:], mask,
                                        start=False, stop=(i == 1), skip_group_check=True)
                ins.then_inc(s_s0, 1)

            def pts0(b, g):
                pe.wait_ge(s_ex0, b * 2 + (g // 2 + 1))
                if not (isinstance(b, int) and b == 0 and g < 2):
                    pe.wait_ge(s_ptd0, b * 4 + (g - 1))
                for i in range(2):
                    for j in range(2):
                        ins = t_.transpose(ps[:, 4 + g % 2, (2 * i + j) * P:(2 * i + j + 1) * P],
                                           prv0[:, 2 * g + i, j * P:(j + 1) * P], ident[:])
                ins.then_inc(s_pt0, 1)

            def pv0(b, g):
                pe.wait_ge(s_ptd0, b * 4 + (g + 1))
                if not (isinstance(b, int) and b == 0) and g == 0:
                    pe.wait_ge(s_on0, b)
                for i in range(2):
                    h = 2 * g + i
                    dst = ps[:, 6, h * DH:(h + 1) * DH]
                    t_.matmul(dst, pt[:, g % 2, 2 * i * P:(2 * i + 1) * P],
                              vvf[:, bass.ds(b * 512 + h * DH, DH)], start=True, stop=False,
                              skip_group_check=True)
                    ins = t_.matmul(dst, pt[0:CR, g % 2, (2 * i + 1) * P:(2 * i + 2) * P],
                                    vvf[0:CR, bass.ds(b * 512 + (8 * 512 + h * DH), DH)], start=False,
                                    stop=True, skip_group_check=True)
                ins.then_inc(s_pv0, 1)

            def ot0(b):
                pe.wait_ge(s_on0, b + 1)
                for c in range(C0):
                    ins = t_.transpose(ps[:, 7, c * P:(c + 1) * P], cnf[:, c * P:(c + 1) * P], ident[:])
                ins.then_inc(s_ot0, 1)

            def y0(b):
                pe.wait_ge(s_ots0, b + 1)
                for c in range(C0):
                    ins = t_.matmul(ps[:, 7, 0:D], ot[:, c, :], wo0[:, c, :], start=(c == 0), stop=(c == C0 - 1))
                ins.then_inc(s_y0, 1)

            def body0(b, first=False, last=False):
                pts0(b, 0)
                pts0(b, 1)
                if not last:
                    scores0(b + 1, 0)
                pv0(b, 0)
                pv0(b, 1)
                if not first:
                    ot0(b - 1)
                pts0(b, 2)
                pts0(b, 3)
                if not last:
                    scores0(b + 1, 1)
                pv0(b, 2)
                if not first:
                    y0(b - 1)
                pv0(b, 3)

            pe.wait_ge(loads["wo0"], 16)
            pe.wait_ge(s_mask, 1)
            pe.wait_ge(s_rone, 1)
            scores0(0, 0)
            scores0(0, 1)
            for i in range(KFIN_AHEAD, len(KFIN)):
                key_norms(i)
            pe.wait_ge(s_kfin, len(KFIN))
            body0(0, first=True)
            with pe.Fori(1, NB - 1) as b:
                body0(b)
            body0(NB - 1, last=True)

            def key1(i):
                c, half = i // 2, i % 2
                if i >= 4:
                    pe.wait_ge(s_k1e, i - 3)
                mm3(ps[:, i % 4, 0:CHALF], two(kv1w, c * P, P), two(feat, TOK + half * CHALF, CHALF))\
                    .then_inc(s_k1, 1)

            pe.wait_ge(s_cs, 1)
            pe.wait_ge(s_kv1w, 4)
            pe.wait_ge(s_ex0, 2 * NB)
            key1(0)
            key1(1)
            ot0(NB - 1)
            key1(2)
            key1(3)
            y0(NB - 1)
            for i in range(4, 2 * C1):
                key1(i)
            for i in range(2 * NB):
                b, half = i // 2, i % 2
                if i >= 4:
                    pe.wait_ge(s_v1e, i - 3)
                else:
                    pe.wait_ge(s_k1e, 2 * C1 - 3 + i)
                mm3(ps[0:CR, i % 4, :], two(feat, TOK + b * CR, CR), two(kv1w, 1024 + half * 512, 512))\
                    .then_inc(s_v1, 1)

            def feat_t(k):
                for t in range(NB):
                    pe.wait_ge(s_xn, 2 * k + t // 4 + 1)
                    ins = t_.transpose(ps[:, XT_BANK[k] + t // 4, (t % 4) * P:(t % 4 + 1) * P], xn[:, t, :], ident[:])
                    if t % 4 == 3:
                        ins.then_inc(s_xt, 1)

            feat_t(0)
            pe.wait_ge(s_gw, 1)
            pe.wait_ge(s_xlo, 2)
            for t in range(NB):
                ins = mm3(ps[:, 6, t * NE:(t + 1) * NE], two(feat, t * P, P), two(gatesp, 0, NE))
            ins.then_inc(s_lg, 1)

            def gu(e, par, i):
                c, th = i // 2, i % 2
                if not (isinstance(e, int) and e == 0 and i < 2):
                    pe.wait_ge(s_sil, e * 8 + (i - 1))
                rhs = two(feat, th * HALF, HALF)
                mm3(ps[:, i % 2, :], two(wsp[par], c * P, P), rhs).then_inc(s_g, 1)
                if not (isinstance(e, int) and e == 0 and i < 2):
                    pe.wait_ge(s_h, e * 8 + (i - 1))
                ins = mm3(ps[:, 2 + i % 2, :], two(wsp[par], FF + c * P, P), rhs)
                ins.then_inc(s_u, 1)

            def y(e, par, i):
                c, th = i // 2, i % 2
                pe.wait_ge(s_hhi, e * 8 + (i + 1))
                pe.wait_ge(s_hlo, e * 8 + (i + 1))
                if c == 0 and not (isinstance(e, int) and e == 0):
                    pe.wait_ge(s_yt, e * 2 + (th - 1))
                ins = mm3(ps[:, 4 + th, :], two(wsp[par], 2 * FF + c * P, P),
                          (hidsp[:, 0, i % 2, :], hidsp[:, 1, i % 2, :]), start=(c == 0), stop=(c == CF - 1))
                ins.then_inc(s_yy, 1)
                return ins

            def expert(e, par, next_ready):
                for i in range(8):
                    if i + 2 < 8:
                        gu(e, par, i + 2)
                    elif next_ready is not None:
                        if i == 6:
                            pe.wait_ge(s_msp[1 - par], next_ready * MP)
                        gu(e + 1, 1 - par, i - 6)
                    y(e, par, i)
                    if i == (7 if isinstance(e, int) and e == 0 else 4):
                        pe.wait_ge(s_wst, e + 1)
                        if not (isinstance(e, int) and e == 0):
                            pe.wait_ge(s_wbs, e * 2)
                        for t in range(NB):
                            ins = t_.transpose(ps[:, 6 + t // 4, (t % 4) * P:(t % 4 + 1) * P],
                                               wtes[:, t:t + 1].to_broadcast([P, P]), ident[:])
                            if t % 4 == 3:
                                ins.then_inc(s_wb, 1)

            pe.wait_ge(s_msp[0], MP)
            pe.wait_ge(s_v1e, 2 * NB)
            gu(0, 0, 0)
            gu(0, 0, 1)
            expert(0, 0, 1)
            expert(1, 1, 2)
            with pe.Fori(1, NE // 2 - 1) as i:
                expert(i * 2, 0, i + 1)
                expert(i * 2 + 1, 1, i + 2)
            expert(NE - 2, 0, NE // 2)
            expert(NE - 1, 1, None)

            for t in range(NB):
                pe.wait_ge(s_ya, 2 * NE + 1 + t // 4)
                ins = t_.transpose(ps[:, t // 4, (t % 4) * P:(t % 4 + 1) * P], yacc[:, t * P:(t + 1) * P], ident[:])
                if t % 4 == 3:
                    ins.then_inc(s_yT, 1)
            pe.wait_ge(s_wq, 1)
            pe.wait_ge(s_yt, 2 * NE)
            pe.wait_ge(s_wbs, 2 * NE)
            for i in range(3):
                for c in range(CQ):
                    ins = t_.transpose(ps[:, 4 + i, c * P:(c + 1) * P], wqn[:, i * CQ + c, :], ident[:])
                ins.then_inc(s_wqt, 1)
            feat_t(1)
            pe.wait_ge(s_q1w, 1)
            pe.wait_ge(s_wqf, 3)
            def query1(i):
                c, half = i % C1, i // C1
                pe.wait_ge(s_xlo, 3 + half)
                if i // 2 >= 2:
                    pe.wait_ge(s_q1a if i % 2 == 0 else s_q1d, i // 2 - 1)
                mm3(ps[:, (4 if i % 2 == 0 else 6) + (i // 2) % 2, :], two(wsp[0], c * P, P),
                    two(feat, half * HALF, HALF)).then_inc(s_q1, 1)

            def scores1(b, hf):
                pe.wait_ge(s_st1, b * 6 + (3 * hf + 3))
                if not (isinstance(b, int) and b == 0):
                    pe.wait_ge(s_sub1, b * 2 + (hf - 1))
                    if hf == 0 and not (isinstance(b, int) and b < 3):
                        pe.wait_ge(s_x3, b - 2)
                for i in range(4):
                    c = 4 * hf + i
                    ins = t_.matmul(ps[:, 2 * hf + i // 2, (i % 2) * 2 * CR:(i % 2 + 1) * 2 * CR], qst[:, c, :],
                                    kstv1[:, c, :], start=True, stop=True, skip_group_check=True)
                ins.then_inc(s_s1, 1)

            def pts1(b, g):
                pe.wait_ge(s_ex1, b * 2 + (g // 2 + 1))
                if g < 2:
                    if not (isinstance(b, int) and b == 0):
                        pe.wait_ge(s_pta1, b * 4 + (g - 1))
                elif not (isinstance(b, int) and b == 0):
                    pe.wait_ge(s_ota1, b * 2 + (g - 3))
                for i in range(4):
                    ins = t_.transpose(ps[0:CR, 4 + g % 2, i * P:(i + 1) * P], prv1[:, 4 * g + i, 0:CR], ident[:])
                ins.then_inc(s_pt1, 1)

            def pv1(b, g):
                pe.wait_ge(s_pta1, b * 4 + (g + 1))
                if not (isinstance(b, int) and b == 0) and g % 2 == 0:
                    pe.wait_ge(s_on1, b * 2 + (g // 2 - 1))
                for i in range(4):
                    h = 4 * g + i
                    k = (h % 8) * DH
                    ins = t_.matmul(ps[:, 6 + g // 2, k:k + DH], pt[0:CR, g % 2, i * P:(i + 1) * P],
                                    vvf[0:CR, bass.ds(b * 1024 + h * DH, DH)], start=True, stop=True,
                                    skip_group_check=True)
                ins.then_inc(s_pv1, 1)

            def ot1(b, k):
                pe.wait_ge(s_on1, b * 2 + (k + 1))
                for c in range(4):
                    ins = t_.transpose(ps[:, 4 + k, c * P:(c + 1) * P], cnf[:, (4 * k + c) * P:(4 * k + c + 1) * P],
                                       ident[:])
                ins.then_inc(s_ot1, 1)

            def y1(b, last_scores=None):
                pe.wait_ge(s_ota1, b * 2 + 2)
                pe.wait_ge(s_sub1, b * 2 + 5 if last_scores is None else last_scores)
                if last_scores == 2 * NB:
                    pe.wait_ge(s_x3, b)
                for c in range(C1):
                    ins = t_.matmul(ps[:, 0, YCOL:YCOL + D], ot[:, c, :], wo1[:, c, :], start=(c == 0),
                                    stop=(c == C1 - 1), skip_group_check=True)
                ins.then_inc(s_y1, 1)

            def body1(b, first=False, last=False):
                pts1(b, 0)
                pts1(b, 1)
                if not last:
                    scores1(b + 1, 0)
                pv1(b, 0)
                if not first:
                    ot1(b - 1, 0)
                pv1(b, 1)
                if not first:
                    ot1(b - 1, 1)
                if not last:
                    scores1(b + 1, 1)
                pts1(b, 2)
                pts1(b, 3)
                if not first:
                    y1(b - 1, 2 * NB if last else None)
                pv1(b, 2)
                pv1(b, 3)

            for i in range(14):
                query1(i)
            scores1(0, 0)
            query1(14)
            scores1(0, 1)
            query1(15)
            pe.wait_ge(loads["wo1"], 16)
            pe.wait_ge(s_q1a, C1)
            pe.wait_ge(s_q1d, C1)
            body1(0, first=True)
            body1(1)
            with pe.Fori(2, NB - 1) as b:
                body1(b)
            body1(NB - 1, last=True)
            pe.wait_ge(s_pta1, 4 * NB)
            ot1(NB - 1, 0)
            ot1(NB - 1, 1)
            y1(NB - 1, 2 * NB)

            gcount = [0]

            def global_max():
                k = gcount[0]
                gcount[0] += 1
                pe.wait_ge(s_am, k + 1)
                t_.transpose(ps[:, 7, 0:P], qs[:, 0:1].to_broadcast([P, P]), ident[:]).then_inc(s_gmb, 1)

            for t in range(NB):
                pe.wait_ge(s_x4, t // 4 + 1)
                ins = t_.transpose(ps[:, t // 4, (t % 4) * P:(t % 4 + 1) * P], xn[:, t, :], ident[:])
                if t % 4 == 3:
                    ins.then_inc(s_xqt, 1)
            global_max()
            pe.wait_ge(s_wqlo, 1)
            for i in range(4 * CQ):
                chunk = CQ + i // 2 if i < 2 * CQ else i // 2 - CQ
                pe.wait_ge(s_xqlo, i % 2 + 1)
                if i >= 4:
                    pe.wait_ge(s_uge, i - 3)
                mm3(ps[:, 2 + i % 4, :], two(wsp[1], chunk * P, P), two(feat, (i % 2) * HALF, HALF))\
                    .then_inc(s_ug, 1)
                if i == 2 * CQ + 1:
                    global_max()
            for _ in range(3):
                global_max()
            for c in range(CQ):
                pe.wait_ge(s_oint, c + 1)
                for t in range(NB):
                    ins = t_.matmul(ps[:, t // 4, (t % 4) * P:(t % 4 + 1) * P],
                                    prb[:, c * TOK + t * P:c * TOK + (t + 1) * P],
                                    wraw[1][:, (2 * CQ + c) * P:(2 * CQ + c + 1) * P], start=(c == 0 and t % 4 == 0),
                                    stop=(c == CQ - 1 and t % 4 == 3), skip_group_check=True)
                    if c == CQ - 1 and t % 4 == 3:
                        ins.then_inc(s_dn, 1)


def kernel(**inputs):
    import concourse.bacc as _bacc
    from concourse.bass_utils import run_bass_kernel_spmd as _run

    g = {k: np.asarray(v) for k, v in inputs.items()}
    f32 = np.float32
    arrays = {
        "x": g["x"], "ctx": g["ctx_1024"],
        "ctxT": g["ctx_1024"].reshape(CTX, D).T,
        "mask": g["mask_BxS2_bk0"].reshape(1, CTX),
        "vec": np.stack([g["L0_xattn_ln_x_w"], g["L0_xattn_ln_x_b"], g["L0_xattn_ln_l_w"], g["L0_xattn_ln_l_b"],
                         np.tile(g["L0_xattn_q_scale"], 2), np.tile(g["L0_xattn_k_scale"], 2)], axis=1),
        "lno": np.broadcast_to(np.stack([g["L0_xattn_ln_o_w"], g["L0_xattn_ln_o_b"]]), (P, 2, D)),
        "Wq": g["L0_xattn_Wq"], "Wkv": g["L0_xattn_Wkv"], "Wo": g["L0_xattn_Wo"],
        "gateT": g["L0_ffn_gate_w"].T,
        "moe": np.concatenate([g["L0_ffn_w1"].transpose(0, 2, 1), g["L0_ffn_w3"].transpose(0, 2, 1),
                               g["L0_ffn_w2"].transpose(0, 2, 1).reshape(NE, CF, P, D).transpose(0, 2, 1, 3)
                               .reshape(NE, P, CF * D)], axis=2),
        "W1q": g["L1_xattn_Wq"], "W1k": g["L1_xattn_Wk"], "W1v": g["L1_xattn_Wv"], "W1o": g["L1_xattn_Wo"],
        "wup": g["L1_ffn_w_up"], "wgate": g["L1_ffn_w_gate"], "wdown": g["L1_ffn_w_down"],
        "ident": np.eye(P, dtype=f32),
        "bones": np.repeat(np.eye(2, dtype=f32), DH, axis=0),
        "hsel": np.repeat(np.eye(H0, dtype=f32), DH, axis=1),
    }
    arrays = {k: np.ascontiguousarray(v) for k, v in arrays.items()}
    nc = _bacc.Bacc("TRN2", target_bir_lowering=False, num_devices=1)
    aps = {k: nc.dram_tensor(f"in_{k}", v.shape, mybir.dt.from_np(v.dtype), kind="ExternalInput").ap()
           for k, v in arrays.items()}
    out = nc.dram_tensor("out_dram", (NB, P, D), F32, kind="ExternalOutput").ap()
    two_layer_kernel(nc, aps, out)
    r = _run(nc, [{f"in_{k}": v for k, v in arrays.items()}], core_ids=[0])
    return r.results[0]["out_dram"]
```

```python
from contextlib import ExitStack

import numpy as np
import concourse.bass as bass
from concourse import mybir

F32 = mybir.dt.float32
F32R = mybir.dt.float32r
BF16 = mybir.dt.bfloat16
I32 = mybir.dt.int32
U8 = mybir.dt.uint8
ALU = mybir.AluOpType
ACT = mybir.ActivationFunctionType
AX = mybir.AxisListType

NB, P, D = 8, 128, 128
TOK = NB * P
CR = 77
CTX = NB * CR
HALF = TOK // 2
CHALF = CTX // 2
H0, H1, DH = 8, 16, 64
C0, C1 = H0 * DH // P, H1 * DH // P
KEYS0 = P + CR
NE, FF = 8, 512
CF = FF // P
MP = 3
FFQ = 384
CQ = FFQ // P
QBLK = 32
YCOL = 512 - D
LN_EPS = 1e-5
L2_EPS2 = 1e-24
NEG = 1e30
POOL_CLIP = 1
MAGIC = 1.5 * 2.0 ** 23
QMAX = 32767.0
RSQRT_SEED = float(0x5F3759DF)


def two_layer_kernel(nc, a, out):
    ctx = ExitStack()
    with ctx:
        def sb(name, shape, dt=F32):
            return ctx.enter_context(nc.sbuf_tensor(name, shape, dt))

        def sem(name):
            return ctx.enter_context(nc.semaphore(name))

        ps = ctx.enter_context(nc.psum_tensor("ps", [P, 8, 512], F32))

        x = sb("x", [P, NB, D])
        xn = sb("xn", [P, NB, D])
        cn = sb("cn", [P, NB, D])
        feat = sb("feat", [P, 2, TOK + CTX], F32R)
        kt1 = sb("kt1", [P, C1, CTX])
        qk = sb("qk", [P, 8, TOK])
        kc = sb("kc", [P, C0, CTX])
        vv = sb("vv", [P, 16, 512])
        sq = sb("sq", [P, 4, 512])
        wraw = [sb(f"wraw{i}", [P, 1536]) for i in range(2)]
        wsp = [sb(f"wsp{i}", [P, 2, 1536], F32R) for i in range(2)]
        kv1w = sb("kv1w", [P, 2, 2048], F32R)
        pr = sb("pr", [P, 2048])
        pt = sb("pt", [P, 2, 512])
        ot = sb("ot", [P, C1, P])
        qst = sb("qst", [P, C1, P])
        kst = sb("kst", [P, C0 * KEYS0])
        ident = sb("ident", [P, P])
        lno = sb("lno", [P, 2, D])
        vec = sb("vec", [P, 6])
        qks = sb("qks", [P, 1])
        bones = sb("bones", [P, 2])
        gatew = sb("gatew", [P, NE])
        gatesp = sb("gatesp", [P, 2, NE], F32R)
        maskb = sb("maskb", [P, CTX], BF16)
        rowone = sb("rowone", [P, P], BF16)
        st = sb("st", [P, 16, 6])
        mv = sb("mv", [P, 16, 2])
        var = sb("var", [P, 16])
        rstd = sb("rstd", [P, 16])
        nmr = sb("nmr", [P, NB])
        nt = sb("nt", [P, 192])
        rn = sb("rn", [P, 192])
        rqst = sb("rqst", [P, H0])
        mx = sb("mx", [P, H1])
        nbias = sb("nbias", [P, H0])
        sums = sb("sums", [P, H1])
        rsum = sb("rsum", [P, H1])
        wtes = sb("wtes", [P, NB])
        qs = sb("qs", [P, 24])
        magic = sb("magic", [P, 4])

        xf = x[:].rearrange("p b d -> p (b d)")
        xnf = xn[:].rearrange("p b d -> p (b d)")
        cnf = cn[:].rearrange("p b d -> p (b d)")
        ktf = kt1[:].rearrange("p c k -> p (c k)")
        featf = ktf[:, 0:TOK + CTX]
        qkf = qk[:].rearrange("p c k -> p (c k)")
        kcf = kc[:].rearrange("p c k -> p (c k)")
        vvf = vv[:].rearrange("p c k -> p (c k)")
        sqf = sq[:].rearrange("p c k -> p (c k)")
        wo1 = sqf[:, 0:C1 * D].rearrange("p (c d) -> p c d", c=C1)
        kstv0 = kst[:, 0:C0 * KEYS0].rearrange("p (c k) -> p c k", c=C0)
        kstv1 = wraw[0][:, 0:C1 * 2 * CR].rearrange("p (c k) -> p c k", c=C1)
        prv0 = pr[:].rearrange("p (h k) -> p h k", h=H0)
        prv1 = pr[:].rearrange("p (h k) -> p h k", h=H1)
        silu = qkf[:, 0:1024].rearrange("p (s n) -> p s n", s=2)
        hid = qkf[:, 1024:2048].rearrange("p (s n) -> p s n", s=2)
        ytmp = qkf[:, 2048:3072].rearrange("p (s n) -> p s n", s=2)
        yacc = qkf[:, 3072:4096]
        wteb = qkf[:, 4096:5120]
        hidsp = kv1w[:].rearrange("p s n -> p (s n)")[:, 0:2048].rearrange("p (a s n) -> p a s n", a=2, s=2)
        NQ = CQ * TOK
        upb, gab, sgb, prb = qkf[:, 0:NQ], qkf[:, NQ:2 * NQ], vvf[:, 0:NQ], vvf[:, NQ:2 * NQ]
        SX, IX, SU, IU, SG, IG, SG2, IG2, SO, IO, UX = range(1, 12)

        rkhi, rklo = feat[0:H0, 0, :], feat[0:H0, 1, :]
        hselr = wsp[1][0:H0, 0, 0:C0 * P]
        wo0 = sqf[:, C1 * D:(C1 + C0) * D].rearrange("p (c d) -> p c d", c=C0)
        wqn = kcf[:, 0:3 * CQ * D].rearrange("p (c d) -> p c d", d=D)
        rt = kcf[:, 3 * CQ * D:3 * CQ * D + 12 * NB * NE].rearrange("p (k n) -> p k n", n=NB * NE)
        hsel = pt[0:H0, 0, :]

        wqs = kcf[:, 2048:2048 + 9 * CQ * D // QBLK].rearrange("p (k n) -> p k n", k=3)
        wblk = wqn.rearrange("p c (k w) -> p (c k) w", w=QBLK)
        wmax, wscale, winv = (wqs[:, i, :] for i in range(3))
        n2 = kst[:, 0:192]
        mask8 = kst[0:1, 256:256 + CTX // 4].bitcast(U8)
        wtef = rt[:, 11, :]

        loads = {}

        def load_sem(name):
            loads[name] = sem("ld_" + name)
            return loads[name]

        for name in ("x", "ctx", "ident", "vec", "w0", "w0kv", "small", "mask", "wo0", "wqn", "lno", "gate",
                     "hsel", "ctxraw", "kv1k", "kv1v", "q1", "wo1"):
            load_sem(name)
        ld_moe = [sem("ld_moe0"), sem("ld_moe1")]
        s_out = sem("s_out")
        dv = sem("dve_chain")
        pl = sem("pool_chain")
        ac = sem("act_chain")
        s_norm1, s_cnorm1 = sem("latents_normed"), sem("ctx_normed")
        s_trn1 = sem("feat1_in_psum")
        s_ff1 = sem("feat1_f32")
        s_fhi1 = sem("feat1_hi")
        s_flo1 = sem("feat1_lo")
        s_w0hi, s_w0 = sem("w0_hi"), sem("w0_split")
        s_nmr = sem("ctx_mean_rstd")
        s_qks = sem("qk_scale")
        s_pq, s_pk, s_pv = sem("proj_q"), sem("proj_k"), sem("proj_v")
        s_qev, s_kev = sem("q_evacuated"), sem("k_evacuated")
        s_sqq, s_sqk = sem("q_squared"), sem("k_squared")
        s_n2q, s_n2k = sem("q_norms_psum"), sem("k_norms_psum")
        s_va, s_vd = sem("v_evac_act"), sem("v_evac_dve")
        s_rn = sem("head_rnorm")
        s_rkp, s_rkt, s_rkhi = sem("rk_rows_psum"), sem("rk_rows_split"), sem("rk_rows_hi")
        s_rkb, s_kfin = sem("rk_bcast_psum"), sem("k_final")
        s_mask, s_rone, s_padz = sem("mask_bias"), sem("ones_row"), sem("pad_zeroed")
        s_hsel = sem("hsel_r")
        s_st0 = sem("qk_staged0")
        s_s0, s_nb0, s_ex0 = sem("scores0"), sem("bias0"), sem("probs0")
        s_mx0 = sem("max0")
        s_pt0, s_pte0 = sem("pt0_psum"), sem("pt0_sb")
        s_pv0, s_rs0, s_on0 = sem("pv0"), sem("rsum0"), sem("o0_scaled")
        s_ot0, s_ots0, s_y0, s_ys0 = sem("ot0_psum"), sem("ot0_sb"), sem("y0_psum"), sem("y0_sb")
        s_xb = sem("x_plus_bias")
        s_cs = sem("ctxraw_split")
        s_kv1w = sem("kv1_weights_split")
        s_k1, s_k1e, s_v1, s_v1e = sem("k1_psum"), sem("k1_sb"), sem("v1_psum"), sem("v1_sb")
        s_xn, s_xt, s_xhi, s_xlo = sem("x_normed"), sem("xt_psum"), sem("xt_hi"), sem("xt_lo")
        s_gw, s_lg, s_rex, s_rin = sem("gate_split"), sem("logits"), sem("route_exp"), sem("route_in")
        s_wte = sem("token_weights")
        s_msp = [sem("moe_split0"), sem("moe_split1")]
        s_g, s_u, s_sil, s_h = sem("moe_g"), sem("moe_u"), sem("moe_silu"), sem("moe_h")
        s_hhi, s_hlo, s_yy = sem("moe_h_hi"), sem("moe_h_lo"), sem("moe_y_step")
        s_wst, s_wb, s_wbs = sem("wte_staged"), sem("wte_bcast_psum"), sem("wte_bcast_sb")
        s_yt, s_ya = sem("y_weighted"), sem("y_added")
        s_msub = sem("moe_split_hi")
        s_yT = sem("moe_out_tok")
        s_wqs = sem("wq_scales")
        s_wq, s_wqt, s_wqhi, s_wqf, s_wqlo = (sem("wq_dequant"), sem("wqT_psum"), sem("wqT_hi"), sem("wqT_f32"),
                                              sem("wqT_lo"))
        s_q1w = sem("q1w_split")
        s_q1, s_q1e = sem("q1_psum"), sem("q1_sb")
        s_st1, s_stq1 = sem("k_staged1"), sem("q_staged1")
        s_s1, s_mx1, s_sub1 = sem("scores1"), sem("max1"), sem("shifted1")
        s_ex1, s_rs1 = sem("probs1"), sem("rsum1")
        s_sum1 = sem("sum1")
        s_pt1, s_pta1 = sem("pt1_psum"), sem("pt1_sb")
        s_pv1, s_on1, s_ot1, s_ota1 = sem("pv1"), sem("o1_scaled"), sem("ot1_psum"), sem("ot1_sb")
        s_bn1 = sem("x3_stats")
        s_y1, s_x3 = sem("y1_psum"), sem("x3")
        s_am, s_gmb = sem("absmax_col"), sem("absmax_bcast")
        s_x4, s_xqt, s_xsc = sem("x4_normed"), sem("x4T_psum"), sem("x4_scale")
        s_xqm, s_xqhi, s_xqlo = sem("x_ints_magic"), sem("x_ints_hi"), sem("x_ints_lo")
        s_ug, s_uge = sem("gate_up_psum"), sem("gate_up_sb")
        s_magic = sem("magic_cols")
        s_gint, s_sig, s_sgm = sem("gate_ints"), sem("gate_sigmoid"), sem("sigmoid_magic")
        s_clip = sem("sigmoid_clipped")
        s_usc, s_upm, s_up = sem("up_scale"), sem("up_ints_magic"), sem("up_ints")
        s_g2s, s_g2m = sem("g2_scale"), sem("g2_ints_magic")
        s_oint = sem("o_ints")
        s_dn, s_res = sem("down_psum"), sem("result")

        QKSEQ = []
        for c in range(C0):
            QKSEQ += [("q", c, 0), ("k", c, 0), ("q", c, 1), ("k", c, 1), ("k", c, 2), ("k", c, 3)]
        QSEQ = [g for g in QKSEQ if g[0] == "q"]
        KSEQ = [g for g in QKSEQ if g[0] == "k"]
        V_AMONG = 9
        ORDER = []
        for i, group in enumerate(QKSEQ):
            ORDER.append(group)
            if i >= 6 and i % 2 == 0:
                ORDER.append(("v", (i - 6) // 2, None))
        KFIN = [(c, part) for parts in ((0, 2), (1, 3)) for part in parts for c in range(C0)]
        KFIN_AHEAD = 12

        def v_on_act(t):
            return t >= V_AMONG or t % 2 == 0

        def v_out(t):
            return (s_va if v_on_act(t) else s_vd), sum(v_on_act(u) == v_on_act(t) for u in range(t + 1))

        def v_bank(t):
            return (2, 3, 7)[t % 3]

        def row_bank(part):
            return (0, 1, 4, 5)[part]

        XT_BANK = (4, 2)

        LO_ON_POOL = 6

        YT_BANK = (6, 0)

        def gu_bank(i):
            return (0, 1, 4, 5)[i % 4]

        def kfin_bank(i):
            return (6, 7, 4, 5)[i % 4]

        def cols(part):
            return (part * HALF, HALF) if part < 2 else (TOK + (part - 2) * CHALF, CHALF)

        def kdst(c, part):
            if part < 2:
                return qk[:, C0 + c, part * HALF:(part + 1) * HALF]
            return kc[:, c, (part - 2) * CHALF:(part - 1) * CHALF]

        def tile_cols(t):
            return (t * P, P) if t < NB else (TOK + (t - NB) * CR, CR)

        block = ctx.enter_context(nc.Block())

        @block.sync
        def _(sp):
            def load(dst, src, name):
                sp.dma_start(dst, src).then_inc(loads[name], 16)

            load(x[:], a["x"].rearrange("b t d -> t b d"), "x")
            load(cn[0:CR], a["ctx"].rearrange("b t d -> t b d"), "ctx")
            load(wraw[0][:, 0:512], a["Wq"], "w0")
            load(wraw[0][:, 512:1536], a["Wkv"], "w0kv")
            load(wraw[1][:, 0:1024], a["W1k"], "kv1k")
            load(lno[:], a["lno"], "lno")
            sp.wait_ge(s_w0, 2)
            load(wraw[0][:, 0:1024], a["W1v"], "kv1v")
            sp.wait_ge(s_flo1, 4)
            load(ktf[:, 0:CTX], a["ctxT"], "ctxraw")
            sp.wait_ge(s_n2q, len(QSEQ))
            sp.wait_ge(s_n2k, len(KSEQ))
            load(wo0, a["Wo"].rearrange("(c p) d -> p c d", p=P), "wo0")
            load(wo1, a["W1o"].rearrange("(c p) d -> p c d", p=P), "wo1")
            sp.wait_ge(s_kv1w, 4)
            for e in range(2):
                sp.dma_start(wraw[e][:], a["moe"][e]).then_inc(ld_moe[e], 16)
            sp.wait_ge(s_st0, 8 * NB)
            load(wqn[:, 0:CQ], a["wup"].rearrange("(c p) d -> p c d", p=P), "wqn")
            load(wqn[:, CQ:2 * CQ], a["wgate"].rearrange("(c p) d -> p c d", p=P), "wqn")
            load(wqn[:, 2 * CQ:3 * CQ], a["wdown"].rearrange("p (c k) -> p c k", c=CQ), "wqn")
            with sp.Fori(0, NE // 2 - 1) as i:
                for par in range(2):
                    sp.wait_ge(s_msp[par], i * MP + MP)
                    sp.dma_start(wraw[par][:].unsqueeze(1), a["moe"].rearrange("e p n -> p e n")
                                 [:, bass.ds(i * 2 + (2 + par), 1), :]).then_inc(ld_moe[par], 16)
            sp.wait_ge(s_msp[0], NE // 2 * MP)
            load(wraw[0][:, 0:1024], a["W1q"], "q1")
            for i in range(2):
                half = slice(i * NB // 2, (i + 1) * NB // 2)
                sp.wait_ge(s_res, i + 1)
                sp.dma_start(out[half].rearrange("b t d -> t b d"), xn[:, half, :]).then_inc(s_out, 16)
            sp.wait_ge(s_out, 32)

        @block.gpsimd
        def _(pool):
            g = nc.gpsimd
            n = [0]

            def link(ins):
                n[0] += 1
                ins.then_inc(pl, 1)
                pool.wait_ge(pl, n[0])

            g.memset(rowone[:], 0.0).then_inc(pl, 1)
            g.memset(maskb[:], 0.0).then_inc(pl, 1)
            n[0] = 2
            pool.wait_ge(pl, 2)
            g.memset(rowone[0:1, :], 1.0).then_inc(s_rone, 1)
            g.memset(pr[:], 0.0).then_inc(s_padz, 1)
            g.memset(magic[:, 0:1], MAGIC).then_inc(s_magic, 1)
            g.memset(magic[:, 1:2], -MAGIC).then_inc(s_magic, 1)
            g.memset(magic[:, 2:3], 0.0).then_inc(s_magic, 1)
            pool.wait_ge(loads["mask"], 16)
            g.tensor_scalar(maskb[0:1, :], mask8, -1.0, NEG, ALU.add, ALU.mult).then_inc(s_mask, 1)

            def split(dst, lo_cols, raw, s):
                k, w = lo_cols
                link(g.tensor_copy(dst[:, 0, k:k + w], raw))
                g.tensor_tensor(dst[:, 1, k:k + w], raw, dst[:, 0, k:k + w].bitcast(F32), ALU.subtract).then_inc(s, 1)

            for i, k in enumerate((slice(0, 512), slice(512, 1536))):
                pool.wait_ge(s_w0hi, i + 1)
                g.tensor_tensor(wsp[0][:, 1, k], wraw[0][:, k], wsp[0][:, 0, k].bitcast(F32),
                                ALU.subtract).then_inc(s_w0, 1)
            pool.wait_ge(loads["gate"], 16)
            split(gatesp, (0, NE), gatew[:], s_gw)
            pool.wait_ge(loads["kv1k"], 16)
            split(kv1w, (0, 512), wraw[1][:, 0:512], s_kv1w)
            split(kv1w, (512, 512), wraw[1][:, 512:1024], s_kv1w)
            pool.wait_ge(loads["kv1v"], 16)
            split(kv1w, (1024, 512), wraw[0][:, 0:512], s_kv1w)
            split(kv1w, (1536, 512), wraw[0][:, 512:1024], s_kv1w)

            pool.wait_ge(loads["lno"], 16)
            pool.wait_ge(s_norm1, 2)
            g.tensor_tensor(x[:], x[:], lno[:, 1:2, :].to_broadcast([P, NB, D]), ALU.add).then_inc(s_xb, 1)

            def stage0(b, hf, first=False):
                c = slice(2 * hf, 2 * hf + 2)
                ck = slice(C0 + 2 * hf, C0 + 2 * hf + 2)
                if not first:
                    pool.wait_ge(s_s0, b * 2 + (hf - 1))
                g.tensor_copy(qst[:, c, :], qk[:, c, bass.ds(b * P, P)]).then_inc(s_st0, 1)
                g.tensor_copy(kstv0[:, c, 0:P], qk[:, ck, bass.ds(b * P, P)]).then_inc(s_st0, 1)
                g.tensor_copy(kstv0[:, c, P:KEYS0], kc[:, c, bass.ds(b * CR, CR)]).then_inc(s_st0, 1)
                if not first:
                    pool.wait_ge(s_ex0, b * 2 + (hf - 1))
                pool.wait_ge(s_rn, 1)
                g.tensor_copy(rqst[:, 4 * hf:4 * hf + 4], rn[:, bass.ds(b * H0 + 4 * hf, 4)]).then_inc(s_st0, 1)

            pool.wait_ge(s_qev, len(QSEQ))
            pool.wait_ge(s_kfin, len(KFIN) // 2)
            stage0(0, 0, first=True)
            stage0(0, 1, first=True)
            pool.wait_ge(s_kfin, len(KFIN))
            with pool.Fori(1, NB) as b:
                stage0(b, 0)
                stage0(b, 1)

            pool.wait_ge(loads["ctxraw"], 16)
            pool.wait_ge(s_pk, len(KSEQ))
            pool.wait_ge(s_pv, 16)
            pool.wait_ge(s_rkb, len(KSEQ))
            split(feat, (TOK, CTX), ktf[:, 0:CTX], s_cs)

            for e in range(2):
                pool.wait_ge(ld_moe[e], 16)
                for j in range(MP):
                    split(wsp[e], (j * FF, FF), wraw[e][:, j * FF:(j + 1) * FF], s_msp[e])
            pool.wait_ge(s_ys0, NB)

            def add_expert(e):
                for th in range(2):
                    pool.wait_ge(s_yt, e * 2 + (th + 1))
                    g.tensor_tensor(yacc[:, th * HALF:(th + 1) * HALF], yacc[:, th * HALF:(th + 1) * HALF],
                                    ytmp[:, th, :], ALU.add).then_inc(s_ya, 1)

            for th in range(2):
                g.memset(yacc[:, th * HALF:(th + 1) * HALF], 0.0).then_inc(s_ya, 1)
            for i in range(LO_ON_POOL):
                slot = i % 2
                pool.wait_ge(s_hhi, i + 1)
                g.tensor_tensor(hidsp[:, 1, slot, :], hid[:, slot, :], hidsp[:, 0, slot, :].bitcast(F32),
                                ALU.subtract).then_inc(s_hlo, 1)
            def of_blocks(col):
                return col.unsqueeze(2).to_broadcast([P, 3 * CQ * D // QBLK, QBLK])

            pool.wait_ge(s_wqs, 1)
            link(g.tensor_tensor(wblk, wblk, of_blocks(winv), ALU.mult))
            link(g.tensor_scalar(wblk, wblk, MAGIC, 1.0, ALU.add, ALU.mult))
            link(g.tensor_scalar(wblk, wblk, -MAGIC, 1.0, ALU.add, ALU.mult))
            g.tensor_tensor(wblk, wblk, of_blocks(wscale), ALU.mult).then_inc(s_wq, 1)
            with pool.Fori(0, NE // 2 - 1) as i:
                for par in range(2):
                    for j in range(MP):
                        k = slice(j * FF, (j + 1) * FF)
                        pool.wait_ge(s_msub, i * (2 * MP) + (par * MP + j + 1))
                        g.tensor_tensor(wsp[par][:, 1, k], wraw[par][:, k], wsp[par][:, 0, k].bitcast(F32),
                                        ALU.subtract).then_inc(s_msp[par], 1)
                    e = i * 2 + par
                    pool.wait_ge(s_ya, e * 2 + 2)
                    add_expert(e)
            pool.wait_ge(loads["q1"], 16)
            pool.wait_ge(s_yy, 8 * (NE - 1))
            split(wsp[0], (0, 1024), wraw[0][:, 0:1024], s_q1w)
            pool.wait_ge(s_ya, (NE - 2) * 2 + 2)
            add_expert(NE - 2)

            def stage_k1(b, hf, count):
                c = slice(4 * hf, 4 * hf + 4)
                for j in range(2):
                    if not (isinstance(count, int) and count == 0 and j == 0):
                        pool.wait_ge(s_st1, count + j)
                    pool.wait_ge(s_k1e, 2 * C1)
                    g.tensor_copy(kstv1[DH * j:DH * (j + 1), c, CR * j:CR * (j + 1)],
                                  kt1[DH * j:DH * (j + 1), c, bass.ds(b * CR, CR)]).then_inc(s_st1, 1)

            def stage1(b, hf):
                pool.wait_ge(s_s1, b * 2 + (hf - 1))
                stage_k1(b, hf, b * 4 + 2 * hf)

            pool.wait_ge(s_q1w, 1)
            link(g.memset(wraw[0][:, 0:C1 * 2 * CR], 0.0))
            stage_k1(0, 0, 0)
            stage_k1(0, 1, 2)
            with pool.Fori(1, NB) as b:
                stage1(b, 0)
                stage1(b, 1)

            pool.wait_ge(s_wqf, 3)
            pool.wait_ge(s_wqhi, 3)
            g.tensor_tensor(wsp[1][:, 1, 0:3 * CQ * D], wraw[1][:, 0:3 * CQ * D],
                            wsp[1][:, 0, 0:3 * CQ * D].bitcast(F32), ALU.subtract).then_inc(s_wqlo, 1)

            w = sgb[:, POOL_CLIP * TOK:(POOL_CLIP + 1) * TOK]
            pool.wait_ge(s_sgm, POOL_CLIP + 1)
            g.tensor_scalar(w, w, MAGIC + 65535.0, MAGIC, ALU.min, ALU.max).then_inc(s_clip, 1)
            for c in range(CQ):
                w = upb[:, c * TOK:(c + 1) * TOK]
                pool.wait_ge(s_upm, c + 1)
                g.tensor_scalar(w, w, -MAGIC, 1.0, ALU.add, ALU.mult).then_inc(s_up, 1)

        @block.scalar
        def _(act):
            s = nc.scalar

            def load(dst, src, name):
                act.dma_start(dst, src).then_inc(loads[name], 16)

            load(ident[:], a["ident"], "ident")
            load(vec[:], a["vec"], "vec")
            load(bones[:], a["bones"], "small")
            load(mask8, a["mask"], "mask")
            load(gatew[:], a["gateT"], "gate")
            load(hsel, a["hsel"], "hsel")
            for name, k in (("w0", slice(0, 512)), ("w0kv", slice(512, 1536))):
                act.wait_ge(loads[name], 16)
                s.activation(wsp[0][:, 0, k], wraw[0][:, k], ACT.Copy).then_inc(s_w0hi, 1)
            act.wait_ge(loads["hsel"], 16)
            s.activation(hselr, hsel, ACT.Copy).then_inc(s_hsel, 1)
            act.wait_ge(s_nmr, 1)
            for t in range(NB):
                ins = s.activation(cn[0:CR, t, :], cn[0:CR, t, :], ACT.Identity, bias=nmr[0:CR, t:t + 1],
                                   scale=rstd[0:CR, NB + t:NB + t + 1])
                if t % 4 == 3:
                    ins.then_inc(s_cnorm1, 1)
            for i in range(4):
                k, w = cols(i)
                act.wait_ge(s_ff1, i + 1)
                s.activation(feat[:, 0, k:k + w], featf[:, k:k + w], ACT.Copy).then_inc(s_fhi1, 1)
            nq = nk = 0
            act.wait_ge(s_qks, 1)

            def v_evac(t):
                r = tile_cols(t)[1]
                act.wait_ge(s_pv, t + 1)
                s.activation(vv[0:r, t, :], ps[0:r, v_bank(t), :], ACT.Copy).then_inc(s_va, 1)

            for kind, c, part in ORDER:
                if kind == "v":
                    if v_on_act(c):
                        v_evac(c)
                elif kind == "q":
                    act.wait_ge(s_pq, nq + 1)
                    if nq >= 2:
                        act.wait_ge(s_n2q, nq - 1)
                    bank = ps[:, 4 + nq % 2, :]
                    s.activation(sq[:, nq % 2, :], bank, ACT.Square).then_inc(s_sqq, 1)
                    s.activation(qk[:, c, part * HALF:(part + 1) * HALF], bank, ACT.Identity,
                                 scale=qks[:]).then_inc(s_qev, 1)
                    nq += 1
                else:
                    w = cols(part)[1]
                    act.wait_ge(s_kev, nk + 1)
                    if nk >= 2:
                        act.wait_ge(s_n2k, nk - 1)
                    s.activation(sq[:, 2 + nk % 2, 0:w], kdst(c, part), ACT.Square).then_inc(s_sqk, 1)
                    nk += 1
            for t in range(V_AMONG, 16):
                v_evac(t)
            for i in range(4):
                k, w = cols(i)
                act.wait_ge(s_rkp, i + 1)
                s.activation(rkhi[:, k:k + w], ps[0:H0, row_bank(i), 0:w], ACT.Copy).then_inc(s_rkhi, 1)

            def exps0(b, hf):
                act.wait_ge(s_nb0, b * 2 + (hf + 1))
                for h in range(4 * hf, 4 * hf + 4):
                    j, i = h % 2, (h // 2) % 2
                    ins = s.activation(prv0[:, h, 0:KEYS0], ps[:, 2 * hf + j, i * KEYS0:(i + 1) * KEYS0], ACT.Exp,
                                       bias=nbias[:, h:h + 1], scale=rqst[:, h:h + 1], accum_out=sums[:, h:h + 1])
                ins.then_inc(s_ex0, 1)

            def ot_evac0(b):
                act.wait_ge(s_ot0, b + 1)
                s.activation(ot[:, 0:C0, :], ps[:, 7, :], ACT.Copy).then_inc(s_ots0, 1)

            def body0(b, first=False):
                act.wait_ge(s_pt0, b * 4 + 2)
                act.wait_ge(s_rs0, b * 2 + 1)
                exps0(b + 1, 0)
                if not first:
                    ot_evac0(b - 1)
                act.wait_ge(s_pt0, b * 4 + 4)
                act.wait_ge(s_rs0, b * 2 + 2)
                exps0(b + 1, 1)

            act.wait_ge(s_padz, 1)
            exps0(0, 0)
            exps0(0, 1)
            body0(0, first=True)
            with act.Fori(1, NB - 1) as b:
                body0(b)

            def pt_evac0(g):
                b = NB - 1
                act.wait_ge(s_pt0, b * 4 + (g + 1))
                act.wait_ge(s_pv0, b * 4 + (g - 1))
                s.activation(pt[:, g % 2, :], ps[:, 4 + g % 2, :], ACT.Copy).then_inc(s_pte0, 1)

            pt_evac0(0)
            pt_evac0(1)
            ot_evac0(NB - 2)
            pt_evac0(2)
            pt_evac0(3)

            def k1_evac(i):
                c, half = i // 2, i % 2
                act.wait_ge(s_k1, i + 1)
                s.activation(kt1[:, c, half * CHALF:(half + 1) * CHALF], ps[:, i % 4, 0:CHALF],
                             ACT.Copy).then_inc(s_k1e, 1)

            def v1_evac(i):
                act.wait_ge(s_v1, i + 1)
                s.activation(vv[0:CR, i, :], ps[0:CR, i % 4, :], ACT.Copy).then_inc(s_v1e, 1)

            act.wait_ge(s_magic, 3)
            s.activation(magic[:, 3:4], magic[:, 2:3], ACT.Silu).then_inc(ac, 1)
            act.wait_ge(s_cs, 1)
            for i in range(2 * C1):
                k1_evac(i)
                if i == 1:
                    ot_evac0(NB - 1)

            def feat_hi(n0, i):
                act.wait_ge(s_xt, n0 + i + 1)
                s.activation(feat[:, 0, i * HALF:(i + 1) * HALF], ps[:, XT_BANK[n0 // 2] + i, :],
                             ACT.Copy).then_inc(s_xhi, 1)

            for i in range(2 * NB):
                v1_evac(i)
                if i == 3:
                    feat_hi(0, 0)
                if i == 11:
                    feat_hi(0, 1)

            def token_weights(e, th):
                act.wait_ge(s_wb, e * 2 + (th + 1))
                if not (isinstance(e, int) and e == 0):
                    act.wait_ge(s_yt, e * 2)
                s.activation(wteb[:, th * HALF:(th + 1) * HALF], ps[:, 6 + th, :], ACT.Copy).then_inc(s_wbs, 1)

            def silu_step(e, i, first=False):
                act.wait_ge(s_g, e * 8 + (i + 1))
                if not first:
                    act.wait_ge(s_h, e * 8 + (i - 1))
                s.activation(silu[:, i % 2, :], ps[:, i % 2, :], ACT.Silu).then_inc(s_sil, 1)

            def moe(e, first=False, last=False):
                for i in range(8):
                    slot = i % 2
                    if not (last and i == 7):
                        silu_step(e, i + 1, first and i == 0)
                    act.wait_ge(s_h, e * 8 + (i + 1))
                    if not (first and i < 2):
                        act.wait_ge(s_yy, e * 8 + (i - 1))
                    s.activation(hidsp[:, 0, slot, :], hid[:, slot, :], ACT.Copy).then_inc(s_hhi, 1)
                    k = i - (3 if last else 6 if first else 5)
                    if k in (0, 1):
                        token_weights(e, k)
                    if i == 2 and first:
                        for k in range(2):
                            act.wait_ge(s_rin, k + 1)
                            s.activation(rt[:, 6 + k, :], rt[:, 6 + k, :], ACT.Exp).then_inc(s_rex, 1)

            silu_step(0, 0, first=True)
            moe(0, first=True)
            with act.Fori(1, NE - 1) as e:
                moe(e)
            moe(NE - 1, last=True)

            act.wait_ge(ac, 1)
            s.activation(magic[:, 3:4], magic[:, 2:3], ACT.Exp).then_inc(ac, 1)

            def ffn_weights(parts):
                act.wait_ge(s_wqt, 3)
                for i in parts:
                    s.activation(wsp[1][:, 0, i * FFQ:(i + 1) * FFQ], ps[:, 1 + i, 0:FFQ],
                                 ACT.Copy).then_inc(s_wqhi, 1)
                    s.activation(wraw[1][:, i * FFQ:(i + 1) * FFQ], ps[:, 1 + i, 0:FFQ], ACT.Copy).then_inc(s_wqf, 1)

            for i in range(2 * C1):
                c, half = i % C1, i // C1
                if c == 0:
                    feat_hi(2, half)
                act.wait_ge(s_q1, i + 1)
                s.activation(qk[:, c, half * HALF:(half + 1) * HALF], ps[:, 4 + i % 4, :], ACT.Copy,
                             scale=DH ** -0.5).then_inc(s_q1e, 1)

            def exps1(b, hf):
                act.wait_ge(s_sub1, b * 2 + (hf + 1))
                v = prv1[:, 8 * hf:8 * hf + 8, 0:CR]
                s.activation(v, v, ACT.Exp).then_inc(s_ex1, 1)

            def pt_evac1(b, g):
                act.wait_ge(s_pt1, b * 4 + (g + 1))
                if not (isinstance(b, int) and b == 0 and g < 2):
                    act.wait_ge(s_pv1, b * 4 + (g - 1))
                s.activation(pt[0:CR, g % 2, :], ps[0:CR, 4 + g % 2, :], ACT.Copy).then_inc(s_pta1, 1)

            def ot_evac1(b, k):
                act.wait_ge(s_ot1, b * 2 + (k + 1))
                s.activation(ot[:, 4 * k:4 * k + 4, :], ps[:, 4 + k, :], ACT.Copy).then_inc(s_ota1, 1)

            def body1(b, first=False, last=False):
                pt_evac1(b, 0)
                pt_evac1(b, 1)
                if not first:
                    ot_evac1(b - 1, 0)
                if not last:
                    exps1(b + 1, 0)
                if not first:
                    ot_evac1(b - 1, 1)
                pt_evac1(b, 2)
                pt_evac1(b, 3)
                if not last:
                    exps1(b + 1, 1)

            exps1(0, 0)
            exps1(0, 1)
            body1(0, first=True)
            with act.Fori(1, NB - 1) as b:
                body1(b)
            body1(NB - 1, last=True)
            ffn_weights((0,))
            ot_evac1(NB - 1, 0)
            ot_evac1(NB - 1, 1)
            ffn_weights((1, 2))

            act.wait_ge(s_xsc, 1)
            for i in range(2):
                act.wait_ge(s_xqt, i + 1)
                t = prb[:, i * HALF:(i + 1) * HALF]
                s.activation(t, ps[:, 2 + i, :], ACT.Identity, bias=magic[:, 0:1], scale=qs[:, IX:IX + 1])\
                    .then_inc(s_xqm, 1)
                act.wait_ge(s_xqm, i + 1)
                s.activation(feat[:, 0, i * HALF:(i + 1) * HALF], t, ACT.Identity,
                             bias=magic[:, 1:2]).then_inc(s_xqhi, 1)
            act.wait_ge(ac, 2)
            s.activation(magic[:, 3:4], magic[:, 2:3], ACT.Sigmoid)
            for i in range(4 * CQ):
                dst = gab if i < 2 * CQ else upb
                k = i % (2 * CQ)
                act.wait_ge(s_ug, i + 1)
                s.activation(dst[:, k * HALF:(k + 1) * HALF], ps[:, gu_bank(i), :], ACT.Copy).then_inc(s_uge, 1)

            def chunk(buf, c):
                return buf[:, c * TOK:(c + 1) * TOK]

            for c in range(CQ):
                act.wait_ge(s_gint, c + 1)
                s.activation(chunk(sgb, c), chunk(gab, c), ACT.Sigmoid, scale=qs[:, SG:SG + 1]).then_inc(s_sig, 1)
                act.wait_ge(s_sig, c + 1)
                s.activation(chunk(sgb, c), chunk(sgb, c), ACT.Identity, bias=magic[:, 0:1],
                             scale=65536.0).then_inc(s_sgm, 1)
            act.wait_ge(s_usc, 1)
            for c in range(CQ):
                s.activation(chunk(upb, c), chunk(upb, c), ACT.Identity, bias=magic[:, 0:1],
                             scale=qs[:, IU:IU + 1]).then_inc(s_upm, 1)
            act.wait_ge(s_g2s, 1)
            for c in range(CQ):
                s.activation(chunk(gab, c), chunk(gab, c), ACT.Identity, bias=magic[:, 0:1],
                             scale=qs[:, IG2:IG2 + 1]).then_inc(s_g2m, 1)
        @block.vector
        def _(dve):
            v = nc.vector
            n = [0]

            def link(*steps):
                n[0] += 1
                steps[-1].then_inc(dv, 1)
                dve.wait_ge(dv, n[0])

            def rsqrt(y, xx, t):
                link(v.tensor_scalar(t.bitcast(I32), xx.bitcast(I32), 1, None, ALU.logical_shift_right))
                link(v.tensor_scalar(y.bitcast(I32), t.bitcast(I32), -1.0, RSQRT_SEED, ALU.mult, ALU.add))
                for step in range(3):
                    link(v.tensor_tensor(t, y, y, ALU.mult))
                    link(v.scalar_tensor_tensor(out=t, in0=xx, scalar=-0.5, in1=t, op0=ALU.mult, op1=ALU.mult))
                    last = v.scalar_tensor_tensor(out=y, in0=t, scalar=1.5, in1=y, op0=ALU.add, op1=ALU.mult)
                    if step < 2:
                        link(last)
                return last

            def bn_stats(src, tiles):
                for t in tiles:
                    ins = v.bn_stats(st[:, t, :], src[:, t, :])
                return ins

            def norm_factors(tiles):
                for t in tiles:
                    i1 = v.bn_aggr(mv[:, t, :], st[:, t, :])
                link(i1)
                k = slice(tiles[0], tiles[-1] + 1)
                link(v.tensor_scalar(var[:, k], mv[:, k, 1], LN_EPS, None, ALU.add))
                link(rsqrt(rstd[:, k], var[:, k], nt[:, k]))

            def normalise(tiles, done):
                for t in tiles:
                    i1 = v.tensor_scalar(xn[:, t, :], x[:, t, :], mv[:, t, 0:1], rstd[:, t:t + 1], ALU.subtract,
                                         ALU.mult)
                    if t % 4 == 3:
                        i1.then_inc(done, 1)
                return i1

            v.memset(n2, 1.0)
            link(v.memset(var[:], 1.0))
            dve.wait_ge(loads["x"], 16)
            for t in range(NB):
                v.bn_stats(st[:, t, :], x[:, t, :])
            dve.wait_ge(loads["ctx"], 16)
            for t in range(NB):
                i1 = v.bn_stats(st[0:CR, NB + t, :], cn[0:CR, t, :])
            link(i1)
            for t in range(NB):
                v.bn_aggr(mv[:, t, :], st[:, t, :])
                i1 = v.bn_aggr(mv[0:CR, NB + t, :], st[0:CR, NB + t, :])
            link(i1)
            v.tensor_scalar(var[:, 0:NB], mv[:, 0:NB, 1], 1.0 + LN_EPS, LN_EPS * LN_EPS, ALU.mult, ALU.add)
            link(v.tensor_scalar(var[0:CR, NB:2 * NB], mv[0:CR, NB:2 * NB, 1], LN_EPS, None, ALU.add))
            link(rsqrt(rstd[:], var[:], nt[:, 0:2 * NB]))
            v.scalar_tensor_tensor(out=nmr[0:CR, :], in0=mv[0:CR, NB:2 * NB, 0], scalar=-1.0,
                                   in1=rstd[0:CR, NB:2 * NB], op0=ALU.mult, op1=ALU.mult).then_inc(s_nmr, 1)
            for t in range(NB):
                i1 = v.tensor_scalar(xn[:, t, :], x[:, t, :], mv[:, t, 0:1], rstd[:, t:t + 1], ALU.subtract, ALU.mult)
                if t % 4 == 3:
                    i1.then_inc(s_norm1, 1)
            dve.wait_ge(loads["vec"], 16)
            v.scalar_tensor_tensor(out=qks[:], in0=vec[:, 4:5], scalar=8.0, in1=vec[:, 5:6], op0=ALU.mult,
                                   op1=ALU.mult).then_inc(s_qks, 1)

            def feat_affine(i):
                k, w = cols(i)
                wb = 2 if i < 2 else 0
                dve.wait_ge(s_trn1, i + 1)
                v.tensor_scalar(featf[:, k:k + w], ps[:, i, 0:w], vec[:, wb:wb + 1], vec[:, wb + 1:wb + 2], ALU.mult,
                                ALU.add).then_inc(s_ff1, 1)

            def feat_lo(i):
                k, w = cols(i)
                dve.wait_ge(s_ff1, i + 1)
                dve.wait_ge(s_fhi1, i + 1)
                v.tensor_tensor(feat[:, 1, k:k + w], featf[:, k:k + w], feat[:, 0, k:k + w].bitcast(F32),
                                ALU.subtract).then_inc(s_flo1, 1)

            feat_affine(0)
            feat_affine(1)
            feat_lo(0)
            feat_affine(2)
            feat_lo(1)
            feat_affine(3)
            feat_lo(2)
            feat_lo(3)
            i = 0
            for kind, c, part in ORDER:
                if kind == "k":
                    dve.wait_ge(s_pk, i + 1)
                    v.tensor_copy(kdst(c, part), ps[:, i % 2, 0:cols(part)[1]]).then_inc(s_kev, 1)
                    i += 1
                if kind == "v" and not v_on_act(c):
                    r = tile_cols(c)[1]
                    dve.wait_ge(s_pv, c + 1)
                    v.tensor_copy(vv[0:r, c, :], ps[0:r, v_bank(c), :]).then_inc(s_vd, 1)
            dve.wait_ge(s_n2q, len(QSEQ))
            dve.wait_ge(s_n2k, len(KSEQ))
            v.tensor_scalar(n2[:, 0:128], ps[:, 6, 0:128], L2_EPS2, None, ALU.max)
            link(v.tensor_scalar(n2[0:CR, 128:192], ps[0:CR, 6, 128:192], L2_EPS2, None, ALU.max))
            rsqrt(rn[:], n2, nt[:]).then_inc(s_rn, 1)
            for i in range(4):
                k, w = cols(i)
                dve.wait_ge(s_rkhi, i + 1)
                v.tensor_tensor(rklo[:, k:k + w], ps[0:H0, row_bank(i), 0:w], rkhi[:, k:k + w].bitcast(F32),
                                ALU.subtract).then_inc(s_rkt, 1)

            def key_over_norm(i):
                c, part = KFIN[i]
                dve.wait_ge(s_rkb, i + 1)
                v.tensor_tensor(kdst(c, part), kdst(c, part), ps[:, kfin_bank(i), 0:cols(part)[1]],
                                ALU.mult).then_inc(s_kfin, 1)

            for i in range(KFIN_AHEAD):
                key_over_norm(i)

            def smax0(b, hf):
                dve.wait_ge(s_s0, b * 2 + (hf + 1))
                dve.wait_ge(s_st0, b * 8 + (4 * hf + 4))
                v.tensor_reduce(mx[:, 4 * hf:4 * hf + 4].rearrange("p (i j) -> p j i", j=2),
                                ps[:, 2 * hf:2 * hf + 2, 0:2 * KEYS0].rearrange("p j (i k) -> p j i k", i=2),
                                AX.X, ALU.max, negate=True).then_inc(s_mx0, 1)
                dve.wait_ge(s_mx0, b * 2 + (hf + 1))
                v.tensor_tensor(nbias[:, 4 * hf:4 * hf + 4], mx[:, 4 * hf:4 * hf + 4], rqst[:, 4 * hf:4 * hf + 4],
                                ALU.mult).then_inc(s_nb0, 1)

            def pt_evac0(b, g):
                dve.wait_ge(s_pt0, b * 4 + (g + 1))
                if not (isinstance(b, int) and b == 0 and g < 2):
                    dve.wait_ge(s_pv0, b * 4 + (g - 1))
                v.tensor_copy(pt[:, g % 2, :], ps[:, 4 + g % 2, :]).then_inc(s_pte0, 1)

            def rsum0(b, k):
                dve.wait_ge(s_ex0, b * 2 + (k + 1))
                if not (isinstance(b, int) and b == 0):
                    dve.wait_ge(s_on0, b)
                v.reciprocal(rsum[:, 4 * k:4 * k + 4], sums[:, 4 * k:4 * k + 4]).then_inc(s_rs0, 1)

            def scale0(b, first=False):
                dve.wait_ge(s_pv0, b * 4 + 4)
                dve.wait_ge(s_rs0, b * 2 + 2)
                if not first:
                    dve.wait_ge(s_ot0, b)
                v.tensor_tensor(cnf[:, 0:512].rearrange("p (h d) -> p h d", h=H0),
                                ps[:, 6, :].rearrange("p (h d) -> p h d", h=H0),
                                rsum[:, 0:H0].unsqueeze(2).to_broadcast([P, H0, DH]), ALU.mult).then_inc(s_on0, 1)

            def y_evac0(b):
                dve.wait_ge(s_y0, b + 1)
                dve.wait_ge(s_y0, 1)
                v.tensor_copy(xnf[:, bass.ds(b * D, D)], ps[:, 7, 0:D])
                v.bn_stats(st[:, bass.ds(b, 1), :], ps[:, 7, 0:D]).then_inc(s_ys0, 1)

            def body0(b, first=False):
                rsum0(b, 0)
                pt_evac0(b, 0)
                pt_evac0(b, 1)
                smax0(b + 1, 0)
                rsum0(b, 1)
                pt_evac0(b, 2)
                pt_evac0(b, 3)
                smax0(b + 1, 1)
                if not first:
                    y_evac0(b - 1)
                scale0(b, first)

            smax0(0, 0)
            smax0(0, 1)
            for i in range(KFIN_AHEAD, len(KFIN)):
                key_over_norm(i)
            body0(0, first=True)
            with dve.Fori(1, NB - 1) as b:
                body0(b)

            EARLY, LATE = range(NB - 2), range(NB - 2, NB)

            def add_attention(tiles):
                norm_factors(tiles)
                for t in tiles:
                    i1 = v.scalar_tensor_tensor(out=xn[:, t, :], in0=xn[:, t, :], scalar=mv[:, t, 0:1],
                                                in1=lno[:, 0, :], op0=ALU.subtract, op1=ALU.mult)
                link(i1)
                for t in tiles:
                    i1 = v.scalar_tensor_tensor(out=x[:, t, :], in0=xn[:, t, :], scalar=rstd[:, t:t + 1],
                                                in1=x[:, t, :], op0=ALU.mult, op1=ALU.add)
                link(i1)

            def norm_tokens(tiles, done):
                link(bn_stats(x, tiles))
                norm_factors(tiles)
                return normalise(tiles, done)

            dve.wait_ge(loads["lno"], 16)
            dve.wait_ge(s_xb, 1)
            rsum0(NB - 1, 0)
            rsum0(NB - 1, 1)
            dve.wait_ge(s_ys0, NB - 2)
            add_attention(EARLY)
            y_evac0(NB - 2)
            scale0(NB - 1)
            norm_tokens(EARLY, s_xn)
            y_evac0(NB - 1)
            dve.wait_ge(s_ys0, NB)
            add_attention(LATE)
            norm_tokens(LATE, s_xn)

            def feat_lo_x(n0, i):
                dve.wait_ge(s_xhi, n0 + i + 1)
                v.tensor_tensor(feat[:, 1, i * HALF:(i + 1) * HALF], ps[:, XT_BANK[n0 // 2] + i, :],
                                feat[:, 0, i * HALF:(i + 1) * HALF].bitcast(F32), ALU.subtract).then_inc(s_xlo, 1)

            feat_lo_x(0, 0)
            feat_lo_x(0, 1)
            dve.wait_ge(loads["wqn"], 48)
            link(v.tensor_reduce(wmax, wblk, AX.X, ALU.max, apply_absolute_value=True))
            link(v.tensor_scalar(wscale, wmax, 1.0 / 7.0, 1e-12, ALU.mult, ALU.max))
            v.reciprocal(winv, wscale).then_inc(s_wqs, 1)

            def R(i):
                return rt[:, i, :].rearrange("p (b e) -> p b e", e=NE)

            def bc(col):
                return col.unsqueeze(2).to_broadcast([P, NB, NE])

            LOG, EQ1, LOG2, EQ2, T, ABS, E1, E2, RANK, CAND = range(10)
            small = rt[:, 10, :].rearrange("p (k b) -> p k b", b=NB)
            M1, M2, S1, S2, C1_, C2_ = (small[:, i, :] for i in range(6))
            rank_c = rt[:, RANK, :].rearrange("p (b e) -> p b e", e=NE)
            for e in range(NE):
                i1 = v.memset(rank_c[:, :, e], float(NE - e))
            dve.wait_ge(s_lg, 2)
            link(v.tensor_copy(rt[:, LOG, :], ps[:, 6, 0:64]))
            link(v.scalar_tensor_tensor(out=R(ABS), in0=R(LOG), scalar=-1.0, in1=R(LOG), op0=ALU.mult, op1=ALU.max))

            def choose(src, m, cand_col, eq):
                link(v.tensor_reduce(m, R(src), AX.X, ALU.max))
                link(v.tensor_tensor(R(T), R(src), bc(m), ALU.is_equal))
                link(v.tensor_tensor(R(T), R(T), R(RANK), ALU.mult))
                link(v.tensor_reduce(cand_col, R(T), AX.X, ALU.max))
                link(v.tensor_tensor(R(eq), R(T), bc(cand_col), ALU.is_equal))

            def softmax_in(src, m, e):
                v.tensor_tensor(R(e), R(src), bc(m), ALU.subtract).then_inc(s_rin, 1)

            def keep_sum(m, e, ssum, drop):
                link(v.tensor_tensor(R(T), R(ABS), bc(m), ALU.max))
                link(v.tensor_tensor(R(CAND), bc(m), R(LOG), ALU.subtract))
                link(v.scalar_tensor_tensor(out=R(T), in0=R(T), scalar=0.02, in1=R(CAND), op0=ALU.mult,
                                            op1=ALU.is_ge))
                if drop is not None:
                    link(v.scalar_tensor_tensor(out=R(CAND), in0=R(drop), scalar=0.0, in1=R(T), op0=ALU.is_equal,
                                                op1=ALU.mult))
                    keep = CAND
                else:
                    keep = T
                link(v.tensor_tensor(R(CAND), R(keep), R(e), ALU.mult))
                link(v.tensor_reduce(ssum, R(CAND), AX.X, ALU.add))
                link(v.reciprocal(ssum, ssum))

            def route(k):
                if k == 0:
                    choose(LOG, M1, C1_, EQ1)
                if k == 1:
                    softmax_in(LOG, M1, E1)
                    link(v.scalar_tensor_tensor(out=R(LOG2), in0=R(EQ1), scalar=-NEG, in1=R(LOG), op0=ALU.mult,
                                                op1=ALU.add))
                    choose(LOG2, M2, C2_, EQ2)
                    softmax_in(LOG2, M2, E2)
                if k == 3:
                    dve.wait_ge(s_rex, 1)
                    keep_sum(M1, E1, S1, None)
                if k == 4:
                    dve.wait_ge(s_rex, 2)
                    keep_sum(M2, E2, S2, EQ1)
                if k == 5:
                    link(v.tensor_tensor(R(EQ1), R(EQ1), bc(S1), ALU.mult))
                    link(v.tensor_tensor(R(EQ2), R(EQ2), bc(S2), ALU.mult))
                    v.tensor_tensor(wtef.rearrange("p (e b) -> p b e", b=NB), R(EQ1), R(EQ2), ALU.add)\
                        .then_inc(s_wte, 1)
                    dve.wait_ge(s_wte, 1)
                    stage_weights(0, first=True)

            def weigh(e, th, first=False):
                last = isinstance(e, int) and e == NE - 1
                dve.wait_ge(s_yy, e * 8 + (4 * th + 4 if last else 7 + th))
                dve.wait_ge(s_wbs, e * 2 + (th + 1))
                if not first:
                    dve.wait_ge(s_ya, e * 2 + 2)
                v.tensor_tensor(ytmp[:, th, :], ps[:, 4 + th, :], wteb[:, th * HALF:(th + 1) * HALF],
                                ALU.mult).then_inc(s_yt, 1)

            def stage_weights(e, first=False):
                if not first:
                    dve.wait_ge(s_wb, e * 2)
                    dve.wait_ge(s_wte, 1)
                v.tensor_copy(wtes[:], wtef[:, bass.ds(e * NB, NB)]).then_inc(s_wst, 1)

            def product(e, i, first=False):
                dve.wait_ge(s_u, e * 8 + (i + 1))
                dve.wait_ge(s_sil, e * 8 + (i + 1))
                if not first:
                    dve.wait_ge(s_hhi, e * 8 + (i - 1))
                    dve.wait_ge(s_hlo, e * 8 + (i - 1))
                v.tensor_tensor(hid[:, i % 2, :], silu[:, i % 2, :], ps[:, 2 + i % 2, :], ALU.mult).then_inc(s_h, 1)

            def add_last(th):
                dve.wait_ge(s_yt, 2 * NE - 1 + th)
                v.tensor_tensor(yacc[:, th * HALF:(th + 1) * HALF], yacc[:, th * HALF:(th + 1) * HALF],
                                ytmp[:, th, :], ALU.add).then_inc(s_ya, 1)

            def add_experts(th):
                dve.wait_ge(s_yT, th + 1)
                xh = xf[:, th * HALF:(th + 1) * HALF]
                link(v.tensor_tensor(xh, xh, ps[:, YT_BANK[th], :], ALU.add))
                link(bn_stats(x, range(4 * th, 4 * th + 4)))

            def beside_last(k):
                if k == 4:
                    weigh(NE - 1, 0)
                if k == 5:
                    add_last(0)
                if k == 6:
                    add_experts(0)

            def moe(e, first=False, last=False, loaded=None, par=None):
                for i in range(8):
                    slot = i % 2
                    if not first and i < 2:
                        weigh(e - 1, i, first=isinstance(e, int) and e == 1)
                    if not (last and i == 7):
                        product(e, i + 1, first and i == 0)
                    if not (first and i < LO_ON_POOL):
                        dve.wait_ge(s_hhi, e * 8 + (i + 1))
                        v.tensor_tensor(hidsp[:, 1, slot, :], hid[:, slot, :], hidsp[:, 0, slot, :].bitcast(F32),
                                        ALU.subtract).then_inc(s_hlo, 1)
                    if last:
                        beside_last(i)
                    if first:
                        route(i)
                    elif i == 1:
                        stage_weights(e)
                    if 2 <= i < 2 + MP and loaded is not None:
                        k = slice((i - 2) * FF, (i - 1) * FF)
                        dve.wait_ge(ld_moe[par], loaded)
                        dve.wait_ge(s_yy, e * 8)
                        v.tensor_copy(wsp[par][:, 0, k], wraw[par][:, k]).then_inc(s_msub, 1)

            product(0, 0, first=True)
            moe(0, first=True)
            moe(1, loaded=32, par=0)

            with dve.Fori(1, NE // 2 - 1) as i:
                moe(i * 2, loaded=i * 16 + 16, par=1)
                moe(i * 2 + 1, loaded=i * 16 + 32, par=0)
            moe(NE - 2, loaded=16 * (NE // 2), par=1)
            moe(NE - 1, last=True)
            HALVES = range(NB // 2), range(NB // 2, NB)
            norm_factors(HALVES[0])
            normalise(HALVES[0], s_xn)
            weigh(NE - 1, 1)
            add_last(1)
            feat_lo_x(2, 0)
            add_experts(1)
            norm_factors(HALVES[1])
            normalise(HALVES[1], s_xn)
            feat_lo_x(2, 1)

            def stage_q1(b, hf):
                c = slice(4 * hf, 4 * hf + 4)
                v.tensor_copy(qst[:, c, :], qk[:, c, bass.ds(b * P, P)]).then_inc(s_stq1, 1)

            def sub1(b, hf):
                def S():
                    return ps[:, 2 * hf:2 * hf + 2, 0:4 * CR].rearrange("p j (i k) -> p j i k", i=4)

                m = mx[:, 8 * hf:8 * hf + 8].rearrange("p (j i) -> p j i", j=2)
                dve.wait_ge(s_s1, b * 2 + (hf + 1))
                v.tensor_reduce(m, S(), AX.X, ALU.max).then_inc(s_mx1, 1)
                dve.wait_ge(s_mx1, b * 2 + (hf + 1))
                v.tensor_tensor(prv1[:, 8 * hf:8 * hf + 8, 0:CR].rearrange("p (j i) k -> p j i k", j=2), S(),
                                m.unsqueeze(3).to_broadcast([P, 2, 4, CR]), ALU.subtract).then_inc(s_sub1, 1)

            def sums1(b, k):
                dve.wait_ge(s_ex1, b * 2 + (k + 1))
                if not (isinstance(b, int) and b == 0):
                    dve.wait_ge(s_on1, b * 2 + (k - 1))
                h = slice(8 * k, 8 * k + 8)
                v.tensor_reduce(sums[:, h], prv1[:, h, 0:CR], AX.X, ALU.add).then_inc(s_sum1, 1)
                dve.wait_ge(s_sum1, b * 2 + (k + 1))
                v.reciprocal(rsum[:, h], sums[:, h]).then_inc(s_rs1, 1)

            def scale1(b, k, first=False):
                dve.wait_ge(s_pv1, b * 4 + (2 * k + 2))
                dve.wait_ge(s_rs1, b * 2 + (k + 1))
                if not first:
                    dve.wait_ge(s_ot1, b * 2 + (k - 1))
                v.tensor_tensor(cnf[:, 512 * k:512 * k + 512].rearrange("p (h d) -> p h d", h=8),
                                ps[:, 6 + k, :].rearrange("p (h d) -> p h d", h=8),
                                rsum[:, 8 * k:8 * k + 8].unsqueeze(2).to_broadcast([P, 8, DH]),
                                ALU.mult).then_inc(s_on1, 1)

            def add_y1(b):
                dve.wait_ge(s_y1, b + 1)
                xb = xf[:, bass.ds(b * D, D)]
                v.tensor_tensor(xb, xb, ps[:, 0, YCOL:YCOL + D], ALU.add).then_inc(s_x3, 1)
                dve.wait_ge(s_x3, b + 1)
                dve.wait_ge(s_x3, 1)
                v.bn_stats(st[:, bass.ds(b, 1), :], xb).then_inc(s_bn1, 1)

            def last_q(b):
                return isinstance(b, int) and b == NB - 2

            def body1(b, first=False, last=False):
                sums1(b, 0)
                if not last:
                    dve.wait_ge(s_pt1, b * 4 + 2)
                    sub1(b + 1, 0)
                    if not last_q(b):
                        stage_q1(b + 2, 0)
                scale1(b, 0, first)
                sums1(b, 1)
                if not last:
                    dve.wait_ge(s_pt1, b * 4 + 4)
                    sub1(b + 1, 1)
                    if not last_q(b):
                        stage_q1(b + 2, 1)
                if not first:
                    add_y1(b - 1)
                scale1(b, 1, first)

            dve.wait_ge(s_q1e, C1)
            stage_q1(0, 0)
            stage_q1(0, 1)
            sub1(0, 0)
            stage_q1(1, 0)
            sub1(0, 1)
            stage_q1(1, 1)
            dve.wait_ge(s_q1e, 2 * C1)
            body1(0, first=True)
            with dve.Fori(1, NB - 2) as b:
                body1(b)
            body1(NB - 2)

            def absmax_x(tiles, k):
                return v.tensor_reduce(rt[:, 3, k:k + 1], xn[:, tiles[0]:tiles[-1] + 1, :], AX.XY, ALU.max,
                                       apply_absolute_value=True)

            sums1(NB - 1, 0)
            sums1(NB - 1, 1)
            scale1(NB - 1, 0)
            dve.wait_ge(s_bn1, NB - 2)
            norm_factors(EARLY)
            add_y1(NB - 2)
            scale1(NB - 1, 1)
            link(normalise(EARLY, s_x4))
            absmax_x(EARLY, 0)
            add_y1(NB - 1)
            dve.wait_ge(s_bn1, NB)
            norm_factors(LATE)
            normalise(LATE, s_x4)
            dve.wait_ge(s_x4, 2)
            link(absmax_x(LATE, 1))

            gcount = [0]

            def q(i):
                return qs[:, i:i + 1]

            def global_scale(inv, scale, unit=None):
                k = gcount[0]
                gcount[0] += 1
                if unit is not None:
                    link(v.tensor_scalar(q(UX), unit, 1.0 / QMAX, None, ALU.mult))
                dve.wait_ge(s_gmb, k + 1)
                link(v.tensor_reduce(q(0), ps[:, 7, 0:P], AX.X, ALU.max))
                link(v.tensor_scalar(scale, q(0), 1.0 / QMAX if unit is None else q(UX), 1e-12, ALU.mult, ALU.max))
                last = v.reciprocal(inv, scale)
                if unit is not None:
                    link(last)
                    last = v.tensor_tensor(inv, inv, unit, ALU.mult)
                return last

            def chunk(buf, c):
                return buf[:, c * TOK:(c + 1) * TOK]

            v_abs = dict(apply_absolute_value=True)
            v.tensor_reduce(q(0), rt[:, 3, 0:2], AX.X, ALU.max).then_inc(s_am, 1)
            global_scale(q(IX), q(SX)).then_inc(s_xsc, 1)
            dve.wait_ge(s_xsc, 1)
            for i in range(2):
                dve.wait_ge(s_xqhi, i + 1)
                v.scalar_tensor_tensor(out=feat[:, 1, i * HALF:(i + 1) * HALF], in0=prb[:, i * HALF:(i + 1) * HALF],
                                       scalar=MAGIC, in1=feat[:, 0, i * HALF:(i + 1) * HALF].bitcast(F32),
                                       op0=ALU.subtract, op1=ALU.subtract).then_inc(s_xqlo, 1)

            def absmax(i):
                src = gab if i < 2 * CQ else upb
                k = i % (2 * CQ)
                dve.wait_ge(s_uge, i + 1)
                return v.tensor_reduce(rt[:, 0, i:i + 1], src[:, k * HALF:(k + 1) * HALF], AX.X, ALU.max, **v_abs)

            def gate_ints(c):
                link(v.tensor_scalar(chunk(gab, c), chunk(gab, c), q(IG), MAGIC, ALU.mult, ALU.add))
                v.tensor_scalar(chunk(gab, c), chunk(gab, c), MAGIC, None, ALU.subtract).then_inc(s_gint, 1)

            def gated(c):
                w, gi = chunk(sgb, c), chunk(gab, c)
                if c == POOL_CLIP:
                    dve.wait_ge(s_clip, 1)
                else:
                    dve.wait_ge(s_sgm, c + 1)
                    link(v.tensor_scalar(w, w, MAGIC + 65535.0, MAGIC, ALU.min, ALU.max))
                link(v.scalar_tensor_tensor(out=gi, in0=w, scalar=MAGIC, in1=gi, op0=ALU.subtract, op1=ALU.mult))
                return v.tensor_reduce(rt[:, 1, c:c + 1], gi, AX.X, ALU.max, **v_abs)

            for i in range(2 * CQ):
                i1 = absmax(i)
            link(i1)
            v.tensor_reduce(q(0), rt[:, 0, 0:2 * CQ], AX.X, ALU.max).then_inc(s_am, 1)
            absmax(2 * CQ)
            link(global_scale(q(IG), q(SG), q(SX)))
            gate_ints(0)
            absmax(2 * CQ + 1)
            absmax(2 * CQ + 2)
            gate_ints(1)
            absmax(2 * CQ + 3)
            absmax(2 * CQ + 4)
            gate_ints(2)
            link(absmax(2 * CQ + 5))
            v.tensor_reduce(q(0), rt[:, 0, 2 * CQ:4 * CQ], AX.X, ALU.max).then_inc(s_am, 1)
            gated(0)
            global_scale(q(IU), q(SU), q(SX)).then_inc(s_usc, 1)
            gated(1)
            link(gated(2))
            v.tensor_reduce(q(0), rt[:, 1, 0:CQ], AX.X, ALU.max).then_inc(s_am, 1)
            link(v.tensor_scalar(q(SG), q(SG), 1.0 / 65536.0, None, ALU.mult))
            global_scale(q(IG2), q(SG2), q(SG)).then_inc(s_g2s, 1)
            for c in range(CQ):
                dve.wait_ge(s_g2m, c + 1)
                dve.wait_ge(s_up, c + 1)
                link(v.scalar_tensor_tensor(out=chunk(prb, c), in0=chunk(gab, c), scalar=MAGIC, in1=chunk(upb, c),
                                            op0=ALU.subtract, op1=ALU.mult))
                i1 = v.tensor_reduce(rt[:, 2, c:c + 1], chunk(prb, c), AX.X, ALU.max, **v_abs)
            link(i1)
            v.tensor_reduce(q(0), rt[:, 2, 0:CQ], AX.X, ALU.max).then_inc(s_am, 1)
            dve.wait_ge(s_g2s, 1)
            dve.wait_ge(s_usc, 1)
            link(v.tensor_scalar(q(SG2), q(SG2), q(SU), None, ALU.mult))
            link(global_scale(q(IO), q(SO), q(SG2)))
            for c in range(CQ):
                link(v.tensor_scalar(chunk(prb, c), chunk(prb, c), q(IO), MAGIC, ALU.mult, ALU.add))
                v.tensor_scalar(chunk(prb, c), chunk(prb, c), MAGIC, None, ALU.subtract).then_inc(s_oint, 1)
            for i in range(2):
                dve.wait_ge(s_dn, i + 1)
                v.scalar_tensor_tensor(out=xnf[:, i * HALF:(i + 1) * HALF], in0=ps[:, i, :], scalar=q(SO),
                                       in1=xf[:, i * HALF:(i + 1) * HALF], op0=ALU.mult, op1=ALU.add)\
                    .then_inc(s_res, 1)

        @block.tensor
        def _(pe):
            t_ = nc.tensor

            def mm3(dst, lhs, rhs, start=True, stop=True, **kw):
                t_.matmul(dst, lhs[0], rhs[1], start=start, stop=False, **kw)
                t_.matmul(dst, lhs[1], rhs[0], start=False, stop=False, **kw)
                return t_.matmul(dst, lhs[0], rhs[0], start=False, stop=stop, **kw)

            def two(buf, k, w):
                return buf[:, 0, k:k + w], buf[:, 1, k:k + w]

            def keep_warm(bank, count):
                for _ in range(count):
                    t_.matmul(ps[:, bank, 0:P], ident[:], ident[:], start=True, stop=True)

            pe.wait_ge(loads["ident"], 16)
            for t in range(NB):
                pe.wait_ge(s_norm1, t // 4 + 1)
                ins = t_.transpose(ps[:, t // 4, (t % 4) * P:(t % 4 + 1) * P], xn[:, t, :], ident[:])
                if t % 4 == 3:
                    ins.then_inc(s_trn1, 1)
            for t in range(NB):
                pe.wait_ge(s_cnorm1, t // 4 + 1)
                ins = t_.transpose(ps[:, 2 + t // 4, (t % 4) * CR:(t % 4 + 1) * CR], cn[0:CR, t, :],
                                   ident[0:CR, 0:CR])
                if t % 4 == 3:
                    ins.then_inc(s_trn1, 1)

            pe.wait_ge(loads["small"], 16)
            pe.wait_ge(s_w0, 1)
            pe.wait_ge(s_ff1, 2)
            cnt = {"q": 0, "k": 0}
            ncnt = {"q": 0, "k": 0}

            def proj(kind, c, part):
                i = cnt[kind]
                cnt[kind] += 1
                k, w = cols(part)
                pe.wait_ge(s_flo1, part + 1)
                if kind == "k":
                    pe.wait_ge(s_w0, 2)
                    if i >= 2:
                        pe.wait_ge(s_kev, i - 1)
                elif i >= 2:
                    pe.wait_ge(s_qev, i - 1)
                bank = ps[:, (4 if kind == "q" else 0) + i % 2, 0:w]
                wcol = (0 if kind == "q" else 512) + c * P
                mm3(bank, two(wsp[0], wcol, P), two(feat, k, w)).then_inc(s_pq if kind == "q" else s_pk, 1)

            def norms(kind, c, part):
                i = ncnt[kind]
                ncnt[kind] += 1
                pe.wait_ge(s_sqq if kind == "q" else s_sqk, i + 1)
                slot = (0 if kind == "q" else 2) + i % 2
                rows = P if part < 2 else CR
                base = 0 if kind == "q" else (64 if part < 2 else 128)
                for j in range(4):
                    b = (part % 2) * 4 + j
                    k = base + b * H0 + 2 * c
                    ins = t_.matmul(ps[0:rows, 6, k:k + 2], sq[:, slot, j * rows:(j + 1) * rows], bones[:],
                                    start=True, stop=True)
                ins.then_inc(s_n2q if kind == "q" else s_n2k, 1)

            def value(t):
                k, w = tile_cols(t)
                pe.wait_ge(s_flo1, t // 4 + 1)
                pe.wait_ge(s_ff1, 4)
                if t >= 3:
                    pe.wait_ge(*v_out(t - 3))
                mm3(ps[0:w, v_bank(t), :], two(feat, k, w), two(wsp[0], 1024, 512)).then_inc(s_pv, 1)

            LAG = 3
            i = 0
            for g in ORDER:
                if g[0] == "v":
                    value(g[1])
                    continue
                proj(*g)
                if i >= LAG:
                    norms(*QKSEQ[i - LAG])
                i += 1
            for g in QKSEQ[-LAG:]:
                norms(*g)
            for t in range(V_AMONG, 16):
                value(t)
            pe.wait_ge(s_rn, 1)
            pe.wait_ge(s_qev, len(QSEQ))
            pe.wait_ge(s_kev, len(KSEQ))
            for t in range(16):
                k, w = tile_cols(t)
                part = (t // 4)
                ins = t_.transpose(ps[0:H0, row_bank(part), (t % 4) * w:(t % 4 + 1) * w],
                                   rn[0:w, 64 + t * H0:64 + (t + 1) * H0], ident[0:w, 0:w])
                if t % 4 == 3:
                    ins.then_inc(s_rkp, 1)
            pe.wait_ge(s_hsel, 1)
            pe.wait_ge(*v_out(15))
            keep_warm(3, 10)
            pe.wait_ge(s_rkt, 4)

            def key_norms(i):
                c, part = KFIN[i]
                k, w = cols(part)
                if i >= 4:
                    pe.wait_ge(s_kfin, i - 3)
                bank = ps[:, kfin_bank(i), 0:w]
                t_.matmul(bank, hselr[:, c * P:(c + 1) * P], rklo[:, k:k + w], start=True, stop=False)
                t_.matmul(bank, hselr[:, c * P:(c + 1) * P], rkhi[:, k:k + w], start=False, stop=True)\
                    .then_inc(s_rkb, 1)

            for i in range(KFIN_AHEAD):
                key_norms(i)

            def scores0(b, hf):
                pe.wait_ge(s_st0, b * 8 + (4 * hf + 3))
                if not (isinstance(b, int) and b == 0):
                    pe.wait_ge(s_ex0, b * 2 + (hf - 1))
                for i in range(2):
                    for j in range(2):
                        c = 2 * hf + i
                        t_.matmul(ps[:, 2 * hf + j, i * KEYS0:(i + 1) * KEYS0], qst[DH * j:DH * (j + 1), c, :],
                                  kstv0[DH * j:DH * (j + 1), c, :], start=(i == 0), stop=False,
                                  skip_group_check=True)
                mask = maskb[:, bass.ds(b * CR, CR)]
                for j in range(2):
                    for i in range(2):
                        ins = t_.matmul(ps[:, 2 * hf + j, i * KEYS0 + P:(i + 1) * KEYS0], rowone[:], mask,
                                        start=False, stop=(i == 1), skip_group_check=True)
                ins.then_inc(s_s0, 1)

            def pts0(b, g):
                pe.wait_ge(s_ex0, b * 2 + (g // 2 + 1))
                if not (isinstance(b, int) and b == 0 and g < 2):
                    pe.wait_ge(s_pte0, b * 4 + (g - 1))
                for i in range(2):
                    for j in range(2):
                        ins = t_.transpose(ps[:, 4 + g % 2, (2 * i + j) * P:(2 * i + j + 1) * P],
                                           prv0[:, 2 * g + i, j * P:(j + 1) * P], ident[:])
                ins.then_inc(s_pt0, 1)

            def pv0(b, g):
                pe.wait_ge(s_pte0, b * 4 + (g + 1))
                if not (isinstance(b, int) and b == 0) and g == 0:
                    pe.wait_ge(s_on0, b)
                for i in range(2):
                    h = 2 * g + i
                    dst = ps[:, 6, h * DH:(h + 1) * DH]
                    t_.matmul(dst, pt[:, g % 2, 2 * i * P:(2 * i + 1) * P],
                              vvf[:, bass.ds(b * 512 + h * DH, DH)], start=True, stop=False,
                              skip_group_check=True)
                    ins = t_.matmul(dst, pt[0:CR, g % 2, (2 * i + 1) * P:(2 * i + 2) * P],
                                    vvf[0:CR, bass.ds(b * 512 + (8 * 512 + h * DH), DH)], start=False,
                                    stop=True, skip_group_check=True)
                ins.then_inc(s_pv0, 1)

            def ot0(b):
                pe.wait_ge(s_on0, b + 1)
                for c in range(C0):
                    ins = t_.transpose(ps[:, 7, c * P:(c + 1) * P], cnf[:, c * P:(c + 1) * P], ident[:])
                ins.then_inc(s_ot0, 1)

            def y0(b):
                pe.wait_ge(s_ots0, b + 1)
                for c in range(C0):
                    ins = t_.matmul(ps[:, 7, 0:D], ot[:, c, :], wo0[:, c, :], start=(c == 0), stop=(c == C0 - 1))
                ins.then_inc(s_y0, 1)

            def body0(b, first=False, last=False):
                pts0(b, 0)
                pts0(b, 1)
                if not last:
                    scores0(b + 1, 0)
                if first:
                    keep_warm(7, 6)
                pv0(b, 0)
                pv0(b, 1)
                if not first:
                    ot0(b - 1)
                pts0(b, 2)
                pts0(b, 3)
                if not last:
                    scores0(b + 1, 1)
                pv0(b, 2)
                if not first:
                    y0(b - 1)
                pv0(b, 3)

            pe.wait_ge(loads["wo0"], 16)
            pe.wait_ge(s_mask, 1)
            pe.wait_ge(s_rone, 1)
            keep_warm(3, 8)
            scores0(0, 0)
            keep_warm(3, 4)
            scores0(0, 1)
            for i in range(KFIN_AHEAD, len(KFIN)):
                key_norms(i)
            pe.wait_ge(s_kfin, len(KFIN))
            keep_warm(7, 4)
            body0(0, first=True)
            with pe.Fori(1, NB - 1) as b:
                body0(b)
            body0(NB - 1, last=True)

            def key1(i):
                c, half = i // 2, i % 2
                if i >= 4:
                    pe.wait_ge(s_k1e, i - 3)
                mm3(ps[:, i % 4, 0:CHALF], two(kv1w, c * P, P), two(feat, TOK + half * CHALF, CHALF))\
                    .then_inc(s_k1, 1)

            pe.wait_ge(s_cs, 1)
            pe.wait_ge(s_kv1w, 4)
            pe.wait_ge(s_ex0, 2 * NB)
            key1(0)
            key1(1)
            ot0(NB - 1)
            key1(2)
            key1(3)
            y0(NB - 1)
            for i in range(4, 2 * C1):
                key1(i)

            def value1(i):
                b, half = i // 2, i % 2
                if i >= 4:
                    pe.wait_ge(s_v1e, i - 3)
                else:
                    pe.wait_ge(s_k1e, 2 * C1 - 3 + i)
                mm3(ps[0:CR, i % 4, :], two(feat, TOK + b * CR, CR), two(kv1w, 1024 + half * 512, 512))\
                    .then_inc(s_v1, 1)

            def feat_t(k, half):
                pe.wait_ge(s_xn, 2 * k + half + 1)
                for t in range(4 * half, 4 * half + 4):
                    ins = t_.transpose(ps[:, XT_BANK[k] + half, (t % 4) * P:(t % 4 + 1) * P], xn[:, t, :], ident[:])
                ins.then_inc(s_xt, 1)

            def logits(half):
                pe.wait_ge(s_gw, 1)
                pe.wait_ge(s_xlo, half + 1)
                for t in range(4 * half, 4 * half + 4):
                    ins = mm3(ps[:, 6, t * NE:(t + 1) * NE], two(feat, t * P, P), two(gatesp, 0, NE))
                ins.then_inc(s_lg, 1)

            for i in range(2 * NB):
                value1(i)
                if i == 3:
                    feat_t(0, 0)
                if i == 11:
                    feat_t(0, 1)
                    logits(0)
            logits(1)

            def chunk_half(e, i):
                return (i % CF, i // CF) if isinstance(e, int) and e == NE - 1 else (i // 2, i % 2)

            def gu(e, par, i):
                c, th = chunk_half(e, i)
                if not (isinstance(e, int) and e == 0 and i < 2):
                    pe.wait_ge(s_sil, e * 8 + (i - 1))
                rhs = two(feat, th * HALF, HALF)
                mm3(ps[:, i % 2, :], two(wsp[par], c * P, P), rhs).then_inc(s_g, 1)
                if not (isinstance(e, int) and e == 0 and i < 2):
                    pe.wait_ge(s_h, e * 8 + (i - 1))
                ins = mm3(ps[:, 2 + i % 2, :], two(wsp[par], FF + c * P, P), rhs)
                ins.then_inc(s_u, 1)

            def y(e, par, i):
                c, th = chunk_half(e, i)
                pe.wait_ge(s_hhi, e * 8 + (i + 1))
                pe.wait_ge(s_hlo, e * 8 + (i + 1))
                if c == 0 and not (isinstance(e, int) and e == 0):
                    pe.wait_ge(s_yt, e * 2 + (th - 1))
                ins = mm3(ps[:, 4 + th, :], two(wsp[par], 2 * FF + c * P, P),
                          (hidsp[:, 0, i % 2, :], hidsp[:, 1, i % 2, :]), start=(c == 0), stop=(c == CF - 1))
                ins.then_inc(s_yy, 1)
                return ins

            def expert(e, par, next_ready):
                for i in range(8):
                    if i + 2 < 8:
                        gu(e, par, i + 2)
                    elif next_ready is not None:
                        if i == 6:
                            pe.wait_ge(s_msp[1 - par], next_ready * MP)
                        gu(e + 1, 1 - par, i - 6)
                    y(e, par, i)
                    if i == (4 if not isinstance(e, int) else 5 if e == 0 else 2 if e == NE - 1 else 4):
                        pe.wait_ge(s_wst, e + 1)
                        if not (isinstance(e, int) and e == 0):
                            pe.wait_ge(s_wbs, e * 2)
                        for t in range(NB):
                            ins = t_.transpose(ps[:, 6 + t // 4, (t % 4) * P:(t % 4 + 1) * P],
                                               wtes[:, t:t + 1].to_broadcast([P, P]), ident[:])
                            if t % 4 == 3:
                                ins.then_inc(s_wb, 1)
                    if next_ready is None and i == 5:
                        sum_t(0)

            def sum_t(th):
                pe.wait_ge(s_wbs, 2 * NE)
                pe.wait_ge(s_ya, 2 * NE + 1 + th)
                for t in range(4):
                    k = th * HALF + t * P
                    ins = t_.transpose(ps[:, YT_BANK[th], t * P:(t + 1) * P], yacc[:, k:k + P], ident[:])
                ins.then_inc(s_yT, 1)

            pe.wait_ge(s_msp[0], MP)
            pe.wait_ge(s_v1e, 2 * NB)
            gu(0, 0, 0)
            gu(0, 0, 1)
            expert(0, 0, 1)
            expert(1, 1, 2)
            with pe.Fori(1, NE // 2 - 1) as i:
                expert(i * 2, 0, i + 1)
                expert(i * 2 + 1, 1, i + 2)
            expert(NE - 2, 0, NE // 2)
            expert(NE - 1, 1, None)

            keep_warm(1, 12)
            feat_t(1, 0)
            sum_t(1)
            keep_warm(1, 4)

            pe.wait_ge(s_q1w, 1)
            def query1(i):
                c, half = i % C1, i // C1
                pe.wait_ge(s_xlo, 3 + half)
                if i >= 4:
                    pe.wait_ge(s_q1e, i - 3)
                mm3(ps[:, 4 + i % 4, :], two(wsp[0], c * P, P),
                    two(feat, half * HALF, HALF)).then_inc(s_q1, 1)

            def scores1(b, hf):
                pe.wait_ge(s_st1, b * 4 + (2 * hf + 2))
                pe.wait_ge(s_stq1, b * 2 + (hf + 1))
                if not (isinstance(b, int) and b == 0):
                    pe.wait_ge(s_sub1, b * 2 + (hf - 1))
                    if hf == 0 and not (isinstance(b, int) and b < 3):
                        pe.wait_ge(s_x3, b - 2)
                for i in range(4):
                    c = 4 * hf + i
                    ins = t_.matmul(ps[:, 2 * hf + i // 2, (i % 2) * 2 * CR:(i % 2 + 1) * 2 * CR], qst[:, c, :],
                                    kstv1[:, c, :], start=True, stop=True, skip_group_check=True)
                ins.then_inc(s_s1, 1)

            def pts1(b, g):
                pe.wait_ge(s_ex1, b * 2 + (g // 2 + 1))
                if g < 2:
                    if not (isinstance(b, int) and b == 0):
                        pe.wait_ge(s_pta1, b * 4 + (g - 1))
                elif not (isinstance(b, int) and b == 0):
                    pe.wait_ge(s_ota1, b * 2 + (g - 3))
                for i in range(4):
                    ins = t_.transpose(ps[0:CR, 4 + g % 2, i * P:(i + 1) * P], prv1[:, 4 * g + i, 0:CR], ident[:])
                ins.then_inc(s_pt1, 1)

            def pv1(b, g):
                pe.wait_ge(s_pta1, b * 4 + (g + 1))
                if not (isinstance(b, int) and b == 0) and g % 2 == 0:
                    pe.wait_ge(s_on1, b * 2 + (g // 2 - 1))
                for i in range(4):
                    h = 4 * g + i
                    k = (h % 8) * DH
                    ins = t_.matmul(ps[:, 6 + g // 2, k:k + DH], pt[0:CR, g % 2, i * P:(i + 1) * P],
                                    vvf[0:CR, bass.ds(b * 1024 + h * DH, DH)], start=True, stop=True,
                                    skip_group_check=True)
                ins.then_inc(s_pv1, 1)

            def ot1(b, k):
                pe.wait_ge(s_on1, b * 2 + (k + 1))
                for c in range(4):
                    ins = t_.transpose(ps[:, 4 + k, c * P:(c + 1) * P], cnf[:, (4 * k + c) * P:(4 * k + c + 1) * P],
                                       ident[:])
                ins.then_inc(s_ot1, 1)

            def y1(b, last_scores=None):
                pe.wait_ge(s_ota1, b * 2 + 2)
                pe.wait_ge(s_sub1, b * 2 + 5 if last_scores is None else last_scores)
                if last_scores == 2 * NB:
                    pe.wait_ge(s_x3, b)
                for c in range(C1):
                    ins = t_.matmul(ps[:, 0, YCOL:YCOL + D], ot[:, c, :], wo1[:, c, :], start=(c == 0),
                                    stop=(c == C1 - 1), skip_group_check=True)
                ins.then_inc(s_y1, 1)

            def ffn_weights_t():
                pe.wait_ge(s_wq, 1)
                pe.wait_ge(s_sub1, 2 * NB)
                for i in range(3):
                    for c in range(CQ):
                        ins = t_.transpose(ps[:, 1 + i, c * P:(c + 1) * P], wqn[:, i * CQ + c, :], ident[:])
                    ins.then_inc(s_wqt, 1)

            def body1(b, first=False, last=False):
                pts1(b, 0)
                pts1(b, 1)
                if last:
                    ffn_weights_t()
                else:
                    scores1(b + 1, 0)
                pv1(b, 0)
                if not first:
                    ot1(b - 1, 0)
                pv1(b, 1)
                if not first:
                    ot1(b - 1, 1)
                if not last:
                    scores1(b + 1, 1)
                pts1(b, 2)
                pts1(b, 3)
                if not first:
                    y1(b - 1, 2 * NB if last else None)
                pv1(b, 2)
                pv1(b, 3)

            for i in range(2 * C1):
                if i == C1:
                    feat_t(1, 1)
                if i == 14:
                    scores1(0, 0)
                if i == 15:
                    scores1(0, 1)
                query1(i)
            pe.wait_ge(loads["wo1"], 16)
            pe.wait_ge(s_q1e, 2 * C1)
            body1(0, first=True)
            body1(1)
            with pe.Fori(2, NB - 1) as b:
                body1(b)
            body1(NB - 1, last=True)
            pe.wait_ge(s_pta1, 4 * NB)
            ot1(NB - 1, 0)
            ot1(NB - 1, 1)
            y1(NB - 1, 2 * NB)

            gcount = [0]

            def global_max():
                k = gcount[0]
                gcount[0] += 1
                pe.wait_ge(s_am, k + 1)
                t_.transpose(ps[:, 7, 0:P], qs[:, 0:1].to_broadcast([P, P]), ident[:]).then_inc(s_gmb, 1)

            keep_warm(6, 16)
            pe.wait_ge(s_wqf, 3)
            for t in range(NB):
                pe.wait_ge(s_x4, t // 4 + 1)
                ins = t_.transpose(ps[:, 2 + t // 4, (t % 4) * P:(t % 4 + 1) * P], xn[:, t, :], ident[:])
                if t % 4 == 3:
                    ins.then_inc(s_xqt, 1)
            global_max()
            keep_warm(6, 12)
            pe.wait_ge(s_wqlo, 1)
            for i in range(4 * CQ):
                chunk = CQ + i // 2 if i < 2 * CQ else i // 2 - CQ
                pe.wait_ge(s_xqlo, i % 2 + 1)
                if i >= 4:
                    pe.wait_ge(s_uge, i - 3)
                mm3(ps[:, gu_bank(i), :], two(wsp[1], chunk * P, P), two(feat, (i % 2) * HALF, HALF))\
                    .then_inc(s_ug, 1)
                if i == 2 * CQ + 1:
                    global_max()
            global_max()
            global_max()
            keep_warm(6, 30)
            global_max()
            keep_warm(6, 6)
            for c in range(CQ):
                pe.wait_ge(s_oint, c + 1)
                for t in range(NB):
                    ins = t_.matmul(ps[:, t // 4, (t % 4) * P:(t % 4 + 1) * P],
                                    prb[:, c * TOK + t * P:c * TOK + (t + 1) * P],
                                    wraw[1][:, (2 * CQ + c) * P:(2 * CQ + c + 1) * P], start=(c == 0 and t % 4 == 0),
                                    stop=(c == CQ - 1 and t % 4 == 3), skip_group_check=True)
                    if c == CQ - 1 and t % 4 == 3:
                        ins.then_inc(s_dn, 1)


def kernel(**inputs):
    import concourse.bacc as _bacc
    from concourse.bass_utils import run_bass_kernel_spmd as _run

    g = {k: np.asarray(v) for k, v in inputs.items()}
    f32 = np.float32
    arrays = {
        "x": g["x"], "ctx": g["ctx_1024"],
        "ctxT": g["ctx_1024"].reshape(CTX, D).T,
        "mask": g["mask_BxS2_bk0"].reshape(1, CTX),
        "vec": np.stack([g["L0_xattn_ln_x_w"], g["L0_xattn_ln_x_b"], g["L0_xattn_ln_l_w"], g["L0_xattn_ln_l_b"],
                         np.tile(g["L0_xattn_q_scale"], 2), np.tile(g["L0_xattn_k_scale"], 2)], axis=1),
        "lno": np.broadcast_to(np.stack([g["L0_xattn_ln_o_w"], g["L0_xattn_ln_o_b"]]), (P, 2, D)),
        "Wq": g["L0_xattn_Wq"], "Wkv": g["L0_xattn_Wkv"], "Wo": g["L0_xattn_Wo"],
        "gateT": g["L0_ffn_gate_w"].T,
        "moe": np.concatenate([g["L0_ffn_w1"].transpose(0, 2, 1), g["L0_ffn_w3"].transpose(0, 2, 1),
                               g["L0_ffn_w2"].transpose(0, 2, 1).reshape(NE, CF, P, D).transpose(0, 2, 1, 3)
                               .reshape(NE, P, CF * D)], axis=2),
        "W1q": g["L1_xattn_Wq"], "W1k": g["L1_xattn_Wk"], "W1v": g["L1_xattn_Wv"], "W1o": g["L1_xattn_Wo"],
        "wup": g["L1_ffn_w_up"], "wgate": g["L1_ffn_w_gate"], "wdown": g["L1_ffn_w_down"],
        "ident": np.eye(P, dtype=f32),
        "bones": np.repeat(np.eye(2, dtype=f32), DH, axis=0),
        "hsel": np.repeat(np.eye(H0, dtype=f32), DH, axis=1),
    }
    arrays = {k: np.ascontiguousarray(v) for k, v in arrays.items()}
    nc = _bacc.Bacc("TRN2", target_bir_lowering=False, num_devices=1)
    aps = {k: nc.dram_tensor(f"in_{k}", v.shape, mybir.dt.from_np(v.dtype), kind="ExternalInput").ap()
           for k, v in arrays.items()}
    out = nc.dram_tensor("out_dram", (NB, P, D), F32, kind="ExternalOutput").ap()
    two_layer_kernel(nc, aps, out)
    r = _run(nc, [{f"in_{k}": v for k, v in arrays.items()}], core_ids=[0])
    return r.results[0]["out_dram"]
```
